# Optimizing a Trainium2 kernel written in Bass

```python
import numpy as np
import jax
import jax.numpy as jnp

def _softmax(x, axis=-1):
    return jax.nn.softmax(x, axis=axis)

def _gelu(x):
    return jax.nn.gelu(x, approximate=True)

def _silu(x):
    return jax.nn.silu(x)

def _sigmoid(x):
    return jax.nn.sigmoid(x)

def _layernorm(x, axis=-1, eps=1e-05):
    m = jnp.mean(x, axis=axis, keepdims=True)
    v = jnp.var(x, axis=axis, keepdims=True)
    return (x - m) / jnp.sqrt(v + eps)

def _scatter_add(tgt, idx, src, axis=0):
    return tgt.at[idx].add(src)

def _segment_sum(src, seg, n):
    return jax.ops.segment_sum(src, seg, n)
kernel_name = 'mk_perceiver_d1_seqx_r2_171e0f'

def setup_inputs(seed: int=0):
    np.random.seed(seed)
    _w = jnp.asarray

    def _rec_inputs():
        import jax
        import jax.numpy as jnp
        _rk = jax.random.key(seed)
        x = -0.0002928 + 1 * jax.random.normal(jax.random.fold_in(_rk, 1), (16, 64, 512), jnp.float32)
        _lenS = 64 - jax.random.randint(jax.random.fold_in(_rk, 7), (16,), 0, max(1, 64 // 4) + 1, jnp.int32)
        _lenS2 = 1601 - jax.random.randint(jax.random.fold_in(_rk, 8), (16,), 0, max(1, 1601 // 4) + 1, jnp.int32)
        _ctx_1024P = jax.random.normal(jax.random.fold_in(_rk, 11), (16, 16, 512), jnp.float32)
        _ctx_1024c = jax.random.dirichlet(jax.random.fold_in(_rk, 511), 0.3 * jnp.ones((16,), jnp.float32), (16, 1601))
        _ctx_1024t = jnp.einsum('bsk,bkd->bsd', _ctx_1024c, _ctx_1024P)
        _ctx_1024t = _ctx_1024t * jax.lax.rsqrt(jnp.mean(jnp.square(_ctx_1024t)) + 1e-12) * 0.953939
        ctx_1024 = -1.39393e-06 + 0.999914 * (_ctx_1024t + 0.3 * jax.random.normal(jax.random.fold_in(_rk, 611), (16, 1601, 512), jnp.float32))
        return (x, ctx_1024)
    x, ctx_1024 = _rec_inputs()

    def _L0_xattn_setup():
        import jax, jax.numpy as jnp
        import numpy as np
        DIM = 512
        HEADS = 16
        HEAD_DIM = DIM // HEADS
        SCALE = HEAD_DIM ** (-0.5)

        def _split_heads(t):
            b, n, _ = t.shape
            return t.reshape(b, n, HEADS, HEAD_DIM).transpose(0, 2, 1, 3)
        key = jax.random.key(seed)
        ks = jax.random.split(key, 7)
        B, N, M = (2, 1024, 1024)
        x = jax.random.normal(ks[0], (B, N, DIM), dtype=jnp.float32)
        y = jax.random.normal(ks[1], (B, M, DIM), dtype=jnp.float32)
        s = DIM ** (-0.5)
        Wq = jax.random.normal(ks[2], (DIM, DIM), dtype=jnp.float32) * s
        Wk = jax.random.normal(ks[3], (DIM, DIM), dtype=jnp.float32) * s
        Wv = jax.random.normal(ks[4], (DIM, DIM), dtype=jnp.float32) * s
        Wp = jax.random.normal(ks[5], (DIM, DIM), dtype=jnp.float32) * s
        bp = jax.random.normal(ks[6], (DIM,), dtype=jnp.float32) * 0.01
        return {'x': x, 'y': y, 'Wq': Wq, 'Wk': Wk, 'Wv': Wv, 'Wp': Wp, 'bp': bp}
    _L0_xattn_all = _L0_xattn_setup()
    _L0_xattn_in = {k: v for k, v in _L0_xattn_all.items() if k in ('Wq', 'Wk', 'Wv', 'Wp', 'bp')}
    del _L0_xattn_all

    def _L0_attn_setup():
        import jax, jax.numpy as jnp
        import numpy as np
        import math
        NUM_HEADS = 16

        def _alibi_bias(L, num_heads):
            slopes = jnp.power(2.0, jnp.linspace(-4.0, -0.3, num_heads))
            pos = jnp.arange(L, dtype=jnp.float32)
            return -(slopes[:, None] * pos[None, :])
        key = jax.random.key(seed)
        ks = jax.random.split(key, 9)
        B, L, D = (2, 1024, 512)
        s = 0.02
        return {'x': jax.random.normal(ks[0], (B, L, D), dtype=jnp.float32), 'Wq': jax.random.normal(ks[1], (D, D), dtype=jnp.float32) * s, 'bq': jax.random.normal(ks[2], (D,), dtype=jnp.float32) * s, 'Wk': jax.random.normal(ks[3], (D, D), dtype=jnp.float32) * s, 'bk': jax.random.normal(ks[4], (D,), dtype=jnp.float32) * s, 'Wv': jax.random.normal(ks[5], (D, D), dtype=jnp.float32) * s, 'bv': jax.random.normal(ks[6], (D,), dtype=jnp.float32) * s, 'Wo': jax.random.normal(ks[7], (D, D), dtype=jnp.float32) * s, 'bo': jax.random.normal(ks[8], (D,), dtype=jnp.float32) * s}
    _L0_attn_all = _L0_attn_setup()
    _L0_attn_in = {k: v for k, v in _L0_attn_all.items() if k in ('Wq', 'bq', 'Wk', 'bk', 'Wv', 'bv', 'Wo', 'bo')}
    del _L0_attn_all

    def _L0_ffn_setup():
        import jax, jax.numpy as jnp
        import numpy as np
        import math
        BETA = 0.9
        THRESHOLD = 1.0
        NUM_STEPS = 5
        ALPHA = 2.0

        @jax.custom_vjp
        def spike_fn(u):
            return (u > 0).astype(u.dtype)

        def _spike_fwd(u):
            return (spike_fn(u), u)

        def _spike_bwd(u, g):
            s = jnp.pi / 2.0 * ALPHA * u
            return (g * (ALPHA / 2.0) / (1.0 + s * s),)
        spike_fn.defvjp(_spike_fwd, _spike_bwd)
        key = jax.random.key(seed)
        k1, k2, k3 = jax.random.split(key, 3)
        n_embd = 512
        x = jax.random.normal(k1, (4, 1024, n_embd), dtype=jnp.float32)
        W_fc = jax.random.normal(k2, (4 * n_embd, n_embd), dtype=jnp.float32) / math.sqrt(n_embd)
        W_proj = jax.random.normal(k3, (n_embd, 4 * n_embd), dtype=jnp.float32) / math.sqrt(4 * n_embd)
        return {'x': x, 'W_fc': W_fc, 'W_proj': W_proj}
    _L0_ffn_all = _L0_ffn_setup()
    _L0_ffn_in = {k: v for k, v in _L0_ffn_all.items() if k in ('W_fc', 'W_proj')}
    del _L0_ffn_all
    return {'x': x, 'ctx_1024': ctx_1024, 'L0_xattn_Wq': _L0_xattn_in['Wq'], 'L0_xattn_Wk': _L0_xattn_in['Wk'], 'L0_xattn_Wv': _L0_xattn_in['Wv'], 'L0_xattn_Wp': _L0_xattn_in['Wp'], 'L0_xattn_bp': _L0_xattn_in['bp'], 'L0_attn_Wq': _L0_attn_in['Wq'], 'L0_attn_bq': _L0_attn_in['bq'], 'L0_attn_Wk': _L0_attn_in['Wk'], 'L0_attn_bk': _L0_attn_in['bk'], 'L0_attn_Wv': _L0_attn_in['Wv'], 'L0_attn_bv': _L0_attn_in['bv'], 'L0_attn_Wo': _L0_attn_in['Wo'], 'L0_attn_bo': _L0_attn_in['bo'], 'L0_ffn_W_fc': _L0_ffn_in['W_fc'], 'L0_ffn_W_proj': _L0_ffn_in['W_proj']}

def reference(x, ctx_1024, L0_xattn_Wq, L0_xattn_Wk, L0_xattn_Wv, L0_xattn_Wp, L0_xattn_bp, L0_attn_Wq, L0_attn_bq, L0_attn_Wk, L0_attn_bk, L0_attn_Wv, L0_attn_bv, L0_attn_Wo, L0_attn_bo, L0_ffn_W_fc, L0_ffn_W_proj):
    import jax
    import jax.numpy as jnp

    def _L0_xattn_ref(x, y, Wq, Wk, Wv, Wp, bp):
        import jax, jax.numpy as jnp
        import numpy as np
        DIM = 512
        HEADS = 16
        HEAD_DIM = DIM // HEADS
        SCALE = HEAD_DIM ** (-0.5)

        def _split_heads(t):
            b, n, _ = t.shape
            return t.reshape(b, n, HEADS, HEAD_DIM).transpose(0, 2, 1, 3)
        q = _split_heads(x @ Wq)
        k = _split_heads(y @ Wk)
        v = _split_heads(y @ Wv)
        attn = jnp.einsum('bhid,bhjd->bhij', q, k) * SCALE
        attn = jax.nn.softmax(attn, axis=-1)
        out = jnp.einsum('bhij,bhjd->bhid', attn, v)
        b, h, n, d = out.shape
        out = out.transpose(0, 2, 1, 3).reshape(b, n, h * d)
        return out @ Wp + bp

    def _L0_attn_ref(x, Wq, bq, Wk, bk, Wv, bv, Wo, bo):
        import jax, jax.numpy as jnp
        import numpy as np
        import math
        NUM_HEADS = 16

        def _alibi_bias(L, num_heads):
            slopes = jnp.power(2.0, jnp.linspace(-4.0, -0.3, num_heads))
            pos = jnp.arange(L, dtype=jnp.float32)
            return -(slopes[:, None] * pos[None, :])
        B, L, D = x.shape
        H = NUM_HEADS
        hd = D // H
        scale = math.sqrt(hd)

        def proj(W, b):
            return (jnp.einsum('bld,ed->ble', x, W) + b).reshape(B, L, H, hd)
        q = proj(Wq, bq)
        k = proj(Wk, bk)
        v = proj(Wv, bv)
        scores = jnp.einsum('bqhd,bkhd->bhqk', q, k) / scale
        bias = _alibi_bias(L, H)
        scores = scores + bias[None, :, None, :]
        attn = jax.nn.softmax(scores, axis=-1)
        out = jnp.einsum('bhqk,bkhd->bqhd', attn, v).reshape(B, L, D)
        return jnp.einsum('bld,ed->ble', out, Wo) + bo

    def _L0_ffn_ref(x, W_fc, W_proj):
        import jax, jax.numpy as jnp
        import numpy as np
        import math
        BETA = 0.9
        THRESHOLD = 1.0
        NUM_STEPS = 5
        ALPHA = 2.0

        @jax.custom_vjp
        def spike_fn(u):
            return (u > 0).astype(u.dtype)

        def _spike_fwd(u):
            return (spike_fn(u), u)

        def _spike_bwd(u, g):
            s = jnp.pi / 2.0 * ALPHA * u
            return (g * (ALPHA / 2.0) / (1.0 + s * s),)
        spike_fn.defvjp(_spike_fwd, _spike_bwd)
        h = jnp.square(jax.nn.relu(jnp.einsum('bsd,fd->bsf', x, W_fc)))
        y = jnp.einsum('bsf,df->bsd', h, W_proj)

        def step(mem, _):
            reset = jax.lax.stop_gradient(spike_fn(mem - THRESHOLD))
            mem_new = BETA * mem + y - reset * THRESHOLD
            spk = spike_fn(mem_new - THRESHOLD)
            return (mem_new, spk)
        mem0 = jnp.zeros_like(y)
        _, spks = jax.lax.scan(step, mem0, None, length=NUM_STEPS)
        return jnp.sum(spks, axis=0) / NUM_STEPS
    x = x + _L0_xattn_ref(_layernorm(x, axis=-1), ctx_1024, L0_xattn_Wq, L0_xattn_Wk, L0_xattn_Wv, L0_xattn_Wp, L0_xattn_bp)
    x = x + _L0_attn_ref(_layernorm(x, axis=-1), L0_attn_Wq, L0_attn_bq, L0_attn_Wk, L0_attn_bk, L0_attn_Wv, L0_attn_bv, L0_attn_Wo, L0_attn_bo)
    x = x + _L0_ffn_ref(_layernorm(x, axis=-1), L0_ffn_W_fc, L0_ffn_W_proj)
    return x

_drawn_inputs = setup_inputs


def setup_inputs(seed=0):
    import zlib

    import numpy as np

    out = dict(_drawn_inputs(seed))
    spreads = {}
    factors = {'L0_xattn_bp': 5.608,
     'L0_attn_Wq': 5.262,
     'L0_attn_bq': 30.413,
     'L0_attn_Wk': 4.988,
     'L0_attn_bk': 64.0,
     'L0_attn_bv': 6.251,
     'L0_attn_bo': 3.395}
    for name, (base, spread) in spreads.items():
        noise = np.random.default_rng([zlib.crc32(name.encode()), seed]).standard_normal(out[name].shape)
        drawn = base * np.exp(spread * noise) if base else spread * noise
        out[name] = jnp.asarray(drawn.astype(out[name].dtype))
    for name, factor in factors.items():
        out[name] = (out[name] * factor).astype(out[name].dtype)
    return out
```

```python
import numpy as np
import concourse.bass as bass
from concourse import mybir
from contextlib import ExitStack

F32 = mybir.dt.float32
F32R = mybir.dt.float32r
ALU = mybir.AluOpType
ACT = mybir.ActivationFunctionType
AX = mybir.AxisListType

B, N, M, D = 16, 64, 1601, 512
H, DH = 16, 32
FF = 2048
P = 128
DC = D // P
MP = M + M % 2
TOK = B * N
TT = TOK // P
JT = -(-M // P)
JL = M - (JT - 1) * P
KW = 402
KC = -(-MP // KW)
KWL = MP - (KC - 1) * KW
NBLK = H * DH // P
PAIRS = H // 2
TG = -(-JT // 2)
RING = 3
PT_RING = 4
P_RING = 4
SCALE = float(DH) ** -0.5
EPS = 1e-5

STEADY = [("V",), ("S", 0), ("K", 1, 0, 2), ("N", 0), ("S", 1), ("K", 1, 2, 4), ("N", 1), ("S", 2),
          ("T", 0), ("N", 2), ("S", 3), ("K", 2, 0, 4), ("N", 3), ("S", 4), ("K", 3, 0, 4), ("N", 4),
          ("S", 5), ("Y", 0), ("T", 1), ("N", 5), ("Y", 1), ("S", 6), ("Y", 2), ("T", 2), ("N", 6),
          ("Y", 3), ("S", 7), ("K", 4, 0, 4), ("N", 7), ("T", 3)]
LAST = [s for s in STEADY if s[0] != "Y" and s[:2] != ("K", 4)]


def ring_units(order, act, dve):
    units = []
    for step in order:
        if step[0] == "V":
            new = [("V", t) for t in range(JT)]
        elif step[0] == "K":
            new = [("K", (step[1], c)) for c in range(step[2], step[3])]
        elif step[0] == "T":
            new = [("T", (step[1], g)) for g in range(TG)]
        else:
            continue
        for kind, index in new:
            by = "dve" if kind == "K" or len(units) % 2 else "act"
            act += kind == "K" or by == "act"
            dve += by == "dve"
            units.append((kind, index, by, act, dve))
    return units


UNITS = ring_units(STEADY, 0, 0)
LAST_UNITS = ring_units(LAST, 0, 0)
NU = len(UNITS)
ACT_N, DVE_N = UNITS[-1][3], UNITS[-1][4]
FIRST = KC
assert NU % RING == 0
PV_CREDIT, EXP_CREDIT, O_CREDIT, S_CREDIT, ST_CREDIT = 8, 2, 1, 1, 16
PV_N = NBLK * TG


def kchunk(c):
    return c * KW, KW if c < KC - 1 else KWL


def jtile(t):
    return P if t < JT - 1 else JL


def prologue(nc, x, wq, wk, wv, q_dram, wk_s, wv_s, ident):
    ctx = ExitStack()
    with ctx:
        sb = lambda n, s, d=F32: ctx.enter_context(nc.sbuf_tensor(n, s, d))
        sem = lambda n: ctx.enter_context(nc.semaphore(n))
        xs = sb("p_x", [P, TT, D])
        xn = sb("p_xn", [P, TT, D])
        xnT = sb("p_xnT", [P, DC, TOK])
        wq_sb = sb("p_wq", [P, DC, D])
        wraw = sb("p_wraw", [P, 2, DC, D])
        qs = sb("p_q", [P, NBLK, 2, TOK], F32R)
        stats = sb("p_stats", [P, TT, 6])
        mv = sb("p_mv", [P, TT, 2])
        ve = sb("p_ve", [P, 5, TT])
        ps = [ctx.enter_context(nc.psum_tensor(f"p_ps{i}", [P, 512], F32)) for i in range(4)]
        x_in, wq_in, w_in = sem("p_x_in"), sem("p_wq_in"), sem("p_w_in")
        ident_ok, ln_step, root_ok, xn_ok = sem("p_ident"), sem("p_ln_step"), sem("p_root"), sem("p_xn")
        xt_ps, xt_ok, q_ps, q_hi, q_lo, q_out = (sem("p_xt_ps"), sem("p_xt_ok"), sem("p_q_ps"),
                                                 sem("p_q_hi"), sem("p_q_lo"), sem("p_q_out"))
        w_hi, w_lo = sem("p_w_hi"), sem("p_w_lo")
        block = ctx.enter_context(nc.Block())

        @block.sync
        def _(sp):
            sp.dma_start(xs[:], x.rearrange("(t p) d -> p t d", p=P)).then_inc(x_in, 16)
            sp.dma_start(wq_sb[:], wq.rearrange("(c p) e -> p c e", p=P)).then_inc(wq_in, 16)
            sp.dma_start(wraw[:, 0], wk.rearrange("(c p) e -> p c e", p=P)).then_inc(w_in, 16)
            sp.dma_start(wraw[:, 1], wv.rearrange("(c p) e -> p c e", p=P)).then_inc(w_in, 16)
            sp.wait_ge(q_lo, NBLK * 2)
            sp.dma_start(q_dram, qs[:].bitcast(F32).rearrange("p i s t -> p (i s) t")).then_inc(q_out, 16)
            sp.wait_ge(q_out, 16)

        @block.gpsimd
        def _(pool):
            pool.memset(ident[:], 0.0).then_inc(ident_ok, 1)
            pool.wait_ge(ident_ok, 1)
            pool.affine_select(out=ident[:], in_=ident[:], compare_op=ALU.not_equal, fill=1.0, base=0,
                               pattern=[[-1, P]], channel_multiplier=1).then_inc(ident_ok, 1)

        @block.vector
        def _(dve):
            step = 0
            dve.wait_ge(x_in, 16)
            for t in range(TT):
                dve.bn_stats(stats[:, t, :], xs[:, t, :]).then_inc(ln_step, 1)
            for t in range(TT):
                dve.wait_ge(ln_step, t + 1)
                dve.bn_aggr(mv[:, t, :], stats[:, t, :]).then_inc(ln_step, 1)
            step = 2 * TT
            dve.wait_ge(ln_step, step)
            dve.tensor_scalar_add(ve[:, 0, :], mv[:, :, 1], EPS).then_inc(ln_step, 1)
            dve.wait_ge(root_ok, 1)
            dve.reciprocal(ve[:, 2, :], ve[:, 1, :]).then_inc(ln_step, 1)
            dve.wait_ge(ln_step, step + 2)
            dve.tensor_tensor(ve[:, 3, :], ve[:, 2, :], ve[:, 2, :], ALU.mult).then_inc(ln_step, 1)
            dve.wait_ge(ln_step, step + 3)
            dve.tensor_tensor(ve[:, 4, :], ve[:, 3, :], ve[:, 0, :], ALU.mult).then_inc(ln_step, 1)
            dve.wait_ge(ln_step, step + 4)
            dve.tensor_scalar(ve[:, 3, :], ve[:, 4, :], -0.5, 1.5, ALU.mult, ALU.add).then_inc(ln_step, 1)
            dve.wait_ge(ln_step, step + 5)
            dve.tensor_tensor(ve[:, 4, :], ve[:, 2, :], ve[:, 3, :], ALU.mult).then_inc(ln_step, 1)
            dve.wait_ge(ln_step, step + 6)
            for t in range(TT):
                dve.tensor_scalar(xn[:, t, :], xs[:, t, :], mv[:, t, 0:1], ve[:, 4, t:t + 1],
                                  ALU.subtract, ALU.mult).then_inc(xn_ok, 1)
            for w, dst in enumerate((wk_s, wv_s)):
                dve.wait_ge(w_hi, w + 1)
                dve.tensor_tensor(dst[:, 1], wraw[:, w], dst[:, 0].bitcast(F32), ALU.subtract).then_inc(w_lo, 1)
            for n in range(NBLK * 2):
                i, half = n // 2, n % 2
                dve.wait_ge(q_hi, n + 1)
                dve.tensor_tensor(qs[:, i, 1, half * 512:half * 512 + 512], ps[n % 4][:],
                                  qs[:, i, 0, half * 512:half * 512 + 512].bitcast(F32),
                                  ALU.subtract).then_inc(q_lo, 1)

        @block.scalar
        def _(act):
            act.wait_ge(ln_step, 2 * TT + 1)
            act.activation(ve[:, 1, :], ve[:, 0, :], ACT.Sqrt).then_inc(root_ok, 1)
            for w, dst in enumerate((wk_s, wv_s)):
                act.wait_ge(w_in, 32)
                act.activation(dst[:, 0], wraw[:, w], ACT.Copy).then_inc(w_hi, 1)
            for t in range(TT):
                act.wait_ge(xt_ps, t + 1)
                act.activation(xnT[:, :, t * P:(t + 1) * P],
                               ps[t % 4][:].rearrange("p (c q) -> p c q", c=DC), ACT.Copy).then_inc(xt_ok, 1)
            for n in range(NBLK * 2):
                i, half = n // 2, n % 2
                act.wait_ge(q_ps, n + 1)
                act.activation(qs[:, i, 0, half * 512:half * 512 + 512], ps[n % 4][:], ACT.Copy).then_inc(q_hi, 1)

        @block.tensor
        def _(pe):
            pe.wait_ge(ident_ok, 2)
            for t in range(TT):
                pe.wait_ge(xn_ok, t + 1)
                if t >= 4:
                    pe.wait_ge(xt_ok, t - 3)
                for c in range(DC):
                    mm = pe.transpose(ps[t % 4][:, c * P:(c + 1) * P], xn[:, t, c * P:(c + 1) * P], ident[:])
                mm.then_inc(xt_ps, 1)
            pe.wait_ge(wq_in, 16)
            pe.wait_ge(xt_ok, TT)
            for n in range(NBLK * 2):
                i, half = n // 2, n % 2
                if n >= 4:
                    pe.wait_ge(q_lo, n - 3)
                for c in range(DC):
                    mm = pe.matmul(ps[n % 4][:], wq_sb[:, c, i * P:(i + 1) * P],
                                   xnT[:, c, half * 512:half * 512 + 512], start=(c == 0), stop=(c == DC - 1))
                mm.then_inc(q_ps, 1)


def cross_attention(nc, yT, q_dram, o_dram, wk_s, wv_s, ident):
    ctx = ExitStack()
    with ctx:
        sb = lambda n, s, d=F32: ctx.enter_context(nc.sbuf_tensor(n, s, d))
        sem = lambda n: ctx.enter_context(nc.semaphore(n))
        y_raw = sb("y_raw", [P, 2, MP])
        y_hi = sb("y_hi", [P, DC, MP], F32R)
        y_lo = sb("y_lo", [P, DC, MP], F32R)
        k_s = sb("k_s", [P, 2, 2, MP], F32R)
        v_sb = sb("v_sb", [P, JT, D])
        q_s = sb("q_s", [P, 2, NBLK * 2, P], F32R)
        prob = sb("prob", [P, P_RING, MP])
        pT = sb("pT", [P, PT_RING, 512])
        o_sb = sb("o_sb", [P, NBLK, N])
        peak = sb("peak", [P, 2, 4])
        total = sb("total", [P, 2, 4])
        s_ps = ctx.enter_context(nc.psum_tensor("s_ps", [P, KC * 512], F32))
        ring = [ctx.enter_context(nc.psum_tensor(f"ring{i}", [P, 512], F32)) for i in range(RING)]
        o_ps = ctx.enter_context(nc.psum_tensor("o_ps", [P, N], F32))
        s_v = s_ps[:].rearrange("p (c k) -> p c k", c=KC)

        y_in = [sem("y_in0"), sem("y_in1")]
        y_hi_ok, y_lo_ok, q_zero, q_in = sem("y_hi_ok"), sem("y_lo_ok"), sem("q_zero"), sem("q_in")
        full = sem("ring_full")
        act_out, dve_out = sem("ring_act_out"), sem("ring_dve_out")
        s_full = sem("scores_full")
        peak_step = sem("peak_step")
        bias_ok, exp_ok, norm_ok = sem("bias_ok"), sem("exp_ok"), sem("norm_ok")
        pv_ok = sem("pv_ok")
        o_out, o_stored = sem("o_out"), sem("o_stored")
        block = ctx.enter_context(nc.Block())

        def per_batch(batch, units):
            return {(kind, index): (u, by, FIRST + batch * ACT_N + a, FIRST + batch * DVE_N + d)
                    for u, (kind, index, by, a, d) in enumerate(units)}

        def emptied(eng, batch, units, u):
            _, _, by, a, d = units[u] if u >= 0 else UNITS[u]
            if u < 0:
                a, d = a - ACT_N, d - DVE_N
            if by == "act":
                eng.wait_ge(act_out, FIRST + batch * ACT_N + a)
            else:
                eng.wait_ge(dve_out, FIRST + batch * DVE_N + d)

        def bank(u):
            return ring[(FIRST + u) % RING]

        @block.sync
        def _(sp):
            sp.sem_inc(o_stored, ST_CREDIT)

            def load(batch, c):
                sp.dma_start(y_raw[:, c % 2, :],
                             yT[bass.ds(batch, 1), c].rearrange("a p m -> (a p) m")).then_inc(y_in[c % 2], 16)

            def load_q(batch):
                for k in range(4):
                    for second in range(2):
                        g = 2 * second + k % 2
                        sp.dma_start(
                            q_s[k * DH:(k + 1) * DH, second, :, (k % 2) * N:(k % 2 + 1) * N].bitcast(F32),
                            q_dram[g * DH:(g + 1) * DH, :, bass.ds(batch * N, N)]).then_inc(q_in, 16)

            for c in range(DC):
                if c >= 2:
                    sp.wait_ge(y_lo_ok, c - 1)
                load(0, c)
            sp.wait_ge(q_zero, 1)
            load_q(0)

            def store(batch):
                sp.wait_ge(o_out, O_CREDIT + NBLK * (batch + 1))
                sp.dma_start(o_dram[:, :, bass.ds(batch * N, N)], o_sb[:]).then_inc(o_stored, 16)

            with sp.Fori(0, B - 1) as b:
                for c in range(DC):
                    sp.wait_ge(y_lo_ok, DC * (b + 1) + c - 1)
                    load(b + 1, c)
                sp.wait_ge(s_full, S_CREDIT + 2 * PAIRS * (b + 1))
                load_q(b + 1)
                store(b)
            store(B - 1)
            sp.wait_ge(o_stored, ST_CREDIT + 16 * B)

        @block.gpsimd
        def _(pool):
            pool.memset(q_s[:].bitcast(F32), 0.0).then_inc(q_zero, 1)

        @block.scalar
        def _(act):
            act.sem_inc(exp_ok, EXP_CREDIT)
            act.sem_inc(o_out, O_CREDIT)

            def split(batch, c):
                act.wait_ge(y_in[c % 2], 16 * (2 * batch + c // 2 + 1))
                act.activation(y_hi[:, c, :], y_raw[:, c % 2, :], ACT.Copy).then_inc(y_hi_ok, 1)

            def empty_k(unit_no, i, c):
                at, w = kchunk(c)
                act.wait_ge(full, unit_no + 1)
                src = bank_of(unit_no)
                act.activation(k_s[0:64, i % 2, 0, at:at + w], src[0:64, 0:w], ACT.Copy)
                act.activation(k_s[64:P, i % 2, 1, at:at + w], src[64:P, 0:w], ACT.Copy).then_inc(act_out, 1)

            def bank_of(_):
                return current[0]

            current = [None]

            def run(batch, order, units):
                u = 0
                for step in order:
                    if step[0] == "V":
                        for t in range(JT):
                            if units[u][2] == "act":
                                if t < 2:
                                    act.wait_ge(pv_ok, PV_CREDIT + PV_N * batch)
                                act.wait_ge(full, FIRST + NU * batch + u + 1)
                                m = jtile(t)
                                act.activation(v_sb[0:m, t, :], bank(u)[0:m, :], ACT.Copy).then_inc(act_out, 1)
                            u += 1
                    elif step[0] == "K":
                        _, i, c0, c1 = step
                        if c0 == 0:
                            done = {1: 0, 2: 4, 3: 8, 4: 12}[i]
                            act.wait_ge(s_full, S_CREDIT + 2 * PAIRS * batch + done)
                        for c in range(c0, c1):
                            current[0] = bank(u)
                            empty_k(FIRST + NU * batch + u, i, c)
                            u += 1
                    elif step[0] == "S":
                        p = step[1]
                        pair = PAIRS * batch + p
                        act.wait_ge(pv_ok, PV_CREDIT + PV_N * batch + TG * (p // 2 - 1))
                        act.wait_ge(bias_ok, pair + 1)
                        dst = prob[:, p % P_RING, :]
                        act.activation(dst[:, 0:3 * KW].rearrange("p (c k) -> p c k", c=3),
                                       s_v[:, 0:3, 0:KW], ACT.Exp, bias=peak[:, p % 2, 2:3], scale=SCALE,
                                       accum_out=total[:, p % 2, 0:1]).then_inc(exp_ok, 1)
                        act.activation(dst[:, 3 * KW:M], s_v[:, 3, 0:M - 3 * KW], ACT.Exp,
                                       bias=peak[:, p % 2, 2:3], scale=SCALE,
                                       accum_out=total[:, p % 2, 1:2]).then_inc(exp_ok, 1)
                    elif step[0] == "Y":
                        if step[1] == 0:
                            last = max(n for n, x in enumerate(units) if x[0] == "K" and x[1][0] == 3)
                            act.wait_ge(full, FIRST + NU * batch + last + 1)
                        split(batch + 1, step[1])
                    elif step[0] == "T":
                        i = step[1]
                        for g in range(TG):
                            if units[u][2] == "act":
                                act.wait_ge(pv_ok, PV_CREDIT + PV_N * batch + TG * i + g - PT_RING + 1)
                                act.wait_ge(full, FIRST + NU * batch + u + 1)
                                m, w = (P, 512) if g < TG - 1 else (JL, 256)
                                act.activation(pT[0:m, (TG * i + g) % PT_RING, 0:w], bank(u)[0:m, 0:w],
                                               ACT.Copy).then_inc(act_out, 1)
                            u += 1
                        act.wait_ge(pv_ok, PV_CREDIT + PV_N * batch + TG * (i + 1))
                        if i == 0:
                            act.wait_ge(o_stored, ST_CREDIT + 16 * batch)
                        act.activation(o_sb[:, i, :], o_ps[:], ACT.Copy).then_inc(o_out, 1)

            for c in range(DC):
                split(0, c)
            for c in range(KC):
                current[0] = ring[c % RING]
                empty_k(c, 0, c)
            with act.Fori(0, B - 1) as b:
                run(b, STEADY, UNITS)
            run(B - 1, LAST, LAST_UNITS)

        @block.vector
        def _(dve):
            def split(batch, c):
                dve.wait_ge(y_hi_ok, DC * batch + c + 1)
                dve.tensor_tensor(y_lo[:, c, :], y_raw[:, c % 2, :], y_hi[:, c, :].bitcast(F32),
                                  ALU.subtract).then_inc(y_lo_ok, 1)

            def empty_k(src, act_count, i, c):
                at, w = kchunk(c)
                dve.wait_ge(act_out, act_count)
                k0, k1 = k_s[:, i % 2, 0, at:at + w], k_s[:, i % 2, 1, at:at + w]
                dve.tensor_tensor(k0[64:P], src[0:64, 0:w], k0[0:64].bitcast(F32), ALU.subtract)
                dve.tensor_tensor(k1[0:64], src[64:P, 0:w], k1[64:P].bitcast(F32),
                                  ALU.subtract).then_inc(dve_out, 1)

            def run(batch, order, units):
                u = 0
                for step in order:
                    if step[0] == "V":
                        for t in range(JT):
                            if units[u][2] == "dve":
                                if t < 2:
                                    dve.wait_ge(pv_ok, PV_CREDIT + PV_N * batch)
                                dve.wait_ge(full, FIRST + NU * batch + u + 1)
                                m = jtile(t)
                                dve.tensor_copy(v_sb[0:m, t, :], bank(u)[0:m, :]).then_inc(dve_out, 1)
                            u += 1
                    elif step[0] == "K":
                        _, i, c0, c1 = step
                        for c in range(c0, c1):
                            empty_k(bank(u), FIRST + batch * ACT_N + units[u][3], i, c)
                            u += 1
                    elif step[0] == "S":
                        p = step[1]
                        done = S_CREDIT + 2 * (PAIRS * batch + p)
                        small = 4 * (PAIRS * batch + p)
                        dve.wait_ge(s_full, done + 1)
                        dve.tensor_reduce(peak[:, p % 2, 0:1], s_v[:, 0:3, 0:KW], AX.XY, ALU.max).then_inc(peak_step, 1)
                        dve.wait_ge(s_full, done + 2)
                        dve.tensor_reduce(peak[:, p % 2, 1:2], s_v[:, 3, 0:M - 3 * KW], AX.X,
                                          ALU.max).then_inc(peak_step, 1)
                        dve.wait_ge(peak_step, small + 2)
                        dve.tensor_scalar(peak[:, p % 2, 2:3], peak[:, p % 2, 0:1], peak[:, p % 2, 1:2],
                                          -SCALE, ALU.max, ALU.mult).then_inc(bias_ok, 1)
                    elif step[0] == "N":
                        p = step[1]
                        small = 4 * (PAIRS * batch + p)
                        dve.wait_ge(exp_ok, EXP_CREDIT + 2 * (PAIRS * batch + p) + 2)
                        dve.tensor_tensor(total[:, p % 2, 2:3], total[:, p % 2, 0:1], total[:, p % 2, 1:2],
                                          ALU.add).then_inc(peak_step, 1)
                        dve.wait_ge(peak_step, small + 3)
                        dve.reciprocal(total[:, p % 2, 3:4], total[:, p % 2, 2:3]).then_inc(peak_step, 1)
                        dve.wait_ge(peak_step, small + 4)
                        dve.tensor_scalar(prob[:, p % P_RING, 0:M], prob[:, p % P_RING, 0:M],
                                          total[:, p % 2, 3:4], None, ALU.mult).then_inc(norm_ok, 1)
                    elif step[0] == "Y":
                        split(batch + 1, step[1])
                    elif step[0] == "T":
                        i = step[1]
                        for g in range(TG):
                            if units[u][2] == "dve":
                                dve.wait_ge(pv_ok, PV_CREDIT + PV_N * batch + TG * i + g - PT_RING + 1)
                                dve.wait_ge(full, FIRST + NU * batch + u + 1)
                                m, w = (P, 512) if g < TG - 1 else (JL, 256)
                                dve.tensor_copy(pT[0:m, (TG * i + g) % PT_RING, 0:w],
                                                bank(u)[0:m, 0:w]).then_inc(dve_out, 1)
                            u += 1

            for c in range(DC):
                split(0, c)
            for c in range(KC):
                empty_k(ring[c % RING], c + 1, 0, c)
            with dve.Fori(0, B - 1) as b:
                run(b, STEADY, UNITS)
            run(B - 1, LAST, LAST_UNITS)

        @block.tensor
        def _(pe):
            def three(out, left, right, rows, cols):
                for c in range(DC):
                    for n, (a, b) in enumerate(((0, 0), (1, 0), (0, 1))):
                        mm = pe.matmul(out, left(a, c), right(b, c),
                                       start=(c == 0 and n == 0), stop=(c == DC - 1 and n == 2))
                return mm

            y_part = (y_hi, y_lo)

            def project_k(out, i, c):
                at, w = kchunk(c)
                return three(out[:, 0:w], lambda a, d: wk_s[:, a, d, i * P:(i + 1) * P],
                             lambda a, d: y_part[a][:, d, at:at + w], P, w)

            def project_v(out, t):
                m = jtile(t)
                return three(out[0:m, :], lambda a, d: y_part[a][:, d, t * P:t * P + m],
                             lambda a, d: wv_s[:, a, d, :], m, D)

            def scores(batch, p):
                pair = PAIRS * batch + p
                for c in range(KC):
                    at, w = kchunk(c)
                    if c == 0:
                        pe.wait_ge(exp_ok, EXP_CREDIT + 2 * pair - 1)
                    if c == KC - 1:
                        pe.wait_ge(exp_ok, EXP_CREDIT + 2 * pair)
                    for part in range(2):
                        mm = pe.matmul(s_v[:, c, 0:w], q_s[:, p % 2, p // 2 * 2 + part, :],
                                       k_s[:, (p // 2) % 2, p % 2, at:at + w], start=(part == 0), stop=(part == 1))
                    if c >= KC - 2:
                        mm.then_inc(s_full, 1)

            def run(batch, order, units):
                u = 0
                number = {(x[0], x[1]): n for n, x in enumerate(units)}
                for step in order:
                    if step[0] == "V":
                        pe.wait_ge(y_lo_ok, DC * (batch + 1))
                        for t in range(JT):
                            emptied(pe, batch, units, u - RING)
                            project_v(bank(u), t).then_inc(full, 1)
                            u += 1
                    elif step[0] == "K":
                        _, i, c0, c1 = step
                        if i == NBLK:
                            pe.wait_ge(y_lo_ok, DC * (batch + 2))
                        for c in range(c0, c1):
                            emptied(pe, batch, units, u - RING)
                            project_k(bank(u), i % NBLK, c).then_inc(full, 1)
                            u += 1
                    elif step[0] == "S":
                        p = step[1]
                        if p == 0:
                            pe.wait_ge(q_in, 128 * (batch + 1))
                            behind = DVE_N - UNITS[NU - TG - 1][4]
                            pe.wait_ge(dve_out, FIRST + DVE_N * batch - behind)
                        elif p % 2 == 0:
                            d = units[number["K", (p // 2, KC - 1)]][4]
                            pe.wait_ge(dve_out, FIRST + DVE_N * batch + d)
                        scores(batch, p)
                    elif step[0] == "T":
                        i = step[1]
                        first = u
                        pe.wait_ge(norm_ok, PAIRS * batch + 2 * i + 2)
                        for g in range(TG + 2):
                            if g < TG:
                                emptied(pe, batch, units, u - RING)
                                for k, t in enumerate(range(2 * g, min(2 * g + 2, JT))):
                                    m = jtile(t)
                                    for second in range(2):
                                        at = k * 256 + second * P
                                        mm = pe.transpose(
                                            bank(u)[0:m, at:at + P],
                                            prob[:, (2 * i + second) % P_RING, t * P:t * P + m], ident[:])
                                mm.then_inc(full, 1)
                                u += 1
                            if g >= 2:
                                h = g - 2
                                if h == 0:
                                    pe.wait_ge(o_out, O_CREDIT + NBLK * batch + i)
                                emptied(pe, batch, units, first + h)
                                for k, t in enumerate(range(2 * h, min(2 * h + 2, JT))):
                                    m = jtile(t)
                                    for head in range(4):
                                        at = k * 256 + head * N
                                        mm = pe.matmul(
                                            o_ps[head * DH:(head + 1) * DH, :],
                                            v_sb[0:m, t, (4 * i + head) * DH:(4 * i + head + 1) * DH],
                                            pT[0:m, (TG * i + h) % PT_RING, at:at + N],
                                            start=(t == 0), stop=(t == JT - 1))
                                mm.then_inc(pv_ok, 1)

            pe.sem_inc(pv_ok, PV_CREDIT)
            pe.sem_inc(s_full, S_CREDIT)
            pe.wait_ge(y_lo_ok, DC)
            for c in range(KC):
                if c >= RING:
                    pe.wait_ge(dve_out, c - RING + 1)
                project_k(ring[c % RING], 0, c).then_inc(full, 1)
            pe.wait_ge(dve_out, KC)
            with pe.Fori(0, B - 1) as b:
                run(b, STEADY, UNITS)
            run(B - 1, LAST, LAST_UNITS)


def three_passes(pe, out, left, right):
    for c in range(DC):
        for n, (a, b) in enumerate(((0, 0), (1, 0), (0, 1))):
            mm = pe.matmul(out, left(a, c), right(b, c),
                           start=(c == 0 and n == 0), stop=(c == DC - 1 and n == 2))
    return mm


def project_and_norm(nc, tag, left, w, x, xnT, rows, ident, load=None, split_hi=None, split_lo=None,
                     ready=None, bias=None):
    ctx = ExitStack()
    with ctx:
        sb = lambda n, s, d=F32: ctx.enter_context(nc.sbuf_tensor(f"{tag}_{n}", s, d))
        sem = lambda n: ctx.enter_context(nc.semaphore(f"{tag}_{n}"))
        stats, mv = sb("stats", [P, TT, 6]), sb("mv", [P, TT, 2])
        ve = sb("ve", [P, 5, TT])
        bank = [ctx.enter_context(nc.psum_tensor(f"{tag}_ps{i}", [P, 512], F32)) for i in range(8)]
        biased, added, step, var_ok, root_ok = sem("biased"), sem("added"), sem("step"), sem("var"), sem("root")
        xn_ok, full, turned, hi_ok, lo_ok = sem("xn_ok"), sem("full"), sem("turned"), sem("hi_ok"), sem("lo_ok")
        block = ctx.enter_context(nc.Block())
        xn = rows.rearrange("p (t d) -> p t d", t=TT)
        HALF = TT // 2

        @block.sync
        def _(sp):
            if load:
                load(sp)

        @block.gpsimd
        def _(pool):
            bias(pool, biased)

        @block.vector
        def _(dve):
            if split_lo:
                split_lo(dve)
            n = 0
            for half in range(2):
                tiles = range(half * HALF, (half + 1) * HALF)
                for t in tiles:
                    dve.wait_ge(biased, t + 1)
                    dve.wait_ge(full, t + 1)
                    dve.tensor_tensor(x[:, t, :], bank[t % 4][:], x[:, t, :], ALU.add).then_inc(added, 1)
                for t in tiles:
                    dve.wait_ge(added, t + 1)
                    dve.bn_stats(stats[:, t, :], x[:, t, :]).then_inc(step, 1)
                    n += 1
                first = n - HALF
                for k, t in enumerate(tiles):
                    dve.wait_ge(step, first + k + 1)
                    dve.bn_aggr(mv[:, t, :], stats[:, t, :]).then_inc(step, 1)
                    n += 1
                at = slice(half * HALF, (half + 1) * HALF)
                dve.wait_ge(step, n)
                dve.tensor_scalar_add(ve[:, 0, at], mv[:, at, 1], EPS).then_inc(var_ok, 1)
                dve.wait_ge(root_ok, half + 1)
                dve.reciprocal(ve[:, 2, at], ve[:, 1, at]).then_inc(step, 1)
                n += 1
                for out, a, b in ((3, 2, 2), (4, 3, 0)):
                    dve.wait_ge(step, n)
                    dve.tensor_tensor(ve[:, out, at], ve[:, a, at], ve[:, b, at], ALU.mult).then_inc(step, 1)
                    n += 1
                dve.wait_ge(step, n)
                dve.tensor_scalar(ve[:, 3, at], ve[:, 4, at], -0.5, 1.5, ALU.mult, ALU.add).then_inc(step, 1)
                n += 1
                dve.wait_ge(step, n)
                dve.tensor_tensor(ve[:, 4, at], ve[:, 2, at], ve[:, 3, at], ALU.mult).then_inc(step, 1)
                n += 1
                dve.wait_ge(step, n)
                for t in tiles:
                    dve.tensor_scalar(xn[:, t, :], x[:, t, :], mv[:, t, 0:1], ve[:, 4, t:t + 1],
                                      ALU.subtract, ALU.mult).then_inc(xn_ok, 1)
            for t in range(TT):
                dve.wait_ge(hi_ok, t + 1)
                dve.tensor_tensor(xnT[:, 1, :, t * P:(t + 1) * P],
                                  bank[4 + t % 4][:].rearrange("p (c q) -> p c q", c=DC),
                                  xnT[:, 0, :, t * P:(t + 1) * P].bitcast(F32), ALU.subtract).then_inc(lo_ok, 1)

        @block.scalar
        def _(act):
            if split_hi:
                split_hi(act)
            for half in range(2):
                at = slice(half * HALF, (half + 1) * HALF)
                act.wait_ge(var_ok, half + 1)
                act.activation(ve[:, 1, at], ve[:, 0, at], ACT.Sqrt).then_inc(root_ok, 1)
            for t in range(TT):
                act.wait_ge(turned, t + 1)
                act.activation(xnT[:, 0, :, t * P:(t + 1) * P],
                               bank[4 + t % 4][:].rearrange("p (c q) -> p c q", c=DC),
                               ACT.Copy).then_inc(hi_ok, 1)

        @block.tensor
        def _(pe):
            if ready:
                ready(pe)
            for t in range(TT):
                if t >= 4:
                    pe.wait_ge(added, t - 3)
                three_passes(pe, bank[t % 4][:], lambda a, c: left[:, a, c, t * P:(t + 1) * P],
                             lambda a, c: w[:, a, c, :]).then_inc(full, 1)
            for t in range(TT):
                pe.wait_ge(xn_ok, t + 1)
                if t >= 4:
                    pe.wait_ge(lo_ok, t - 3)
                for c in range(DC):
                    mm = pe.transpose(bank[4 + t % 4][:, c * P:(c + 1) * P], xn[:, t, c * P:(c + 1) * P], ident[:])
                mm.then_inc(turned, 1)


def cross_output(nc, x, o_dram, wp, bp, att, x_sb, xnT, w_raw, w_in, attn_w, ident):
    ctx = ExitStack()
    with ctx:
        rows = ctx.enter_context(nc.sbuf_tensor("co_rows", [P, TT * D], F32))
        wp_raw = ctx.enter_context(nc.sbuf_tensor("wp_raw", [P, DC, D], F32))
        wp_s = ctx.enter_context(nc.sbuf_tensor("wp_s", [P, 2, DC, D], F32R))
        bp_sb = ctx.enter_context(nc.sbuf_tensor("bp_sb", [P, D], F32))
        sem = lambda n: ctx.enter_context(nc.semaphore(n))
        wp_in, o_in, x_in, bp_in = sem("wp_in"), sem("o_in"), sem("x_in"), sem("bp_in")
        split_up, split_low = sem("co_split_hi"), sem("co_split_lo")
        o_raw = rows[:].rearrange("p (c t) -> p c t", c=DC)

        def load(sp):
            sp.dma_start(wp_raw[:], wp.rearrange("(c p) e -> p c e", p=P)).then_inc(wp_in, 16)
            sp.dma_start(o_raw, o_dram).then_inc(o_in, 16)
            sp.dma_start(x_sb[:], x.rearrange("(t p) d -> p t d", p=P)).then_inc(x_in, 16)
            sp.dma_start(bp_sb[:], bp.rearrange("(a d) -> a d", a=1).broadcast_to((P, D))).then_inc(bp_in, 16)
            for n, w in enumerate(attn_w):
                sp.dma_start(w_raw[:, n], w.rearrange("(c p) e -> p c e", p=P)).then_inc(w_in[n], 16)

        def split_hi(act):
            act.wait_ge(wp_in, 16)
            act.activation(wp_s[:, 0], wp_raw[:], ACT.Copy).then_inc(split_up, 1)
            act.wait_ge(o_in, 16)
            for c in range(DC):
                act.activation(att[:, 0, c, :], o_raw[:, c, :], ACT.Copy).then_inc(split_up, 1)

        def split_lo(dve):
            dve.wait_ge(split_up, 1)
            dve.tensor_tensor(wp_s[:, 1], wp_raw[:], wp_s[:, 0].bitcast(F32), ALU.subtract).then_inc(split_low, 1)
            for c in range(DC):
                dve.wait_ge(split_up, c + 2)
                dve.tensor_tensor(att[:, 1, c, :], o_raw[:, c, :], att[:, 0, c, :].bitcast(F32),
                                  ALU.subtract).then_inc(split_low, 1)

        def ready(pe):
            pe.wait_ge(split_low, 1 + DC)

        def bias(pool, biased):
            pool.wait_ge(x_in, 16)
            pool.wait_ge(bp_in, 16)
            for t in range(TT):
                pool.tensor_tensor(x_sb[:, t, :], x_sb[:, t, :], bp_sb[:], ALU.add).then_inc(biased, 1)

        project_and_norm(nc, "co", att, wp_s, x_sb, xnT, rows[:], ident, load, split_hi, split_lo, ready, bias)


def qkv(nc, xnT, w_raw, w_in, bq, bk, bv, qT, kT, v_sb):
    ctx = ExitStack()
    with ctx:
        sb = lambda n, s, d=F32: ctx.enter_context(nc.sbuf_tensor(n, s, d))
        sem = lambda n: ctx.enter_context(nc.semaphore(n))
        w_s = sb("aw_s", [P, 3, 2, DC, D], F32R)
        b_col = sb("b_col", [P, 2, NBLK])
        bv_sb = sb("bv_sb", [P, D])
        bank = [ctx.enter_context(nc.psum_tensor(f"qkv_ps{i}", [P, 512], F32)) for i in range(8)]
        b_in, bv_in, hi_ok, lo_ok = sem("b_in"), sem("bv_in"), sem("aw_hi"), sem("aw_lo")
        full, qk_out, v_out = sem("qkv_full"), sem("qk_out"), sem("v_out")
        block = ctx.enter_context(nc.Block())
        QK = 2 * NBLK * 2

        @block.sync
        def _(sp):
            for n, b in enumerate((bq, bk)):
                sp.dma_start(b_col[:, n, :], b).then_inc(b_in, 16)
            sp.dma_start(bv_sb[:], bv.rearrange("(a d) -> a d", a=1).broadcast_to((P, D))).then_inc(bv_in, 16)

        @block.scalar
        def _(act):
            for n in range(3):
                act.wait_ge(w_in[n], 16)
                act.activation(w_s[:, n, 0], w_raw[:, n], ACT.Copy).then_inc(hi_ok, 1)
            act.wait_ge(b_in, 32)
            for u in range(QK):
                n, i, half = u // 8, u // 2 % NBLK, u % 2
                act.wait_ge(full, u + 1)
                act.activation((qT, kT)[n][:, i, half * 512:(half + 1) * 512], bank[u % 8][:], ACT.Identity,
                               bias=b_col[:, n, i:i + 1]).then_inc(qk_out, 1)

        @block.vector
        def _(dve):
            for n in range(3):
                dve.wait_ge(hi_ok, n + 1)
                dve.tensor_tensor(w_s[:, n, 1], w_raw[:, n], w_s[:, n, 0].bitcast(F32),
                                  ALU.subtract).then_inc(lo_ok, 1)
            dve.wait_ge(bv_in, 16)
            for t in range(TT):
                dve.wait_ge(full, QK + t + 1)
                dve.tensor_tensor(v_sb[:, t, :], bank[(QK + t) % 8][:], bv_sb[:], ALU.add).then_inc(v_out, 1)

        @block.tensor
        def _(pe):
            for u in range(QK):
                n, i, half = u // 8, u // 2 % NBLK, u % 2
                pe.wait_ge(lo_ok, n + 1)
                if u >= 8:
                    pe.wait_ge(qk_out, u - 7)
                three_passes(pe, bank[u % 8][:], lambda a, c: w_s[:, n, a, c, i * P:(i + 1) * P],
                             lambda a, c: xnT[:, a, c, half * 512:(half + 1) * 512]).then_inc(full, 1)
            pe.wait_ge(lo_ok, 3)
            for t in range(TT):
                pe.wait_ge(qk_out, QK - 7 + t)
                three_passes(pe, bank[(QK + t) % 8][:], lambda a, c: xnT[:, a, c, t * P:(t + 1) * P],
                             lambda a, c: w_s[:, 2, a, c, :]).then_inc(full, 1)


def self_attention(nc, qT, kT, v_sb, alibi, wo, att, wo_s, ident):
    ctx = ExitStack()
    with ctx:
        sb = lambda n, s, d=F32: ctx.enter_context(nc.sbuf_tensor(n, s, d))
        sem = lambda n: ctx.enter_context(nc.semaphore(n))
        wo_raw = sb("wo_raw", [P, DC, D])
        al_sb = sb("al_sb", [P, 4, 4 * N])
        sc = sb("sc", [P, 2, H, N])
        ex = sb("ex", [P, 2, H, N])
        pr = sb("pr", [P, 2, H * N])
        pT = sb("sa_pT", [P, 2, H, N])
        small = sb("sa_small", [P, 2, 3, H])
        s_ps = ctx.enter_context(nc.psum_tensor("sa_s", [P, 4, 512], F32))
        t_ps = [ctx.enter_context(nc.psum_tensor(f"sa_t{i}", [P, 4, 2, N], F32)) for i in range(2)]
        o_ps = ctx.enter_context(nc.psum_tensor("sa_o", [P, 2, 512], F32))
        al_in, wo_in, wo_hi, wo_lo = sem("al_in"), sem("wo_in"), sem("wo_hi"), sem("wo_lo")
        s_full, s_out, max_ok, sub_ok, exp_ok = sem("sa_s_full"), sem("sa_s_out"), sem("sa_max"), sem("sa_sub"), sem("sa_exp")
        sum_ok, rec_ok, pr_ok = sem("sa_sum"), sem("sa_rec"), sem("sa_pr")
        turned, pT_act, pT_dve, pv_ok, o_hi, o_lo = (sem("sa_turned"), sem("sa_pT_act"), sem("sa_pT_dve"),
                                                     sem("sa_pv"), sem("sa_o_hi"), sem("sa_o_lo"))
        block = ctx.enter_context(nc.Block())

        @block.sync
        def _(sp):
            sp.dma_start(al_sb[:].rearrange("p g k -> p (g k)"), alibi.broadcast_to((P, H * N))).then_inc(al_in, 16)
            sp.dma_start(wo_raw[:], wo.rearrange("(c p) e -> p c e", p=P)).then_inc(wo_in, 16)

        @block.gpsimd
        def _(pool):
            for t in range(TT + 1):
                if t < TT:
                    k = t % 2
                    pool.wait_ge(max_ok, t + 1)
                    if t >= 2:
                        pool.wait_ge(pr_ok, t - 1)
                    pool.tensor_tensor(ex[:, k], sc[:, k], small[:, k, 0, :].unsqueeze(2).broadcast_to((P, H, N)),
                                       ALU.subtract).then_inc(sub_ok, 1)
                if t >= 1:
                    k = (t - 1) % 2
                    pool.wait_ge(rec_ok, t)
                    if t >= 3:
                        pool.wait_ge(turned, 2 * (t - 2))
                    pool.tensor_tensor(pr[:, k].rearrange("p (h n) -> p h n", h=H), ex[:, k],
                                       small[:, k, 2, :].unsqueeze(2).broadcast_to((P, H, N)),
                                       ALU.mult).then_inc(pr_ok, 1)

        def turned_blocks(t, n):
            for a in range(2):
                for b in range(2):
                    yield (pT[b * N:(b + 1) * N, t % 2, 8 * n + a:8 * n + 8:2, :],
                           t_ps[n][a * N:(a + 1) * N, :, b, :])

        @block.vector
        def _(dve):
            dve.wait_ge(al_in, 16)

            def soft(t):
                k = t % 2
                dve.wait_ge(s_full, t + 1)
                if t >= 2:
                    dve.wait_ge(sub_ok, t - 1)
                dve.scalar_tensor_tensor(sc[:, k].rearrange("p (g i) n -> p g (i n)", g=4), s_ps[:, :, 0:4 * N],
                                         SCALE, al_sb[:], ALU.mult, ALU.add).then_inc(s_out, 1)
                dve.wait_ge(s_out, t + 1)
                dve.tensor_reduce(small[:, k, 0, :], sc[:, k], AX.X, ALU.max).then_inc(max_ok, 1)

            def normal(t):
                k = t % 2
                dve.wait_ge(exp_ok, t + 1)
                if t >= 2:
                    dve.wait_ge(pr_ok, t - 1)
                dve.tensor_reduce(small[:, k, 1, :], ex[:, k], AX.X, ALU.add).then_inc(sum_ok, 1)
                dve.wait_ge(sum_ok, t + 1)
                dve.reciprocal(small[:, k, 2, :], small[:, k, 1, :]).then_inc(rec_ok, 1)

            def turn(t):
                for n in range(2):
                    dve.wait_ge(turned, 2 * t + n + 1)
                    dve.wait_ge(pT_act, 2 * t + n + 1)
                    if t >= 2:
                        dve.wait_ge(pv_ok, t - 1)
                    for dst, src in list(turned_blocks(t, n))[2:]:
                        ins = dve.tensor_copy(dst, src)
                    ins.then_inc(pT_dve, 1)

            def low(t):
                dve.wait_ge(o_hi, t + 1)
                dst = att[:, :, :, t * P:(t + 1) * P].rearrange("p s i (b q) -> p s b i q", b=2)
                src = o_ps[:, :, 0:4 * N].rearrange("p b (i q) -> p b i q", i=4)
                for b in range(2):
                    ins = dve.tensor_tensor(dst[:, 1, b], src[:, b], dst[:, 0, b].bitcast(F32), ALU.subtract)
                ins.then_inc(o_lo, 1)

            for t in range(TT + 2):
                if 1 <= t <= TT:
                    normal(t - 1)
                if t == 1:
                    dve.wait_ge(wo_hi, 1)
                    dve.tensor_tensor(wo_s[:, 1], wo_raw[:], wo_s[:, 0].bitcast(F32), ALU.subtract).then_inc(wo_lo, 1)
                if t >= 2:
                    turn(t - 2)
                    low(t - 2)
                if t < TT:
                    soft(t)
            dve.wait_ge(wo_lo, 1)

        @block.scalar
        def _(act):
            act.wait_ge(wo_in, 16)
            act.activation(wo_s[:, 0], wo_raw[:], ACT.Copy).then_inc(wo_hi, 1)
            for t in range(TT + 2):
                if t >= 2:
                    u = t - 2
                    for n in range(2):
                        act.wait_ge(turned, 2 * u + n + 1)
                        if u >= 2:
                            act.wait_ge(pv_ok, u - 1)
                        for dst, src in list(turned_blocks(u, n))[:2]:
                            ins = act.activation(dst, src, ACT.Copy)
                        ins.then_inc(pT_act, 1)
                    act.wait_ge(pv_ok, u + 1)
                    dst = att[:, 0, :, u * P:(u + 1) * P].rearrange("p i (b q) -> p b i q", b=2)
                    src = o_ps[:, :, 0:4 * N].rearrange("p b (i q) -> p b i q", i=4)
                    for b in range(2):
                        ins = act.activation(dst[:, b], src[:, b], ACT.Copy)
                    ins.then_inc(o_hi, 1)
                if t < TT:
                    act.wait_ge(sub_ok, t + 1)
                    act.activation(ex[:, t % 2], ex[:, t % 2], ACT.Exp).then_inc(exp_ok, 1)

        @block.tensor
        def _(pe):
            def scores(t):
                if t >= 1:
                    pe.wait_ge(s_out, t)
                for i in range(4):
                    for g in range(4):
                        rows = slice(g * DH, (g + 1) * DH)
                        for b in range(2):
                            at = slice(t * P + b * N, t * P + (b + 1) * N)
                            mm = pe.matmul(s_ps[b * N:(b + 1) * N, g, i * N:(i + 1) * N], qT[rows, i, at],
                                           kT[rows, i, at], start=True, stop=True)
                mm.then_inc(s_full, 1)

            def transposes(t):
                pe.wait_ge(pr_ok, t + 1)
                for n in range(2):
                    if t >= 1:
                        pe.wait_ge(pT_dve, 2 * t + n - 1)
                    for j in range(4):
                        mm = pe.transpose(t_ps[n][:, j].rearrange("p b q -> p (b q)"),
                                          pr[:, t % 2, (4 * n + j) * P:(4 * n + j + 1) * P], ident[:])
                    mm.then_inc(turned, 1)

            def weigh(t):
                pe.wait_ge(pT_dve, 2 * t + 2)
                if t >= 1:
                    pe.wait_ge(o_lo, t)
                for b in range(2):
                    rows = slice(b * N, (b + 1) * N)
                    for i in range(4):
                        for g in range(4):
                            mm = pe.matmul(o_ps[g * DH:(g + 1) * DH, b, i * N:(i + 1) * N],
                                           v_sb[rows, t, (4 * i + g) * DH:(4 * i + g + 1) * DH],
                                           pT[rows, t % 2, 4 * g + i, :], start=True, stop=True)
                mm.then_inc(pv_ok, 1)

            for t in range(TT + 1):
                if t < TT:
                    scores(t)
                if t >= 1:
                    transposes(t - 1)
                    weigh(t - 1)


def feed_forward(nc, x_sb, xnT, w_ffn, out):
    FB = FF // P
    HT = TOK // 2
    STEPS, BETA = 5, 0.9
    ctx = ExitStack()
    with ctx:
        sb = lambda n, s, d=F32: ctx.enter_context(nc.sbuf_tensor(n, s, d))
        sem = lambda n: ctx.enter_context(nc.semaphore(n))
        RAW, WS, HS, HB = 4, 3, 3, 3
        w_raw = sb("f_raw", [P, RAW, 2 * D])
        w_s = sb("f_w", [P, WS, 2, 2 * D], F32R)
        relu = sb("f_relu", [P, HS, HT])
        sq = sb("f_sq", [P, HS, HT])
        h_s = sb("f_h", [P, HS, 2, HT], F32R)
        y_sb = sb("f_y", [P, TT, D])
        acc = sb("f_acc", [P, 2, 4, D])
        y_ps = [ctx.enter_context(nc.psum_tensor(f"f_y{i}", [P, 512], F32)) for i in range(4)]
        h_ps = [ctx.enter_context(nc.psum_tensor(f"f_h{i}", [P, 512], F32)) for i in range(HB)]
        w_in = [sem(f"f_w_in{n}") for n in range(RAW)]
        w_hi, w_lo, h_full, relu_ok, sq_ok, h_hi, h_lo = (sem("f_w_hi"), sem("f_w_lo"), sem("f_h_full"), sem("f_relu"),
                                                          sem("f_sq"), sem("f_h_hi"), sem("f_h_lo"))
        y_part, y_out, spike, done, stored = (sem("f_y_part"), sem("f_y_out"), sem("f_spike"), sem("f_done"),
                                              sem("f_stored"))
        block = ctx.enter_context(nc.Block())
        ALL = 2 * FB

        @block.sync
        def _(sp):
            for n in range(ALL):
                if n >= RAW:
                    sp.wait_ge(w_lo, n - RAW + 1)
                sp.dma_start(w_raw[:, n % RAW, :], w_ffn[n % FB]).then_inc(w_in[n % RAW], 16)
            for t in range(TT):
                sp.wait_ge(done, t + 1)
                sp.dma_start(out[t * P:(t + 1) * P, :], x_sb[:, t, :]).then_inc(stored, 16)
            sp.wait_ge(stored, 16 * TT)

        @block.scalar
        def _(act):
            def weights(n):
                act.wait_ge(w_in[n % RAW], 16 * (n // RAW + 1))
                if n >= WS:
                    act.wait_ge(y_part, n - WS + 1)
                act.activation(w_s[:, n % WS, 0, :], w_raw[:, n % RAW, :], ACT.Copy).then_inc(w_hi, 1)

            weights(0)
            weights(1)
            for n in range(ALL):
                act.wait_ge(h_full, n + 1)
                act.activation(relu[:, n % HS, :], h_ps[n % HB][:], ACT.Relu).then_inc(relu_ok, 1)
                if n + 2 < ALL:
                    weights(n + 2)
                act.wait_ge(sq_ok, n + 1)
                if n >= HS:
                    act.wait_ge(y_part, n - HS + 1)
                act.activation(h_s[:, n % HS, 0, :], sq[:, n % HS, :], ACT.Copy).then_inc(h_hi, 1)
                if n % FB == FB - 1:
                    half = n // FB
                    act.wait_ge(y_part, n + 1)
                    for k in range(4):
                        act.activation(y_sb[:, 4 * half + k, :], y_ps[k][:], ACT.Copy).then_inc(y_out, 1)

        @block.vector
        def _(dve):
            count = [0]

            def follow(ins):
                count[0] += 1
                ins.then_inc(spike, 1)

            def weights(n):
                dve.wait_ge(w_hi, n + 1)
                dve.tensor_tensor(w_s[:, n % WS, 1, :], w_raw[:, n % RAW, :], w_s[:, n % WS, 0, :].bitcast(F32),
                                  ALU.subtract).then_inc(w_lo, 1)

            def spikes(t):
                y, (m0, m1, charge, total) = y_sb[:, t, :], (acc[:, t % 2, k, :] for k in range(4))
                dve.wait_ge(y_out, t + 1)
                follow(dve.tensor_scalar(total, y, 1.0, None, ALU.is_gt))
                mem, new = y, m0
                for step in range(1, STEPS):
                    follow(dve.scalar_tensor_tensor(charge, mem, BETA, y, ALU.mult, ALU.add))
                    dve.wait_ge(spike, count[0])
                    follow(dve.scalar_tensor_tensor(new, mem, 1.0, charge, ALU.is_gt, ALU.subtract))
                    dve.wait_ge(spike, count[0])
                    follow(dve.scalar_tensor_tensor(total, new, -1.0, total, ALU.is_lt, ALU.add))
                    nxt = m1 if new is m0 else m0
                    follow(dve.tensor_scalar(nxt, new, -1.0, None, ALU.mult))
                    dve.wait_ge(spike, count[0])
                    mem, new = nxt, new
                    new = m1 if mem is m0 else m0
                dve.scalar_tensor_tensor(x_sb[:, t, :], total, 1.0 / STEPS, x_sb[:, t, :],
                                         ALU.mult, ALU.add).then_inc(done, 1)

            weights(0)
            weights(1)
            for n in range(ALL):
                dve.wait_ge(relu_ok, n + 1)
                dve.scalar_tensor_tensor(sq[:, n % HS, :], h_ps[n % HB][:], 0.0, relu[:, n % HS, :],
                                         ALU.max, ALU.mult).then_inc(sq_ok, 1)
                if n + 2 < ALL:
                    weights(n + 2)
                dve.wait_ge(h_hi, n + 1)
                dve.tensor_tensor(h_s[:, n % HS, 1, :], sq[:, n % HS, :], h_s[:, n % HS, 0, :].bitcast(F32),
                                  ALU.subtract).then_inc(h_lo, 1)
                if n >= FB and n % 4 == 1:
                    spikes((n - FB) // 4)
            for t in range(TT // 2, TT):
                spikes(t)

        @block.tensor
        def _(pe):
            def hidden(n):
                half = n // FB
                pe.wait_ge(w_lo, n + 1)
                if n >= HB:
                    pe.wait_ge(sq_ok, n - HB + 1)
                w = w_s[:, n % WS].rearrange("p s (m c f) -> p s m c f", m=2, c=DC)
                three_passes(pe, h_ps[n % HB][:], lambda a, c: w[:, a, 0, c, :],
                             lambda a, c: xnT[:, a, c, half * HT:(half + 1) * HT]).then_inc(h_full, 1)

            def project(n):
                f = n % FB
                pe.wait_ge(h_lo, n + 1)
                if f == 0 and n:
                    pe.wait_ge(y_out, 4)
                for k in range(4):
                    for m, (a, b) in enumerate(((0, 0), (1, 0), (0, 1))):
                        mm = pe.matmul(y_ps[k][:], h_s[:, n % HS, a, k * P:(k + 1) * P], w_s[:, n % WS, b, D:2 * D],
                                       start=(f == 0 and m == 0), stop=(f == FB - 1 and m == 2))
                mm.then_inc(y_part, 1)

            for n in range(ALL + 1):
                if n < ALL:
                    hidden(n)
                if n >= 1:
                    project(n - 1)


def perceiver(nc, x, yT, xwq, xwk, xwv, xwp, xbp, awq, abq, awk, abk, awv, abv, awo, abo, w_ffn, alibi,
              out, q_dram, o_dram):
    ctx = ExitStack()
    with ctx:
        sb = lambda n, s, d=F32: ctx.enter_context(nc.sbuf_tensor(n, s, d))
        ident = sb("ident", [P, P])
        with nc.sbuf_tensor("wk_s", [P, 2, DC, D], F32R) as wk_s, nc.sbuf_tensor("wv_s", [P, 2, DC, D], F32R) as wv_s:
            prologue(nc, x, xwq, xwk, xwv, q_dram, wk_s, wv_s, ident)
            cross_attention(nc, yT, q_dram, o_dram, wk_s, wv_s, ident)
        x_sb = sb("x_sb", [P, TT, D])
        att = sb("att", [P, 2, DC, TOK], F32R)
        xnT = sb("xnT", [P, 2, DC, TOK], F32R)
        with ExitStack() as inner:
            qT = inner.enter_context(nc.sbuf_tensor("qT", [P, NBLK, TOK], F32))
            kT = inner.enter_context(nc.sbuf_tensor("kT", [P, NBLK, TOK], F32))
            v_sb = inner.enter_context(nc.sbuf_tensor("v_self", [P, TT, D], F32))
            w_in = [inner.enter_context(nc.semaphore(f"aw_in{n}")) for n in range(3)]
            with nc.sbuf_tensor("aw_raw", [P, 3, DC, D], F32) as w_raw:
                cross_output(nc, x, o_dram, xwp, xbp, att, x_sb, xnT, w_raw, w_in, (awq, awk, awv), ident)
                qkv(nc, xnT, w_raw, w_in, abq, abk, abv, qT, kT, v_sb)
            wo_s = inner.enter_context(nc.sbuf_tensor("wo_s", [P, 2, DC, D], F32R))
            self_attention(nc, qT, kT, v_sb, alibi, awo, att, wo_s, ident)
            with nc.sbuf_tensor("so_rows", [P, TT * D], F32) as rows, nc.sbuf_tensor("bo_sb", [P, D], F32) as bo_sb, \
                    nc.semaphore("bo_in") as bo_in:
                def load(sp):
                    sp.dma_start(bo_sb[:], abo.rearrange("(a d) -> a d", a=1).broadcast_to((P, D))).then_inc(bo_in, 16)

                def bias(pool, biased):
                    pool.wait_ge(bo_in, 16)
                    for t in range(TT):
                        pool.tensor_tensor(x_sb[:, t, :], x_sb[:, t, :], bo_sb[:], ALU.add).then_inc(biased, 1)

                project_and_norm(nc, "so", att, wo_s, x_sb, xnT, rows[:], ident, load=load, bias=bias)
        feed_forward(nc, x_sb, xnT, w_ffn, out)


def kernel(x, ctx_1024, L0_xattn_Wq, L0_xattn_Wk, L0_xattn_Wv, L0_xattn_Wp, L0_xattn_bp, L0_attn_Wq, L0_attn_bq,
           L0_attn_Wk, L0_attn_bk, L0_attn_Wv, L0_attn_bv, L0_attn_Wo, L0_attn_bo, L0_ffn_W_fc, L0_ffn_W_proj):
    import concourse.bacc as bacc
    from concourse.bass_utils import run_bass_kernel_spmd

    y = np.zeros((B, D, MP), np.float32)
    y[:, :, :M] = np.asarray(ctx_1024).transpose(0, 2, 1)
    fc = np.asarray(L0_ffn_W_fc).reshape(FF // P, P, DC, P).transpose(0, 3, 2, 1).reshape(FF // P, P, D)
    proj = np.asarray(L0_ffn_W_proj).T.reshape(FF // P, P, D)
    slopes = np.power(np.float32(2.0), np.linspace(-4.0, -0.3, H, dtype=np.float32))
    bias = -(slopes[:, None] * np.arange(N, dtype=np.float32)[None, :])
    bias = bias.reshape(4, 4, N).transpose(1, 0, 2).reshape(1, H * N)

    def turn(w):
        return np.ascontiguousarray(np.asarray(w).T)

    def columns(b):
        return np.ascontiguousarray(np.asarray(b).reshape(NBLK, P).T)

    arrays = {
        "x": np.asarray(x).reshape(TOK, D), "yT": y.reshape(B, DC, P, MP),
        "xwq": L0_xattn_Wq, "xwk": L0_xattn_Wk, "xwv": L0_xattn_Wv, "xwp": L0_xattn_Wp, "xbp": L0_xattn_bp,
        "awq": turn(L0_attn_Wq), "abq": columns(L0_attn_bq), "awk": turn(L0_attn_Wk), "abk": columns(L0_attn_bk),
        "awv": turn(L0_attn_Wv), "abv": L0_attn_bv, "awo": turn(L0_attn_Wo), "abo": L0_attn_bo,
        "w_ffn": np.stack([fc, proj], axis=2).reshape(FF // P, P, 2 * D), "alibi": bias,
    }
    nc = bacc.Bacc("TRN2", target_bir_lowering=False, num_devices=1)
    given = {}
    for name, a in arrays.items():
        arrays[name] = a = np.ascontiguousarray(a)
        given[name] = nc.dram_tensor(name, a.shape, mybir.dt.from_np(a.dtype), kind="ExternalInput").ap()
    out = nc.dram_tensor("out", (TOK, D), F32, kind="ExternalOutput").ap()
    q_dram = nc.dram_tensor("q_scratch", (P, NBLK * 2, TOK), F32, kind="Internal").ap()
    o_dram = nc.dram_tensor("o_scratch", (P, NBLK, TOK), F32, kind="Internal").ap()
    perceiver(nc, **given, out=out, q_dram=q_dram, o_dram=o_dram)
    result = run_bass_kernel_spmd(nc, [arrays], core_ids=[0])
    return result.results[0]["out"].reshape(B, N, D)
```

```python
import numpy as np
import concourse.bass as bass
from concourse import mybir
from contextlib import ExitStack

F32 = mybir.dt.float32
F32R = mybir.dt.float32r
ALU = mybir.AluOpType
ACT = mybir.ActivationFunctionType
AX = mybir.AxisListType

B, N, M, D = 16, 64, 1601, 512
H, DH = 16, 32
FF = 2048
P = 128
DC = D // P
MP = M + M % 2
TOK = B * N
TT = TOK // P
JT = -(-M // P)
JL = M - (JT - 1) * P
KW = 402
KC = -(-MP // KW)
KWL = MP - (KC - 1) * KW
NBLK = H * DH // P
PAIRS = H // 2
TG = -(-JT // 2)
RING = 3
PT_RING = 4
P_RING = 4
SCALE = float(DH) ** -0.5
EPS = 1e-5

STEADY = [("V",),
          ("S", 0), ("K", 1, 0), ("E", 0), ("K", 1, 1), ("N", 0), ("K", 1, 2),
          ("S", 1), ("K", 1, 3), ("E", 1), ("K", 2, 0), ("N", 1), ("K", 2, 1),
          ("S", 2), ("K", 2, 2), ("E", 2), ("T", 0, 0, "ddd"), ("N", 2), ("K", 2, 3),
          ("S", 3), ("T", 0, 3, "aaa"), ("E", 3), ("T", 0, 6, "d"), ("K", 3, 0), ("F", 0), ("O", 0), ("N", 3),
          ("S", 4), ("K", 3, 1), ("E", 4), ("K", 3, 2), ("N", 4), ("K", 3, 3), ("H", 0), ("H", 1), ("H", 2), ("H", 3),
          ("S", 5), ("T", 1, 0, "aaa"), ("E", 5), ("T", 1, 3, "ddd"), ("N", 5), ("L", 0), ("L", 3), ("T", 1, 6, "a"),
          ("S", 6), ("F", 1), ("O", 1), ("T", 2, 0, "aaa"), ("E", 6), ("T", 2, 3, "dd"), ("L", 1), ("N", 6), ("L", 2),
          ("T", 2, 5, "aa"),
          ("S", 7), ("F", 2), ("O", 2), ("K", 4, 0), ("E", 7), ("K", 4, 1), ("N", 7), ("K", 4, 2),
          ("T", 3, 0, "adadada"), ("K", 4, 3), ("F", 3), ("O", 3)]
LAST = [s for s in STEADY if s[0] not in "HL" and s[:2] != ("K", 4)]
POOL_LOW = DC - 1


def ring_units(order):
    units, act, dve = [], 0, 0
    for step in order:
        if step[0] == "V":
            new = [("V", t, "ad"[t % 2]) for t in range(JT)]
        elif step[0] == "K":
            new = [("K", step[1:], "d")]
        elif step[0] == "T":
            new = [("T", (step[1], step[2] + n), by) for n, by in enumerate(step[3])]
        else:
            continue
        for kind, index, by in new:
            act += kind == "K" or by == "a"
            dve += by == "d"
            units.append((kind, index, by, act, dve))
    return units


UNITS = ring_units(STEADY)
LAST_UNITS = ring_units(LAST)
NU = len(UNITS)
ACT_N, DVE_N = UNITS[-1][3], UNITS[-1][4]
FIRST = KC
assert NU % RING == 0
PV_CREDIT, EXP_CREDIT, N_CREDIT, O_CREDIT, S_CREDIT, ST_CREDIT = 8, 2, 2, 1, 1, 16
PV_N = NBLK * TG


def kchunk(c):
    return c * KW, KW if c < KC - 1 else KWL


def jtile(t):
    return P if t < JT - 1 else JL


def prologue(nc, x, wq, wk, wv, q_dram, wk_s, wv_s, ident):
    ctx = ExitStack()
    with ctx:
        sb = lambda n, s, d=F32: ctx.enter_context(nc.sbuf_tensor(n, s, d))
        sem = lambda n: ctx.enter_context(nc.semaphore(n))
        xs = sb("p_x", [P, TT, D])
        xn = sb("p_xn", [P, TT, D])
        xnT = sb("p_xnT", [P, DC, TOK])
        wq_sb = sb("p_wq", [P, DC, D])
        wraw = sb("p_wraw", [P, 2, DC, D])
        qs = sb("p_q", [P, NBLK, 2, TOK], F32R)
        stats = sb("p_stats", [P, TT, 6])
        mv = sb("p_mv", [P, TT, 2])
        ve = sb("p_ve", [P, 5, TT])
        ps = [ctx.enter_context(nc.psum_tensor(f"p_ps{i}", [P, 512], F32)) for i in range(4)]
        x_in, wq_in, w_in = sem("p_x_in"), sem("p_wq_in"), sem("p_w_in")
        ident_ok, ln_step, root_ok, xn_ok = sem("p_ident"), sem("p_ln_step"), sem("p_root"), sem("p_xn")
        xt_ps, xt_ok, q_ps, q_hi, q_lo, q_out = (sem("p_xt_ps"), sem("p_xt_ok"), sem("p_q_ps"),
                                                 sem("p_q_hi"), sem("p_q_lo"), sem("p_q_out"))
        w_hi, w_lo = sem("p_w_hi"), sem("p_w_lo")
        block = ctx.enter_context(nc.Block())

        @block.sync
        def _(sp):
            sp.dma_start(xs[:], x.rearrange("(t p) d -> p t d", p=P)).then_inc(x_in, 16)
            sp.dma_start(wq_sb[:], wq.rearrange("(c p) e -> p c e", p=P)).then_inc(wq_in, 16)
            sp.dma_start(wraw[:, 0], wk.rearrange("(c p) e -> p c e", p=P)).then_inc(w_in, 16)
            sp.dma_start(wraw[:, 1], wv.rearrange("(c p) e -> p c e", p=P)).then_inc(w_in, 16)
            sp.wait_ge(q_lo, NBLK * 2)
            sp.dma_start(q_dram, qs[:].bitcast(F32).rearrange("p i s t -> p (i s) t")).then_inc(q_out, 16)
            sp.wait_ge(q_out, 16)

        @block.gpsimd
        def _(pool):
            pool.memset(ident[:], 0.0).then_inc(ident_ok, 1)
            pool.wait_ge(ident_ok, 1)
            pool.affine_select(out=ident[:], in_=ident[:], compare_op=ALU.not_equal, fill=1.0, base=0,
                               pattern=[[-1, P]], channel_multiplier=1).then_inc(ident_ok, 1)

        @block.vector
        def _(dve):
            step = 0
            dve.wait_ge(x_in, 16)
            for t in range(TT):
                dve.bn_stats(stats[:, t, :], xs[:, t, :]).then_inc(ln_step, 1)
            for t in range(TT):
                dve.wait_ge(ln_step, t + 1)
                dve.bn_aggr(mv[:, t, :], stats[:, t, :]).then_inc(ln_step, 1)
            step = 2 * TT
            dve.wait_ge(ln_step, step)
            dve.tensor_scalar_add(ve[:, 0, :], mv[:, :, 1], EPS).then_inc(ln_step, 1)
            dve.wait_ge(root_ok, 1)
            dve.reciprocal(ve[:, 2, :], ve[:, 1, :]).then_inc(ln_step, 1)
            dve.wait_ge(ln_step, step + 2)
            dve.tensor_tensor(ve[:, 3, :], ve[:, 2, :], ve[:, 2, :], ALU.mult).then_inc(ln_step, 1)
            dve.wait_ge(ln_step, step + 3)
            dve.tensor_tensor(ve[:, 4, :], ve[:, 3, :], ve[:, 0, :], ALU.mult).then_inc(ln_step, 1)
            dve.wait_ge(ln_step, step + 4)
            dve.tensor_scalar(ve[:, 3, :], ve[:, 4, :], -0.5, 1.5, ALU.mult, ALU.add).then_inc(ln_step, 1)
            dve.wait_ge(ln_step, step + 5)
            dve.tensor_tensor(ve[:, 4, :], ve[:, 2, :], ve[:, 3, :], ALU.mult).then_inc(ln_step, 1)
            dve.wait_ge(ln_step, step + 6)
            for t in range(TT):
                dve.tensor_scalar(xn[:, t, :], xs[:, t, :], mv[:, t, 0:1], ve[:, 4, t:t + 1],
                                  ALU.subtract, ALU.mult).then_inc(xn_ok, 1)
            for w, dst in enumerate((wk_s, wv_s)):
                dve.wait_ge(w_hi, w + 1)
                dve.tensor_tensor(dst[:, 1], wraw[:, w], dst[:, 0].bitcast(F32), ALU.subtract).then_inc(w_lo, 1)
            for n in range(NBLK * 2):
                i, half = n // 2, n % 2
                dve.wait_ge(q_hi, n + 1)
                dve.tensor_tensor(qs[:, i, 1, half * 512:half * 512 + 512], ps[n % 4][:],
                                  qs[:, i, 0, half * 512:half * 512 + 512].bitcast(F32),
                                  ALU.subtract).then_inc(q_lo, 1)

        @block.scalar
        def _(act):
            act.wait_ge(ln_step, 2 * TT + 1)
            act.activation(ve[:, 1, :], ve[:, 0, :], ACT.Sqrt).then_inc(root_ok, 1)
            for w, dst in enumerate((wk_s, wv_s)):
                act.wait_ge(w_in, 32)
                act.activation(dst[:, 0], wraw[:, w], ACT.Copy).then_inc(w_hi, 1)
            for t in range(TT):
                act.wait_ge(xt_ps, t + 1)
                act.activation(xnT[:, :, t * P:(t + 1) * P],
                               ps[t % 4][:].rearrange("p (c q) -> p c q", c=DC), ACT.Copy).then_inc(xt_ok, 1)
            for n in range(NBLK * 2):
                i, half = n // 2, n % 2
                act.wait_ge(q_ps, n + 1)
                act.activation(qs[:, i, 0, half * 512:half * 512 + 512], ps[n % 4][:], ACT.Copy).then_inc(q_hi, 1)

        @block.tensor
        def _(pe):
            pe.wait_ge(ident_ok, 2)
            for t in range(TT):
                pe.wait_ge(xn_ok, t + 1)
                if t >= 4:
                    pe.wait_ge(xt_ok, t - 3)
                for c in range(DC):
                    mm = pe.transpose(ps[t % 4][:, c * P:(c + 1) * P], xn[:, t, c * P:(c + 1) * P], ident[:])
                mm.then_inc(xt_ps, 1)
            pe.wait_ge(wq_in, 16)
            pe.wait_ge(xt_ok, TT)
            for n in range(NBLK * 2):
                i, half = n // 2, n % 2
                if n >= 4:
                    pe.wait_ge(q_lo, n - 3)
                for c in range(DC):
                    mm = pe.matmul(ps[n % 4][:], wq_sb[:, c, i * P:(i + 1) * P],
                                   xnT[:, c, half * 512:half * 512 + 512], start=(c == 0), stop=(c == DC - 1))
                mm.then_inc(q_ps, 1)


def cross_attention(nc, yT, q_dram, o_dram, wk_s, wv_s, ident):
    ctx = ExitStack()
    with ctx:
        sb = lambda n, s, d=F32: ctx.enter_context(nc.sbuf_tensor(n, s, d))
        sem = lambda n: ctx.enter_context(nc.semaphore(n))
        y_raw = sb("y_raw", [P, DC, MP])
        y_hi = sb("y_hi", [P, DC, MP], F32R)
        y_lo = sb("y_lo", [P, DC, MP], F32R)
        k_s = sb("k_s", [P, 2, 2, MP], F32R)
        v_sb = sb("v_sb", [P, JT, D])
        q_s = sb("q_s", [P, 2, NBLK * 2, P], F32R)
        prob = sb("prob", [P, P_RING, MP])
        pT = sb("pT", [P, PT_RING, 512])
        o_sb = sb("o_sb", [P, NBLK, N])
        peak = sb("peak", [P, 2, 4])
        total = sb("total", [P, 2, 4])
        s_ps = ctx.enter_context(nc.psum_tensor("s_ps", [P, KC * 512], F32))
        ring = [ctx.enter_context(nc.psum_tensor(f"ring{i}", [P, 512], F32)) for i in range(RING)]
        o_ps = ctx.enter_context(nc.psum_tensor("o_ps", [P, N], F32))
        s_v = s_ps[:].rearrange("p (c k) -> p c k", c=KC)

        y_in = [sem(f"y_in{c}") for c in range(DC)]
        y_hi_ok, y_lo_ok, q_zero, q_in = sem("y_hi_ok"), sem("y_lo_ok"), sem("q_zero"), sem("q_in")
        y_pool_ok = sem("y_pool_ok")
        sum_ok = sem("sum_ok")
        full = sem("ring_full")
        act_out, dve_out = sem("ring_act_out"), sem("ring_dve_out")
        s_full = sem("scores_full")
        peak_step = sem("peak_step")
        bias_ok, exp_ok, norm_ok = sem("bias_ok"), sem("exp_ok"), sem("norm_ok")
        pool_passed = sem("pool_passed")
        pv_ok = sem("pv_ok")
        o_out, o_stored = sem("o_out"), sem("o_stored")
        block = ctx.enter_context(nc.Block())

        def emptied(eng, batch, units, u):
            _, _, by, a, d = units[u] if u >= 0 else UNITS[u]
            if u < 0:
                a, d = a - ACT_N, d - DVE_N
            if by == "a":
                eng.wait_ge(act_out, FIRST + batch * ACT_N + a)
            else:
                eng.wait_ge(dve_out, FIRST + batch * DVE_N + d)

        def bank(u):
            return ring[(FIRST + u) % RING]

        @block.sync
        def _(sp):
            sp.sem_inc(o_stored, ST_CREDIT)

            def load(batch, c):
                sp.dma_start(y_raw[:, c, :],
                             yT[bass.ds(batch, 1), c].rearrange("a p m -> (a p) m")).then_inc(y_in[c], 16)

            def load_q(batch):
                for k in range(4):
                    for second in range(2):
                        g = 2 * second + k % 2
                        sp.dma_start(
                            q_s[k * DH:(k + 1) * DH, second, :, (k % 2) * N:(k % 2 + 1) * N].bitcast(F32),
                            q_dram[g * DH:(g + 1) * DH, :, bass.ds(batch * N, N)]).then_inc(q_in, 16)

            for c in range(DC):
                load(0, c)
            sp.wait_ge(q_zero, 1)
            load_q(0)

            def store(batch):
                sp.wait_ge(o_out, O_CREDIT + NBLK * (batch + 1))
                sp.dma_start(o_dram[:, :, bass.ds(batch * N, N)], o_sb[:]).then_inc(o_stored, 16)

            with sp.Fori(0, B - 1) as b:
                for c in range(DC):
                    if c == POOL_LOW:
                        sp.wait_ge(y_pool_ok, b + 1)
                    else:
                        sp.wait_ge(y_lo_ok, POOL_LOW * b + c + 1)
                    load(b + 1, c)
                sp.wait_ge(s_full, S_CREDIT + 2 * PAIRS * (b + 1))
                load_q(b + 1)
                store(b)
            store(B - 1)
            sp.wait_ge(o_stored, ST_CREDIT + 16 * B)

        @block.gpsimd
        def _(pool):
            pool.sem_inc(norm_ok, N_CREDIT)

            def settle():
                pool.sem_inc(pool_passed, 1)

            def low(pool):
                pool.tensor_tensor(y_lo[:, POOL_LOW, :], y_raw[:, POOL_LOW, :], y_hi[:, POOL_LOW, :].bitcast(F32),
                                   ALU.subtract).then_inc(y_pool_ok, 1)

            def high(batch, c):
                pool.wait_ge(y_in[c], 16 * (batch + 1))
                settle()
                pool.tensor_scalar(y_hi[:, c, :], y_raw[:, c, :], 1.0, 1.0, ALU.mult,
                                   ALU.mult).then_inc(y_hi_ok, 1)

            def run(batch, order, units):
                last = max(n for n, x in enumerate(units) if x[0] == "K" and x[1][0] == NBLK - 1)
                for step in order:
                    if step[0] == "N":
                        p = step[1]
                        pool.wait_ge(sum_ok, PAIRS * batch + p + 1)
                        settle()
                        pool.tensor_scalar(prob[:, p % P_RING, 0:M], prob[:, p % P_RING, 0:M],
                                           total[:, p % 2, 3:4], 1.0, ALU.mult, ALU.mult).then_inc(norm_ok, 1)
                    elif step[0] == "H":
                        if step[1] == 0:
                            pool.wait_ge(full, FIRST + NU * batch + last + 1)
                        high(batch + 1, step[1])
                    elif step[0] == "L" and step[1] == POOL_LOW:
                        pool.wait_ge(y_hi_ok, DC * (batch + 2))
                        low(pool)

            pool.memset(q_s[:].bitcast(F32), 0.0).then_inc(q_zero, 1)
            pool.wait_ge(y_hi_ok, DC)
            low(pool)
            with pool.Fori(0, B - 1) as b:
                run(b, STEADY, UNITS)
            run(B - 1, LAST, LAST_UNITS)

        @block.scalar
        def _(act):
            act.sem_inc(exp_ok, EXP_CREDIT)
            act.sem_inc(o_out, O_CREDIT)

            def empty_k(unit_no, src, i, c):
                at, w = kchunk(c)
                act.wait_ge(full, unit_no + 1)
                act.activation(k_s[0:64, i % 2, 0, at:at + w], src[0:64, 0:w], ACT.Copy)
                act.activation(k_s[64:P, i % 2, 1, at:at + w], src[64:P, 0:w], ACT.Copy).then_inc(act_out, 1)

            def run(batch, order, units):
                u = 0
                for step in order:
                    if step[0] == "V":
                        for t in range(JT):
                            if units[u][2] == "a":
                                if t < 2:
                                    act.wait_ge(pv_ok, PV_CREDIT + PV_N * batch)
                                act.wait_ge(full, FIRST + NU * batch + u + 1)
                                m = jtile(t)
                                act.activation(v_sb[0:m, t, :], bank(u)[0:m, :], ACT.Copy).then_inc(act_out, 1)
                            u += 1
                    elif step[0] == "K":
                        _, i, c = step
                        if c == 0:
                            act.wait_ge(s_full, S_CREDIT + 2 * PAIRS * batch + 4 * (i - 1))
                        empty_k(FIRST + NU * batch + u, bank(u), i, c)
                        u += 1
                    elif step[0] == "E":
                        p = step[1]
                        pair = PAIRS * batch + p
                        act.wait_ge(pv_ok, PV_CREDIT + PV_N * batch + TG * (p // 2 - 1))
                        act.wait_ge(bias_ok, pair + 1)
                        dst = prob[:, p % P_RING, :]
                        act.activation(dst[:, 0:3 * KW].rearrange("p (c k) -> p c k", c=3),
                                       s_v[:, 0:3, 0:KW], ACT.Exp, bias=peak[:, p % 2, 2:3], scale=SCALE,
                                       accum_out=total[:, p % 2, 0:1]).then_inc(exp_ok, 1)
                        act.activation(dst[:, 3 * KW:M], s_v[:, 3, 0:M - 3 * KW], ACT.Exp,
                                       bias=peak[:, p % 2, 2:3], scale=SCALE,
                                       accum_out=total[:, p % 2, 1:2]).then_inc(exp_ok, 1)
                    elif step[0] == "T":
                        _, i, g0, by = step
                        for g in range(g0, g0 + len(by)):
                            if units[u][2] == "a":
                                act.wait_ge(pv_ok, PV_CREDIT + PV_N * batch + TG * i + g - PT_RING + 1)
                                act.wait_ge(full, FIRST + NU * batch + u + 1)
                                m, w = (P, 512) if g < TG - 1 else (JL, 256)
                                act.activation(pT[0:m, (TG * i + g) % PT_RING, 0:w], bank(u)[0:m, 0:w],
                                               ACT.Copy).then_inc(act_out, 1)
                            u += 1
                    elif step[0] == "O":
                        i = step[1]
                        act.wait_ge(pv_ok, PV_CREDIT + PV_N * batch + TG * (i + 1))
                        if i == 0:
                            act.wait_ge(o_stored, ST_CREDIT + 16 * batch)
                        act.activation(o_sb[:, i, :], o_ps[:], ACT.Copy).then_inc(o_out, 1)

            for c in range(DC):
                act.wait_ge(y_in[c], 16)
                act.activation(y_hi[:, c, :], y_raw[:, c, :], ACT.Copy).then_inc(y_hi_ok, 1)
            for c in range(KC):
                empty_k(c, ring[c % RING], 0, c)
            with act.Fori(0, B - 1) as b:
                run(b, STEADY, UNITS)
            run(B - 1, LAST, LAST_UNITS)

        @block.vector
        def _(dve):
            def split(batch, c):
                dve.wait_ge(y_hi_ok, DC * batch + c + 1)
                dve.tensor_tensor(y_lo[:, c, :], y_raw[:, c, :], y_hi[:, c, :].bitcast(F32),
                                  ALU.subtract).then_inc(y_lo_ok, 1)

            def empty_k(src, act_count, i, c):
                at, w = kchunk(c)
                dve.wait_ge(act_out, act_count)
                k0, k1 = k_s[:, i % 2, 0, at:at + w], k_s[:, i % 2, 1, at:at + w]
                dve.tensor_tensor(k0[64:P], src[0:64, 0:w], k0[0:64].bitcast(F32), ALU.subtract)
                dve.tensor_tensor(k1[0:64], src[64:P, 0:w], k1[64:P].bitcast(F32),
                                  ALU.subtract).then_inc(dve_out, 1)

            def run(batch, order, units):
                u = 0
                for step in order:
                    if step[0] == "V":
                        for t in range(JT):
                            if units[u][2] == "d":
                                if t < 2:
                                    dve.wait_ge(pv_ok, PV_CREDIT + PV_N * batch)
                                dve.wait_ge(full, FIRST + NU * batch + u + 1)
                                m = jtile(t)
                                dve.tensor_copy(v_sb[0:m, t, :], bank(u)[0:m, :]).then_inc(dve_out, 1)
                            u += 1
                    elif step[0] == "K":
                        _, i, c = step
                        empty_k(bank(u), FIRST + batch * ACT_N + units[u][3], i, c)
                        u += 1
                    elif step[0] == "S":
                        p = step[1]
                        done = S_CREDIT + 2 * (PAIRS * batch + p)
                        small = 3 * (PAIRS * batch + p)
                        dve.wait_ge(s_full, done + 1)
                        dve.tensor_reduce(peak[:, p % 2, 0:1], s_v[:, 0:3, 0:KW], AX.XY, ALU.max).then_inc(peak_step, 1)
                        dve.wait_ge(s_full, done + 2)
                        dve.tensor_reduce(peak[:, p % 2, 1:2], s_v[:, 3, 0:M - 3 * KW], AX.X,
                                          ALU.max).then_inc(peak_step, 1)
                        dve.wait_ge(peak_step, small + 2)
                        dve.tensor_scalar(peak[:, p % 2, 2:3], peak[:, p % 2, 0:1], peak[:, p % 2, 1:2],
                                          -SCALE, ALU.max, ALU.mult).then_inc(bias_ok, 1)
                    elif step[0] == "N":
                        p = step[1]
                        small = 3 * (PAIRS * batch + p)
                        dve.wait_ge(exp_ok, EXP_CREDIT + 2 * (PAIRS * batch + p) + 2)
                        dve.tensor_tensor(total[:, p % 2, 2:3], total[:, p % 2, 0:1], total[:, p % 2, 1:2],
                                          ALU.add).then_inc(peak_step, 1)
                        dve.wait_ge(norm_ok, N_CREDIT + PAIRS * batch + p - 1)
                        dve.wait_ge(peak_step, small + 3)
                        dve.reciprocal(total[:, p % 2, 3:4], total[:, p % 2, 2:3]).then_inc(sum_ok, 1)
                    elif step[0] == "L" and step[1] != POOL_LOW:
                        split(batch + 1, step[1])
                    elif step[0] == "T":
                        _, i, g0, by = step
                        for g in range(g0, g0 + len(by)):
                            if units[u][2] == "d":
                                dve.wait_ge(pv_ok, PV_CREDIT + PV_N * batch + TG * i + g - PT_RING + 1)
                                dve.wait_ge(full, FIRST + NU * batch + u + 1)
                                m, w = (P, 512) if g < TG - 1 else (JL, 256)
                                dve.tensor_copy(pT[0:m, (TG * i + g) % PT_RING, 0:w],
                                                bank(u)[0:m, 0:w]).then_inc(dve_out, 1)
                            u += 1

            for c in range(POOL_LOW):
                split(0, c)
            for c in range(KC):
                empty_k(ring[c % RING], c + 1, 0, c)
            with dve.Fori(0, B - 1) as b:
                run(b, STEADY, UNITS)
            run(B - 1, LAST, LAST_UNITS)

        @block.tensor
        def _(pe):
            def three(out, left, right, rows, cols):
                for c in range(DC):
                    for n, (a, b) in enumerate(((0, 0), (1, 0), (0, 1))):
                        mm = pe.matmul(out, left(a, c), right(b, c),
                                       start=(c == 0 and n == 0), stop=(c == DC - 1 and n == 2))
                return mm

            y_part = (y_hi, y_lo)

            def project_k(out, i, c):
                at, w = kchunk(c)
                return three(out[:, 0:w], lambda a, d: wk_s[:, a, d, i * P:(i + 1) * P],
                             lambda a, d: y_part[a][:, d, at:at + w], P, w)

            def project_v(out, t):
                m = jtile(t)
                return three(out[0:m, :], lambda a, d: y_part[a][:, d, t * P:t * P + m],
                             lambda a, d: wv_s[:, a, d, :], m, D)

            def scores(batch, p):
                pair = PAIRS * batch + p
                for c in range(KC):
                    at, w = kchunk(c)
                    if c == 0:
                        pe.wait_ge(exp_ok, EXP_CREDIT + 2 * pair - 1)
                    if c == KC - 1:
                        pe.wait_ge(exp_ok, EXP_CREDIT + 2 * pair)
                    for part in range(2):
                        mm = pe.matmul(s_v[:, c, 0:w], q_s[:, p % 2, p // 2 * 2 + part, :],
                                       k_s[:, (p // 2) % 2, p % 2, at:at + w], start=(part == 0), stop=(part == 1))
                    if c >= KC - 2:
                        mm.then_inc(s_full, 1)

            def run(batch, order, units):
                u = 0
                number = {(x[0], x[1]): n for n, x in enumerate(units)}
                for step in order:
                    if step[0] == "V":
                        for t in range(JT):
                            emptied(pe, batch, units, u - RING)
                            project_v(bank(u), t).then_inc(full, 1)
                            u += 1
                    elif step[0] == "K":
                        _, i, c = step
                        if i == NBLK and c == 0:
                            pe.wait_ge(y_lo_ok, POOL_LOW * (batch + 2))
                            pe.wait_ge(y_pool_ok, batch + 2)
                        emptied(pe, batch, units, u - RING)
                        project_k(bank(u), i % NBLK, c).then_inc(full, 1)
                        u += 1
                    elif step[0] == "S":
                        p = step[1]
                        if p == 0:
                            pe.wait_ge(q_in, 128 * (batch + 1))
                            emptied(pe, batch, units, block0_keys - NU)
                        elif p % 2 == 0:
                            emptied(pe, batch, units, number["K", (p // 2, KC - 1)])
                        scores(batch, p)
                    elif step[0] == "T":
                        _, i, g0, by = step
                        if g0 == 0:
                            pe.wait_ge(norm_ok, N_CREDIT + PAIRS * batch + 2 * i + 2)
                        for g in range(g0, g0 + len(by)):
                            emptied(pe, batch, units, u - RING)
                            for k, t in enumerate(range(2 * g, min(2 * g + 2, JT))):
                                m = jtile(t)
                                for second in range(2):
                                    at = k * 256 + second * P
                                    mm = pe.transpose(bank(u)[0:m, at:at + P],
                                                      prob[:, (2 * i + second) % P_RING, t * P:t * P + m], ident[:])
                            mm.then_inc(full, 1)
                            u += 1
                            if g >= 2:
                                weigh(batch, units, number, i, g - 2)
                    elif step[0] == "F":
                        weigh(batch, units, number, step[1], TG - 2)
                        weigh(batch, units, number, step[1], TG - 1)

            def weigh(batch, units, number, i, g):
                if g == 0:
                    pe.wait_ge(o_out, O_CREDIT + NBLK * batch + i)
                emptied(pe, batch, units, number["T", (i, g)])
                for k, t in enumerate(range(2 * g, min(2 * g + 2, JT))):
                    m = jtile(t)
                    for head in range(4):
                        at = k * 256 + head * N
                        mm = pe.matmul(o_ps[head * DH:(head + 1) * DH, :],
                                       v_sb[0:m, t, (4 * i + head) * DH:(4 * i + head + 1) * DH],
                                       pT[0:m, (TG * i + g) % PT_RING, at:at + N],
                                       start=(t == 0), stop=(t == JT - 1))
                mm.then_inc(pv_ok, 1)

            block0_keys = max(n for n, x in enumerate(UNITS) if x[0] == "K")
            pe.sem_inc(pv_ok, PV_CREDIT)
            pe.sem_inc(s_full, S_CREDIT)
            pe.wait_ge(y_lo_ok, POOL_LOW)
            pe.wait_ge(y_pool_ok, 1)
            for c in range(KC):
                if c >= RING:
                    pe.wait_ge(dve_out, c - RING + 1)
                project_k(ring[c % RING], 0, c).then_inc(full, 1)
            pe.wait_ge(dve_out, KC)
            with pe.Fori(0, B - 1) as b:
                run(b, STEADY, UNITS)
            run(B - 1, LAST, LAST_UNITS)


def three_passes(pe, out, left, right):
    for c in range(DC):
        for n, (a, b) in enumerate(((0, 0), (1, 0), (0, 1))):
            mm = pe.matmul(out, left(a, c), right(b, c),
                           start=(c == 0 and n == 0), stop=(c == DC - 1 and n == 2))
    return mm


def project_and_norm(nc, tag, left, w, x, xnT, rows, ident, load=None, split_hi=None, split_lo=None,
                     ready=None, bias=None):
    ctx = ExitStack()
    with ctx:
        sb = lambda n, s, d=F32: ctx.enter_context(nc.sbuf_tensor(f"{tag}_{n}", s, d))
        sem = lambda n: ctx.enter_context(nc.semaphore(f"{tag}_{n}"))
        stats, mv = sb("stats", [P, TT, 6]), sb("mv", [P, TT, 2])
        ve = sb("ve", [P, 5, TT])
        bank = [ctx.enter_context(nc.psum_tensor(f"{tag}_ps{i}", [P, 512], F32)) for i in range(8)]
        biased, added, step, var_ok, root_ok = sem("biased"), sem("added"), sem("step"), sem("var"), sem("root")
        xn_ok, full, turned, hi_ok, lo_ok = sem("xn_ok"), sem("full"), sem("turned"), sem("hi_ok"), sem("lo_ok")
        block = ctx.enter_context(nc.Block())
        xn = rows.rearrange("p (t d) -> p t d", t=TT)
        HALF = TT // 2

        @block.sync
        def _(sp):
            if load:
                load(sp)

        @block.gpsimd
        def _(pool):
            bias(pool, biased)

        @block.vector
        def _(dve):
            if split_lo:
                split_lo(dve)
            n = 0
            for half in range(2):
                tiles = range(half * HALF, (half + 1) * HALF)
                for t in tiles:
                    dve.wait_ge(biased, t + 1)
                    dve.wait_ge(full, t + 1)
                    dve.tensor_tensor(x[:, t, :], bank[t % 4][:], x[:, t, :], ALU.add).then_inc(added, 1)
                for t in tiles:
                    dve.wait_ge(added, t + 1)
                    dve.bn_stats(stats[:, t, :], x[:, t, :]).then_inc(step, 1)
                    n += 1
                first = n - HALF
                for k, t in enumerate(tiles):
                    dve.wait_ge(step, first + k + 1)
                    dve.bn_aggr(mv[:, t, :], stats[:, t, :]).then_inc(step, 1)
                    n += 1
                at = slice(half * HALF, (half + 1) * HALF)
                dve.wait_ge(step, n)
                dve.tensor_scalar_add(ve[:, 0, at], mv[:, at, 1], EPS).then_inc(var_ok, 1)
                dve.wait_ge(root_ok, half + 1)
                dve.reciprocal(ve[:, 2, at], ve[:, 1, at]).then_inc(step, 1)
                n += 1
                for out, a, b in ((3, 2, 2), (4, 3, 0)):
                    dve.wait_ge(step, n)
                    dve.tensor_tensor(ve[:, out, at], ve[:, a, at], ve[:, b, at], ALU.mult).then_inc(step, 1)
                    n += 1
                dve.wait_ge(step, n)
                dve.tensor_scalar(ve[:, 3, at], ve[:, 4, at], -0.5, 1.5, ALU.mult, ALU.add).then_inc(step, 1)
                n += 1
                dve.wait_ge(step, n)
                dve.tensor_tensor(ve[:, 4, at], ve[:, 2, at], ve[:, 3, at], ALU.mult).then_inc(step, 1)
                n += 1
                dve.wait_ge(step, n)
                for t in tiles:
                    dve.tensor_scalar(xn[:, t, :], x[:, t, :], mv[:, t, 0:1], ve[:, 4, t:t + 1],
                                      ALU.subtract, ALU.mult).then_inc(xn_ok, 1)
            for t in range(TT):
                dve.wait_ge(hi_ok, t + 1)
                dve.tensor_tensor(xnT[:, 1, :, t * P:(t + 1) * P],
                                  bank[4 + t % 4][:].rearrange("p (c q) -> p c q", c=DC),
                                  xnT[:, 0, :, t * P:(t + 1) * P].bitcast(F32), ALU.subtract).then_inc(lo_ok, 1)

        @block.scalar
        def _(act):
            if split_hi:
                split_hi(act)
            for half in range(2):
                at = slice(half * HALF, (half + 1) * HALF)
                act.wait_ge(var_ok, half + 1)
                act.activation(ve[:, 1, at], ve[:, 0, at], ACT.Sqrt).then_inc(root_ok, 1)
            for t in range(TT):
                act.wait_ge(turned, t + 1)
                act.activation(xnT[:, 0, :, t * P:(t + 1) * P],
                               bank[4 + t % 4][:].rearrange("p (c q) -> p c q", c=DC),
                               ACT.Copy).then_inc(hi_ok, 1)

        @block.tensor
        def _(pe):
            if ready:
                ready(pe)
            for t in range(TT):
                if t >= 4:
                    pe.wait_ge(added, t - 3)
                three_passes(pe, bank[t % 4][:], lambda a, c: left[:, a, c, t * P:(t + 1) * P],
                             lambda a, c: w[:, a, c, :]).then_inc(full, 1)
            for t in range(TT):
                pe.wait_ge(xn_ok, t + 1)
                if t >= 4:
                    pe.wait_ge(lo_ok, t - 3)
                for c in range(DC):
                    mm = pe.transpose(bank[4 + t % 4][:, c * P:(c + 1) * P], xn[:, t, c * P:(c + 1) * P], ident[:])
                mm.then_inc(turned, 1)


def cross_output(nc, x, o_dram, wp, bp, att, x_sb, xnT, w_raw, w_in, attn_w, ident):
    ctx = ExitStack()
    with ctx:
        rows = ctx.enter_context(nc.sbuf_tensor("co_rows", [P, TT * D], F32))
        wp_raw = ctx.enter_context(nc.sbuf_tensor("wp_raw", [P, DC, D], F32))
        wp_s = ctx.enter_context(nc.sbuf_tensor("wp_s", [P, 2, DC, D], F32R))
        bp_sb = ctx.enter_context(nc.sbuf_tensor("bp_sb", [P, D], F32))
        sem = lambda n: ctx.enter_context(nc.semaphore(n))
        wp_in, o_in, x_in, bp_in = sem("wp_in"), sem("o_in"), sem("x_in"), sem("bp_in")
        split_up, split_low = sem("co_split_hi"), sem("co_split_lo")
        o_raw = rows[:].rearrange("p (c t) -> p c t", c=DC)

        def load(sp):
            sp.dma_start(wp_raw[:], wp.rearrange("(c p) e -> p c e", p=P)).then_inc(wp_in, 16)
            sp.dma_start(o_raw, o_dram).then_inc(o_in, 16)
            sp.dma_start(x_sb[:], x.rearrange("(t p) d -> p t d", p=P)).then_inc(x_in, 16)
            sp.dma_start(bp_sb[:], bp.rearrange("(a d) -> a d", a=1).broadcast_to((P, D))).then_inc(bp_in, 16)
            for n, w in enumerate(attn_w):
                sp.dma_start(w_raw[:, n], w.rearrange("(c p) e -> p c e", p=P)).then_inc(w_in[n], 16)

        def split_hi(act):
            act.wait_ge(wp_in, 16)
            act.activation(wp_s[:, 0], wp_raw[:], ACT.Copy).then_inc(split_up, 1)
            act.wait_ge(o_in, 16)
            for c in range(DC):
                act.activation(att[:, 0, c, :], o_raw[:, c, :], ACT.Copy).then_inc(split_up, 1)

        def split_lo(dve):
            dve.wait_ge(split_up, 1)
            dve.tensor_tensor(wp_s[:, 1], wp_raw[:], wp_s[:, 0].bitcast(F32), ALU.subtract).then_inc(split_low, 1)
            for c in range(DC):
                dve.wait_ge(split_up, c + 2)
                dve.tensor_tensor(att[:, 1, c, :], o_raw[:, c, :], att[:, 0, c, :].bitcast(F32),
                                  ALU.subtract).then_inc(split_low, 1)

        def ready(pe):
            pe.wait_ge(split_low, 1 + DC)

        def bias(pool, biased):
            pool.wait_ge(x_in, 16)
            pool.wait_ge(bp_in, 16)
            for t in range(TT):
                pool.tensor_tensor(x_sb[:, t, :], x_sb[:, t, :], bp_sb[:], ALU.add).then_inc(biased, 1)

        project_and_norm(nc, "co", att, wp_s, x_sb, xnT, rows[:], ident, load, split_hi, split_lo, ready, bias)


def qkv(nc, xnT, w_raw, w_in, bq, bk, bv, qT, kT, v_sb):
    ctx = ExitStack()
    with ctx:
        sb = lambda n, s, d=F32: ctx.enter_context(nc.sbuf_tensor(n, s, d))
        sem = lambda n: ctx.enter_context(nc.semaphore(n))
        w_s = sb("aw_s", [P, 3, 2, DC, D], F32R)
        b_col = sb("b_col", [P, 2, NBLK])
        bv_sb = sb("bv_sb", [P, D])
        bank = [ctx.enter_context(nc.psum_tensor(f"qkv_ps{i}", [P, 512], F32)) for i in range(8)]
        b_in, bv_in, hi_ok, lo_ok = sem("b_in"), sem("bv_in"), sem("aw_hi"), sem("aw_lo")
        full, qk_out, v_out = sem("qkv_full"), sem("qk_out"), sem("v_out")
        block = ctx.enter_context(nc.Block())
        QK = 2 * NBLK * 2

        @block.sync
        def _(sp):
            for n, b in enumerate((bq, bk)):
                sp.dma_start(b_col[:, n, :], b).then_inc(b_in, 16)
            sp.dma_start(bv_sb[:], bv.rearrange("(a d) -> a d", a=1).broadcast_to((P, D))).then_inc(bv_in, 16)

        @block.scalar
        def _(act):
            for n in range(3):
                act.wait_ge(w_in[n], 16)
                act.activation(w_s[:, n, 0], w_raw[:, n], ACT.Copy).then_inc(hi_ok, 1)
            act.wait_ge(b_in, 32)
            for u in range(QK):
                n, i, half = u // 8, u // 2 % NBLK, u % 2
                act.wait_ge(full, u + 1)
                act.activation((qT, kT)[n][:, i, half * 512:(half + 1) * 512], bank[u % 8][:], ACT.Identity,
                               bias=b_col[:, n, i:i + 1]).then_inc(qk_out, 1)

        @block.vector
        def _(dve):
            for n in range(3):
                dve.wait_ge(hi_ok, n + 1)
                dve.tensor_tensor(w_s[:, n, 1], w_raw[:, n], w_s[:, n, 0].bitcast(F32),
                                  ALU.subtract).then_inc(lo_ok, 1)
            dve.wait_ge(bv_in, 16)
            for t in range(TT):
                dve.wait_ge(full, QK + t + 1)
                dve.tensor_tensor(v_sb[:, t, :], bank[(QK + t) % 8][:], bv_sb[:], ALU.add).then_inc(v_out, 1)

        @block.tensor
        def _(pe):
            for u in range(QK):
                n, i, half = u // 8, u // 2 % NBLK, u % 2
                pe.wait_ge(lo_ok, n + 1)
                if u >= 8:
                    pe.wait_ge(qk_out, u - 7)
                three_passes(pe, bank[u % 8][:], lambda a, c: w_s[:, n, a, c, i * P:(i + 1) * P],
                             lambda a, c: xnT[:, a, c, half * 512:(half + 1) * 512]).then_inc(full, 1)
            pe.wait_ge(lo_ok, 3)
            for t in range(TT):
                pe.wait_ge(qk_out, QK - 7 + t)
                three_passes(pe, bank[(QK + t) % 8][:], lambda a, c: xnT[:, a, c, t * P:(t + 1) * P],
                             lambda a, c: w_s[:, 2, a, c, :]).then_inc(full, 1)


def self_attention(nc, qT, kT, v_sb, alibi, wo, att, wo_s, ident):
    ctx = ExitStack()
    with ctx:
        sb = lambda n, s, d=F32: ctx.enter_context(nc.sbuf_tensor(n, s, d))
        sem = lambda n: ctx.enter_context(nc.semaphore(n))
        wo_raw = sb("wo_raw", [P, DC, D])
        al_sb = sb("al_sb", [P, 4, 4 * N])
        sc = sb("sc", [P, 2, H, N])
        ex = sb("ex", [P, 2, H, N])
        pr = sb("pr", [P, 2, H * N])
        pT = sb("sa_pT", [P, 2, H, N])
        small = sb("sa_small", [P, 2, 3, H])
        s_ps = ctx.enter_context(nc.psum_tensor("sa_s", [P, 4, 512], F32))
        t_ps = [ctx.enter_context(nc.psum_tensor(f"sa_t{i}", [P, 4, 2, N], F32)) for i in range(2)]
        o_ps = ctx.enter_context(nc.psum_tensor("sa_o", [P, 2, 512], F32))
        al_in, wo_in, wo_hi, wo_lo = sem("al_in"), sem("wo_in"), sem("wo_hi"), sem("wo_lo")
        s_full, s_out, max_ok, sub_ok, exp_ok = sem("sa_s_full"), sem("sa_s_out"), sem("sa_max"), sem("sa_sub"), sem("sa_exp")
        sum_ok, rec_ok, pr_ok = sem("sa_sum"), sem("sa_rec"), sem("sa_pr")
        turned, pT_act, pT_dve, pv_ok, o_hi, o_lo = (sem("sa_turned"), sem("sa_pT_act"), sem("sa_pT_dve"),
                                                     sem("sa_pv"), sem("sa_o_hi"), sem("sa_o_lo"))
        block = ctx.enter_context(nc.Block())

        @block.sync
        def _(sp):
            sp.dma_start(al_sb[:].rearrange("p g k -> p (g k)"), alibi.broadcast_to((P, H * N))).then_inc(al_in, 16)
            sp.dma_start(wo_raw[:], wo.rearrange("(c p) e -> p c e", p=P)).then_inc(wo_in, 16)

        @block.gpsimd
        def _(pool):
            for t in range(TT + 1):
                if t < TT:
                    k = t % 2
                    pool.wait_ge(max_ok, t + 1)
                    if t >= 2:
                        pool.wait_ge(pr_ok, t - 1)
                    pool.tensor_tensor(ex[:, k], sc[:, k], small[:, k, 0, :].unsqueeze(2).broadcast_to((P, H, N)),
                                       ALU.subtract).then_inc(sub_ok, 1)
                if t >= 1:
                    k = (t - 1) % 2
                    pool.wait_ge(rec_ok, t)
                    if t >= 3:
                        pool.wait_ge(turned, 2 * (t - 2))
                    pool.tensor_tensor(pr[:, k].rearrange("p (h n) -> p h n", h=H), ex[:, k],
                                       small[:, k, 2, :].unsqueeze(2).broadcast_to((P, H, N)),
                                       ALU.mult).then_inc(pr_ok, 1)

        def turned_blocks(t, n):
            for a in range(2):
                for b in range(2):
                    yield (pT[b * N:(b + 1) * N, t % 2, 8 * n + a:8 * n + 8:2, :],
                           t_ps[n][a * N:(a + 1) * N, :, b, :])

        @block.vector
        def _(dve):
            dve.wait_ge(al_in, 16)

            def soft(t):
                k = t % 2
                dve.wait_ge(s_full, t + 1)
                if t >= 2:
                    dve.wait_ge(sub_ok, t - 1)
                dve.scalar_tensor_tensor(sc[:, k].rearrange("p (g i) n -> p g (i n)", g=4), s_ps[:, :, 0:4 * N],
                                         SCALE, al_sb[:], ALU.mult, ALU.add).then_inc(s_out, 1)
                dve.wait_ge(s_out, t + 1)
                dve.tensor_reduce(small[:, k, 0, :], sc[:, k], AX.X, ALU.max).then_inc(max_ok, 1)

            def normal(t):
                k = t % 2
                dve.wait_ge(exp_ok, t + 1)
                if t >= 2:
                    dve.wait_ge(pr_ok, t - 1)
                dve.tensor_reduce(small[:, k, 1, :], ex[:, k], AX.X, ALU.add).then_inc(sum_ok, 1)
                dve.wait_ge(sum_ok, t + 1)
                dve.reciprocal(small[:, k, 2, :], small[:, k, 1, :]).then_inc(rec_ok, 1)

            def turn(t):
                for n in range(2):
                    dve.wait_ge(turned, 2 * t + n + 1)
                    dve.wait_ge(pT_act, 2 * t + n + 1)
                    if t >= 2:
                        dve.wait_ge(pv_ok, t - 1)
                    for dst, src in list(turned_blocks(t, n))[2:]:
                        ins = dve.tensor_copy(dst, src)
                    ins.then_inc(pT_dve, 1)

            def low(t):
                dve.wait_ge(o_hi, t + 1)
                dst = att[:, :, :, t * P:(t + 1) * P].rearrange("p s i (b q) -> p s b i q", b=2)
                src = o_ps[:, :, 0:4 * N].rearrange("p b (i q) -> p b i q", i=4)
                for b in range(2):
                    ins = dve.tensor_tensor(dst[:, 1, b], src[:, b], dst[:, 0, b].bitcast(F32), ALU.subtract)
                ins.then_inc(o_lo, 1)

            for t in range(TT + 2):
                if t < TT:
                    soft(t)
                if 1 <= t <= TT:
                    normal(t - 1)
                if t == 1:
                    dve.wait_ge(wo_hi, 1)
                    dve.tensor_tensor(wo_s[:, 1], wo_raw[:], wo_s[:, 0].bitcast(F32), ALU.subtract).then_inc(wo_lo, 1)
                if t >= 2:
                    turn(t - 2)
                    low(t - 2)
            dve.wait_ge(wo_lo, 1)

        @block.scalar
        def _(act):
            act.wait_ge(wo_in, 16)
            act.activation(wo_s[:, 0], wo_raw[:], ACT.Copy).then_inc(wo_hi, 1)
            for t in range(TT + 2):
                if t >= 2:
                    u = t - 2
                    for n in range(2):
                        act.wait_ge(turned, 2 * u + n + 1)
                        if u >= 2:
                            act.wait_ge(pv_ok, u - 1)
                        for dst, src in list(turned_blocks(u, n))[:2]:
                            ins = act.activation(dst, src, ACT.Copy)
                        ins.then_inc(pT_act, 1)
                    act.wait_ge(pv_ok, u + 1)
                    dst = att[:, 0, :, u * P:(u + 1) * P].rearrange("p i (b q) -> p b i q", b=2)
                    src = o_ps[:, :, 0:4 * N].rearrange("p b (i q) -> p b i q", i=4)
                    for b in range(2):
                        ins = act.activation(dst[:, b], src[:, b], ACT.Copy)
                    ins.then_inc(o_hi, 1)
                if t < TT:
                    act.wait_ge(sub_ok, t + 1)
                    act.activation(ex[:, t % 2], ex[:, t % 2], ACT.Exp).then_inc(exp_ok, 1)

        @block.tensor
        def _(pe):
            def scores(t):
                if t >= 1:
                    pe.wait_ge(s_out, t)
                for i in range(4):
                    for g in range(4):
                        rows = slice(g * DH, (g + 1) * DH)
                        for b in range(2):
                            at = slice(t * P + b * N, t * P + (b + 1) * N)
                            mm = pe.matmul(s_ps[b * N:(b + 1) * N, g, i * N:(i + 1) * N], qT[rows, i, at],
                                           kT[rows, i, at], start=True, stop=True)
                mm.then_inc(s_full, 1)

            def transposes(t):
                pe.wait_ge(pr_ok, t + 1)
                for n in range(2):
                    if t >= 1:
                        pe.wait_ge(pT_dve, 2 * t + n - 1)
                    for j in range(4):
                        mm = pe.transpose(t_ps[n][:, j].rearrange("p b q -> p (b q)"),
                                          pr[:, t % 2, (4 * n + j) * P:(4 * n + j + 1) * P], ident[:])
                    mm.then_inc(turned, 1)

            def weigh(t):
                pe.wait_ge(pT_dve, 2 * t + 2)
                if t >= 1:
                    pe.wait_ge(o_lo, t)
                for b in range(2):
                    rows = slice(b * N, (b + 1) * N)
                    for i in range(4):
                        for g in range(4):
                            mm = pe.matmul(o_ps[g * DH:(g + 1) * DH, b, i * N:(i + 1) * N],
                                           v_sb[rows, t, (4 * i + g) * DH:(4 * i + g + 1) * DH],
                                           pT[rows, t % 2, 4 * g + i, :], start=True, stop=True)
                mm.then_inc(pv_ok, 1)

            for t in range(TT + 2):
                if t < TT:
                    scores(t)
                if t >= 2:
                    transposes(t - 2)
                    weigh(t - 2)


def feed_forward(nc, x_sb, xnT, w_ffn, out):
    FB = FF // P
    STEPS, BETA = 5, 0.9
    GROUPS = [range(0, 4), range(4, 6), range(6, 8)]
    BANKS = [(0, 1, 2, 3), (0, 1), (2, 3)]
    ALL = len(GROUPS) * FB
    OPS = 3 * (STEPS - 1) + 2
    PER_BLOCK = 3
    RAW, WS, HS, HB = 6, 4, 3, 4
    ctx = ExitStack()
    with ctx:
        sb = lambda n, s, d=F32: ctx.enter_context(nc.sbuf_tensor(n, s, d))
        sem = lambda n: ctx.enter_context(nc.semaphore(n))
        w_raw = sb("f_raw", [P, RAW, 2 * D])
        w_s = sb("f_w", [P, WS, 2, 2 * D], F32R)
        relu = sb("f_relu", [P, HS, 512])
        sq = sb("f_sq", [P, HS, 512])
        h_s = sb("f_h", [P, HS, 2, 512], F32R)
        y_sb = sb("f_y", [P, TT, D])
        acc = sb("f_acc", [P, 2, 4, D])
        y_ps = [ctx.enter_context(nc.psum_tensor(f"f_y{i}", [P, 512], F32)) for i in range(4)]
        h_ps = [ctx.enter_context(nc.psum_tensor(f"f_h{i}", [P, 512], F32)) for i in range(HB)]
        w_in = [sem(f"f_w_in{n}") for n in range(RAW)]
        w_hi, w_lo, h_full, relu_ok, sq_ok, h_hi, h_lo = (sem("f_w_hi"), sem("f_w_lo"), sem("f_h_full"), sem("f_relu"),
                                                          sem("f_sq"), sem("f_h_hi"), sem("f_h_lo"))
        y_part, y_out, spike, done, stored = (sem("f_y_part"), sem("f_y_out"), sem("f_spike"), sem("f_done"),
                                              sem("f_stored"))
        block = ctx.enter_context(nc.Block())

        def tokens(n):
            tiles = GROUPS[n // FB]
            return slice(tiles[0] * P, (tiles[-1] + 1) * P), len(tiles) * P

        @block.sync
        def _(sp):
            for n in range(ALL):
                if n >= RAW:
                    sp.wait_ge(w_lo, n - RAW + 1)
                sp.dma_start(w_raw[:, n % RAW, :], w_ffn[n % FB]).then_inc(w_in[n % RAW], 16)
            for t in range(TT):
                sp.wait_ge(done, t + 1)
                sp.dma_start(out[t * P:(t + 1) * P, :], x_sb[:, t, :]).then_inc(stored, 16)
            sp.wait_ge(stored, 16 * TT)

        @block.gpsimd
        def _(pool):
            for n in range(ALL):
                pool.wait_ge(w_hi, n + 1)
                pool.tensor_tensor(w_s[:, n % WS, 1, :], w_raw[:, n % RAW, :], w_s[:, n % WS, 0, :].bitcast(F32),
                                   ALU.subtract).then_inc(w_lo, 1)

        @block.scalar
        def _(act):
            def weights(n):
                act.wait_ge(w_in[n % RAW], 16 * (n // RAW + 1))
                if n >= WS:
                    act.wait_ge(y_part, n - WS + 1)
                act.activation(w_s[:, n % WS, 0, :], w_raw[:, n % RAW, :], ACT.Copy).then_inc(w_hi, 1)

            for n in range(WS - 1):
                weights(n)
            for n in range(ALL):
                w = tokens(n)[1]
                act.wait_ge(h_full, n + 1)
                act.activation(relu[:, n % HS, 0:w], h_ps[n % HB][:, 0:w], ACT.Relu).then_inc(relu_ok, 1)
                act.wait_ge(sq_ok, n + 1)
                if n >= HS:
                    act.wait_ge(y_part, n - HS + 1)
                act.activation(h_s[:, n % HS, 0, 0:w], sq[:, n % HS, 0:w], ACT.Copy).then_inc(h_hi, 1)
                if n + WS - 1 < ALL:
                    weights(n + WS - 1)
                if n % FB == FB - 1:
                    act.wait_ge(y_part, n + 1)
                    for t, k in zip(GROUPS[n // FB], BANKS[n // FB]):
                        act.activation(y_sb[:, t, :], y_ps[k][:], ACT.Copy).then_inc(y_out, 1)

        @block.vector
        def _(dve):
            def spikes(q):
                t, k = q // OPS, q % OPS
                y, (m0, m1, charge, total) = y_sb[:, t, :], (acc[:, t % 2, n, :] for n in range(4))
                step = (k - 1) // 3
                old, new = (y if step == 0 else (m0, m1)[(step - 1) % 2]), (m0, m1)[step % 2]
                if q:
                    dve.wait_ge(spike, q)
                if k == 0:
                    dve.wait_ge(y_out, t + 1)
                    ins = dve.tensor_scalar(total, y, 1.0, None, ALU.is_gt)
                elif k == OPS - 1:
                    ins = dve.scalar_tensor_tensor(x_sb[:, t, :], total, 1.0 / STEPS, x_sb[:, t, :],
                                                   ALU.mult, ALU.add)
                elif k % 3 == 1:
                    ins = dve.scalar_tensor_tensor(charge, old, BETA, y, ALU.mult, ALU.add)
                elif k % 3 == 2:
                    ins = dve.scalar_tensor_tensor(new, old, 1.0, charge, ALU.is_gt, ALU.subtract, reverse1=True)
                else:
                    ins = dve.scalar_tensor_tensor(total, new, 1.0, total, ALU.is_gt, ALU.add)
                ins.then_inc(spike, 1)
                if k == OPS - 1:
                    dve.wait_ge(spike, q + 1)
                    dve.sem_inc(done, 1)

            q = 0
            for n in range(ALL):
                w = tokens(n)[1]
                dve.wait_ge(relu_ok, n + 1)
                dve.scalar_tensor_tensor(sq[:, n % HS, 0:w], h_ps[n % HB][:, 0:w], 0.0, relu[:, n % HS, 0:w],
                                         ALU.max, ALU.mult).then_inc(sq_ok, 1)
                dve.wait_ge(h_hi, n + 1)
                dve.tensor_tensor(h_s[:, n % HS, 1, 0:w], sq[:, n % HS, 0:w], h_s[:, n % HS, 0, 0:w].bitcast(F32),
                                  ALU.subtract).then_inc(h_lo, 1)
                if n % FB:
                    end = min(q + PER_BLOCK, OPS * GROUPS[n // FB][0])
                    for q in range(q, end):
                        spikes(q)
                    q = max(q, end)
            for q in range(q, OPS * TT):
                spikes(q)

        @block.tensor
        def _(pe):
            def hidden(n):
                at, w = tokens(n)
                pe.wait_ge(w_lo, n + 1)
                if n >= HB:
                    pe.wait_ge(sq_ok, n - HB + 1)
                fc = w_s[:, n % WS].rearrange("p s (m c f) -> p s m c f", m=2, c=DC)
                three_passes(pe, h_ps[n % HB][:, 0:w], lambda a, c: fc[:, a, 0, c, :],
                             lambda a, c: xnT[:, a, c, at]).then_inc(h_full, 1)

            def project(n):
                group, f = n // FB, n % FB
                pe.wait_ge(h_lo, n + 1)
                if f == 0 and group:
                    pe.wait_ge(y_out, BANKS[group][-1] + 1)
                for k, bank in enumerate(BANKS[group]):
                    for m, (a, b) in enumerate(((0, 0), (1, 0), (0, 1))):
                        mm = pe.matmul(y_ps[bank][:], h_s[:, n % HS, a, k * P:(k + 1) * P],
                                       w_s[:, n % WS, b, D:2 * D],
                                       start=(f == 0 and m == 0), stop=(f == FB - 1 and m == 2))
                mm.then_inc(y_part, 1)

            for n in range(ALL + 1):
                if n < ALL:
                    hidden(n)
                if n >= 1:
                    project(n - 1)


def perceiver(nc, x, yT, xwq, xwk, xwv, xwp, xbp, awq, abq, awk, abk, awv, abv, awo, abo, w_ffn, alibi,
              out, q_dram, o_dram):
    ctx = ExitStack()
    with ctx:
        sb = lambda n, s, d=F32: ctx.enter_context(nc.sbuf_tensor(n, s, d))
        ident = sb("ident", [P, P])
        with nc.sbuf_tensor("wk_s", [P, 2, DC, D], F32R) as wk_s, nc.sbuf_tensor("wv_s", [P, 2, DC, D], F32R) as wv_s:
            prologue(nc, x, xwq, xwk, xwv, q_dram, wk_s, wv_s, ident)
            cross_attention(nc, yT, q_dram, o_dram, wk_s, wv_s, ident)
        x_sb = sb("x_sb", [P, TT, D])
        att = sb("att", [P, 2, DC, TOK], F32R)
        xnT = sb("xnT", [P, 2, DC, TOK], F32R)
        with ExitStack() as inner:
            qT = inner.enter_context(nc.sbuf_tensor("qT", [P, NBLK, TOK], F32))
            kT = inner.enter_context(nc.sbuf_tensor("kT", [P, NBLK, TOK], F32))
            v_sb = inner.enter_context(nc.sbuf_tensor("v_self", [P, TT, D], F32))
            w_in = [inner.enter_context(nc.semaphore(f"aw_in{n}")) for n in range(3)]
            with nc.sbuf_tensor("aw_raw", [P, 3, DC, D], F32) as w_raw:
                cross_output(nc, x, o_dram, xwp, xbp, att, x_sb, xnT, w_raw, w_in, (awq, awk, awv), ident)
                qkv(nc, xnT, w_raw, w_in, abq, abk, abv, qT, kT, v_sb)
            wo_s = inner.enter_context(nc.sbuf_tensor("wo_s", [P, 2, DC, D], F32R))
            self_attention(nc, qT, kT, v_sb, alibi, awo, att, wo_s, ident)
            with nc.sbuf_tensor("so_rows", [P, TT * D], F32) as rows, nc.sbuf_tensor("bo_sb", [P, D], F32) as bo_sb, \
                    nc.semaphore("bo_in") as bo_in:
                def load(sp):
                    sp.dma_start(bo_sb[:], abo.rearrange("(a d) -> a d", a=1).broadcast_to((P, D))).then_inc(bo_in, 16)

                def bias(pool, biased):
                    pool.wait_ge(bo_in, 16)
                    for t in range(TT):
                        pool.tensor_tensor(x_sb[:, t, :], x_sb[:, t, :], bo_sb[:], ALU.add).then_inc(biased, 1)

                project_and_norm(nc, "so", att, wo_s, x_sb, xnT, rows[:], ident, load=load, bias=bias)
        feed_forward(nc, x_sb, xnT, w_ffn, out)


def kernel(x, ctx_1024, L0_xattn_Wq, L0_xattn_Wk, L0_xattn_Wv, L0_xattn_Wp, L0_xattn_bp, L0_attn_Wq, L0_attn_bq,
           L0_attn_Wk, L0_attn_bk, L0_attn_Wv, L0_attn_bv, L0_attn_Wo, L0_attn_bo, L0_ffn_W_fc, L0_ffn_W_proj):
    import concourse.bacc as bacc
    from concourse.bass_utils import run_bass_kernel_spmd

    y = np.zeros((B, D, MP), np.float32)
    y[:, :, :M] = np.asarray(ctx_1024).transpose(0, 2, 1)
    fc = np.asarray(L0_ffn_W_fc).reshape(FF // P, P, DC, P).transpose(0, 3, 2, 1).reshape(FF // P, P, D)
    proj = np.asarray(L0_ffn_W_proj).T.reshape(FF // P, P, D)
    slopes = np.power(np.float32(2.0), np.linspace(-4.0, -0.3, H, dtype=np.float32))
    bias = -(slopes[:, None] * np.arange(N, dtype=np.float32)[None, :])
    bias = bias.reshape(4, 4, N).transpose(1, 0, 2).reshape(1, H * N)

    def turn(w):
        return np.ascontiguousarray(np.asarray(w).T)

    def columns(b):
        return np.ascontiguousarray(np.asarray(b).reshape(NBLK, P).T)

    arrays = {
        "x": np.asarray(x).reshape(TOK, D), "yT": y.reshape(B, DC, P, MP),
        "xwq": L0_xattn_Wq, "xwk": L0_xattn_Wk, "xwv": L0_xattn_Wv, "xwp": L0_xattn_Wp, "xbp": L0_xattn_bp,
        "awq": turn(L0_attn_Wq), "abq": columns(L0_attn_bq), "awk": turn(L0_attn_Wk), "abk": columns(L0_attn_bk),
        "awv": turn(L0_attn_Wv), "abv": L0_attn_bv, "awo": turn(L0_attn_Wo), "abo": L0_attn_bo,
        "w_ffn": np.stack([fc, proj], axis=2).reshape(FF // P, P, 2 * D), "alibi": bias,
    }
    nc = bacc.Bacc("TRN2", target_bir_lowering=False, num_devices=1)
    given = {}
    for name, a in arrays.items():
        arrays[name] = a = np.ascontiguousarray(a)
        given[name] = nc.dram_tensor(name, a.shape, mybir.dt.from_np(a.dtype), kind="ExternalInput").ap()
    out = nc.dram_tensor("out", (TOK, D), F32, kind="ExternalOutput").ap()
    q_dram = nc.dram_tensor("q_scratch", (P, NBLK * 2, TOK), F32, kind="Internal").ap()
    o_dram = nc.dram_tensor("o_scratch", (P, NBLK, TOK), F32, kind="Internal").ap()
    perceiver(nc, **given, out=out, q_dram=q_dram, o_dram=o_dram)
    result = run_bass_kernel_spmd(nc, [arrays], core_ids=[0])
    return result.results[0]["out"].reshape(B, N, D)
```

```python
import numpy as np
import concourse.bass as bass
from concourse import mybir
from contextlib import ExitStack

F32 = mybir.dt.float32
F32R = mybir.dt.float32r
ALU = mybir.AluOpType
ACT = mybir.ActivationFunctionType
AX = mybir.AxisListType

B, N, M, D = 16, 64, 1601, 512
H, DH = 16, 32
FF = 2048
P = 128
DC = D // P
MP = M + M % 2
TOK = B * N
TT = TOK // P
JT = -(-M // P)
JL = M - (JT - 1) * P
KW = 402
KC = -(-MP // KW)
KWL = MP - (KC - 1) * KW
NBLK = H * DH // P
PAIRS = H // 2
TG = -(-JT // 2)
RING = 3
PT_RING = 4
P_RING = 4
SCALE = float(DH) ** -0.5
EPS = 1e-5

STEADY = [("V", 0, "adadaaadadaaa"),
          ("S", 0), ("K", 1, 0), ("E", 0), ("K", 1, 1), ("N", 0), ("K", 1, 2),
          ("S", 1), ("K", 1, 3), ("E", 1), ("K", 2, 0), ("N", 1), ("K", 2, 1),
          ("S", 2), ("K", 2, 2), ("E", 2), ("T", 0, 0, "d"), ("K", 2, 3), ("T", 0, 1, "dd"), ("N", 2),
          ("S", 3), ("T", 0, 3, "aaa"), ("E", 3), ("T", 0, 6, "d"), ("K", 3, 0), ("N", 3), ("F", 0), ("O", 0),
          ("S", 4), ("K", 3, 1), ("E", 4), ("N", 4), ("K", 3, 2), ("K", 3, 3), ("H", 0), ("H", 1), ("H", 2),
          ("H", 3), ("T", 1, 0, "a"),
          ("S", 5), ("T", 1, 1, "aa"), ("E", 5), ("T", 1, 3, "ddd"), ("N", 5), ("L", 0),
          ("S", 6), ("T", 1, 6, "a"), ("F", 1), ("O", 1), ("L", 3), ("T", 2, 0, "aad"), ("E", 6), ("T", 2, 3, "d"),
          ("L", 1), ("T", 2, 4, "a"), ("L", 2), ("N", 6),
          ("S", 7), ("T", 2, 5, "aa"), ("F", 2), ("E", 7), ("O", 2), ("N", 7), ("K", 4, 0), ("K", 4, 1), ("K", 4, 2),
          ("T", 3, 0, "adaddaa"), ("F", 3), ("K", 4, 3), ("O", 3)]
OUT_STEPS = [("W",), ("P", 0), ("P", 2), ("Z",)]
LAST = [s for s in STEADY if s[0] not in "HL" and s[:2] != ("K", 4)]
LAST[LAST.index(("S", 7)) + 1:LAST.index(("S", 7)) + 1] = OUT_STEPS[:1]
LAST[LAST.index(("E", 7)) + 1:LAST.index(("E", 7)) + 1] = OUT_STEPS[1:3]
LAST.append(OUT_STEPS[3])
STORED = (B - 1) * N
POOL_LOW = DC - 1


def ring_units(order):
    units, act, dve = [], 0, 0
    for step in order:
        if step[0] == "V":
            new = [("V", step[1] + n, by) for n, by in enumerate(step[2])]
        elif step[0] == "K":
            new = [("K", step[1:], "d")]
        elif step[0] == "T":
            new = [("T", (step[1], step[2] + n), by) for n, by in enumerate(step[3])]
        else:
            continue
        for kind, index, by in new:
            act += kind == "K" or by == "a"
            dve += by == "d"
            units.append((kind, index, by, act, dve))
    return units


UNITS = ring_units(STEADY)
LAST_UNITS = ring_units(LAST)
NU = len(UNITS)
ACT_N, DVE_N = UNITS[-1][3], UNITS[-1][4]
FIRST = KC
assert NU % RING == 0
PV_CREDIT, EXP_CREDIT, N_CREDIT, O_CREDIT, S_CREDIT, ST_CREDIT = 8, 2, 2, 1, 1, 16
PV_N = NBLK * TG


def kchunk(c):
    return c * KW, KW if c < KC - 1 else KWL


def jtile(t):
    return P if t < JT - 1 else JL


def three_passes(pe, out, left, right):
    for c in range(DC):
        for n, (a, b) in enumerate(((0, 0), (1, 0), (0, 1))):
            mm = pe.matmul(out, left(a, c), right(b, c),
                           start=(c == 0 and n == 0), stop=(c == DC - 1 and n == 2))
    return mm


class Context:

    def __init__(self, nc, ctx):
        self.raw = ctx.enter_context(nc.sbuf_tensor("y_raw", [P, DC, MP], F32))
        self.parts = ctx.enter_context(nc.sbuf_tensor("y_parts", [P, 2, DC, MP], F32R))
        raw = self.raw[:].rearrange("p c m -> p (c m)")
        parts = self.parts[:].rearrange("p s c m -> p s (c m)")
        self.rows = raw[:, 0:DC * TOK]
        self.w_raw = raw[:, DC * TOK:DC * TOK + DC * D].rearrange("p (c e) -> p c e", c=DC)
        self.att = parts[:, :, 0:DC * TOK].rearrange("p s (c t) -> p s c t", c=DC)
        self.w_out = parts[:, :, DC * TOK:DC * TOK + DC * D].rearrange("p s (c e) -> p s c e", c=DC)


class Shared:

    def __init__(self, nc, ctx, context):
        sb = lambda n, s, d=F32: ctx.enter_context(nc.sbuf_tensor(n, s, d))
        sem = lambda n: ctx.enter_context(nc.semaphore(n))
        self.wk_s, self.wv_s = sb("wk_s", [P, 2, DC, D], F32R), sb("wv_s", [P, 2, DC, D], F32R)
        self.y_raw = context.raw
        self.y_hi, self.y_lo = context.parts[:, 0], context.parts[:, 1]
        self.k_s = sb("k_s", [P, 2, 2, MP], F32R)
        self.y_in = [sem(f"y_in{c}") for c in range(DC)]
        self.y_hi_ok, self.y_lo_ok = sem("y_hi_ok"), sem("y_lo_ok")
        self.y_pool_ok = sem("y_pool_ok")
        self.full = sem("ring_full")
        self.act_out, self.dve_out = sem("ring_act_out"), sem("ring_dve_out")


def keys_high(act, sh, src, i, c):
    at, w = kchunk(c)
    act.activation(sh.k_s[0:64, i % 2, 0, at:at + w], src[0:64, 0:w], ACT.Copy)
    act.activation(sh.k_s[64:P, i % 2, 1, at:at + w], src[64:P, 0:w], ACT.Copy).then_inc(sh.act_out, 1)


def keys_low(dve, sh, src, act_count, i, c):
    at, w = kchunk(c)
    dve.wait_ge(sh.act_out, act_count)
    k0, k1 = sh.k_s[:, i % 2, 0, at:at + w], sh.k_s[:, i % 2, 1, at:at + w]
    dve.tensor_tensor(k0[64:P], src[0:64, 0:w], k0[0:64].bitcast(F32), ALU.subtract)
    dve.tensor_tensor(k1[0:64], src[64:P, 0:w], k1[64:P].bitcast(F32), ALU.subtract).then_inc(sh.dve_out, 1)


def project_keys(pe, sh, out, i, c):
    at, w = kchunk(c)
    return three_passes(pe, out[:, 0:w], lambda a, d: sh.wk_s[:, a, d, i * P:(i + 1) * P],
                        lambda a, d: (sh.y_hi, sh.y_lo)[a][:, d, at:at + w])


def prologue(nc, x, yT, wq, wk, wv, q_dram, sh, ident):
    ctx = ExitStack()
    with ctx:
        sb = lambda n, s, d=F32: ctx.enter_context(nc.sbuf_tensor(n, s, d))
        sem = lambda n: ctx.enter_context(nc.semaphore(n))
        HALF = TT // 2
        NQ = NBLK * 2
        xs = sb("p_x", [P, TT * D], F32R)
        x_rows = xs[:].bitcast(F32).rearrange("p (t d) -> p t d", t=TT)
        qs = xs[:].rearrange("p (r s t) -> p r s t", r=2, s=2)
        xnT = sb("p_xnT", [P, DC, TOK])
        wq_sb = sb("p_wq", [P, DC, D])
        wraw = sb("p_wraw", [P, 2, DC, D])
        stats = sb("p_stats", [P, TT, 6])
        mv = sb("p_mv", [P, TT, 2])
        ve = sb("p_ve", [P, 5, TT])
        ps = [ctx.enter_context(nc.psum_tensor(f"p_ps{i}", [P, 512], F32)) for i in range(4)]
        k_ps = [ctx.enter_context(nc.psum_tensor(f"p_k{i}", [P, 512], F32)) for i in range(KC)]
        x_in, wq_in = [sem("p_x_in0"), sem("p_x_in1")], sem("p_wq_in")
        w_in = [sem("p_wk_in"), sem("p_wv_in")]
        ident_ok, ln_step, root_ok, xn_ok = sem("p_ident"), sem("p_ln_step"), sem("p_root"), sem("p_xn")
        xt_ps, xt_ok, q_ps, q_hi, q_lo = sem("p_xt_ps"), sem("p_xt_ok"), sem("p_q_ps"), sem("p_q_hi"), sem("p_q_lo")
        q_out = [sem("p_q_out0"), sem("p_q_out1")]
        w_hi, w_lo, pool_passed = sem("p_w_hi"), sem("p_w_lo"), sem("p_pool_passed")
        block = ctx.enter_context(nc.Block())

        def queries(n, part):
            i, half = n // 2, n % 2
            return qs[:, i % 2, part, half * 512:half * 512 + 512]

        @block.sync
        def _(sp):
            for half in range(2):
                at = slice(half * HALF * P, (half + 1) * HALF * P)
                sp.dma_start(x_rows[:, half * HALF:(half + 1) * HALF],
                             x[at].rearrange("(t p) d -> p t d", p=P)).then_inc(x_in[half], 16)
            sp.dma_start(wq_sb[:], wq.rearrange("(c p) e -> p c e", p=P)).then_inc(wq_in, 16)
            for c in range(DC):
                sp.dma_start(sh.y_raw[:, c, :], yT[0, c]).then_inc(sh.y_in[c], 16)
            for n, w in enumerate((wk, wv)):
                sp.dma_start(wraw[:, n], w.rearrange("(c p) e -> p c e", p=P)).then_inc(w_in[n], 16)
            for i in range(NBLK):
                sp.wait_ge(q_lo, 2 * i + 2)
                sp.dma_start(q_dram[:, 2 * i:2 * i + 2, :], qs[:, i % 2].bitcast(F32)).then_inc(q_out[i % 2], 16)
            for r in range(2):
                sp.wait_ge(q_out[r], 16 * (NBLK // 2))

        @block.gpsimd
        def _(pool):
            pool.memset(ident[:], 0.0).then_inc(ident_ok, 1)
            pool.wait_ge(ident_ok, 1)
            pool.affine_select(out=ident[:], in_=ident[:], compare_op=ALU.not_equal, fill=1.0, base=0,
                               pattern=[[-1, P]], channel_multiplier=1).then_inc(ident_ok, 1)
            pool.wait_ge(sh.y_hi_ok, DC)
            pool.sem_inc(pool_passed, 1)
            pool.tensor_tensor(sh.y_lo[:, POOL_LOW, :], sh.y_raw[:, POOL_LOW, :],
                               sh.y_hi[:, POOL_LOW, :].bitcast(F32), ALU.subtract).then_inc(sh.y_pool_ok, 1)

        def after(n, weights, context):
            if 2 <= n < 2 + DC:
                context(n - 2)
            if n >= NQ - 2:
                weights(n - (NQ - 2))

        @block.vector
        def _(dve):
            for t in range(TT):
                if t % HALF == 0:
                    dve.wait_ge(x_in[t // HALF], 16)
                dve.bn_stats(stats[:, t, :], x_rows[:, t, :]).then_inc(ln_step, 1)
            for t in range(TT):
                dve.wait_ge(ln_step, t + 1)
                dve.bn_aggr(mv[:, t, :], stats[:, t, :]).then_inc(ln_step, 1)
            step = 2 * TT
            dve.wait_ge(ln_step, step)
            dve.tensor_scalar_add(ve[:, 0, :], mv[:, :, 1], EPS).then_inc(ln_step, 1)
            dve.wait_ge(root_ok, 1)
            dve.reciprocal(ve[:, 2, :], ve[:, 1, :]).then_inc(ln_step, 1)
            dve.wait_ge(ln_step, step + 2)
            dve.tensor_tensor(ve[:, 3, :], ve[:, 2, :], ve[:, 2, :], ALU.mult).then_inc(ln_step, 1)
            dve.wait_ge(ln_step, step + 3)
            dve.tensor_tensor(ve[:, 4, :], ve[:, 3, :], ve[:, 0, :], ALU.mult).then_inc(ln_step, 1)
            dve.wait_ge(ln_step, step + 4)
            dve.tensor_scalar(ve[:, 3, :], ve[:, 4, :], -0.5, 1.5, ALU.mult, ALU.add).then_inc(ln_step, 1)
            dve.wait_ge(ln_step, step + 5)
            dve.tensor_tensor(ve[:, 4, :], ve[:, 2, :], ve[:, 3, :], ALU.mult).then_inc(ln_step, 1)
            dve.wait_ge(ln_step, step + 6)
            for t in range(TT):
                dve.tensor_scalar(x_rows[:, t, :], x_rows[:, t, :], mv[:, t, 0:1], ve[:, 4, t:t + 1],
                                  ALU.subtract, ALU.mult).then_inc(xn_ok, 1)

            def weights(w):
                dve.wait_ge(w_hi, w + 1)
                dst = (sh.wk_s, sh.wv_s)[w]
                dve.tensor_tensor(dst[:, 1], wraw[:, w], dst[:, 0].bitcast(F32), ALU.subtract).then_inc(w_lo, 1)

            def context(c):
                if c != POOL_LOW:
                    dve.wait_ge(sh.y_hi_ok, c + 1)
                    dve.tensor_tensor(sh.y_lo[:, c, :], sh.y_raw[:, c, :], sh.y_hi[:, c, :].bitcast(F32),
                                      ALU.subtract).then_inc(sh.y_lo_ok, 1)

            for n in range(NQ):
                dve.wait_ge(q_hi, n + 1)
                if n >= 4 and n % 2 == 0:
                    dve.wait_ge(q_out[n // 2 % 2], 16 * (n // 4))
                dve.tensor_tensor(queries(n, 1), ps[n % 4][:], queries(n, 0).bitcast(F32),
                                  ALU.subtract).then_inc(q_lo, 1)
                after(n, weights, context)
            for c in range(KC):
                keys_low(dve, sh, k_ps[c], c + 1, 0, c)

        @block.scalar
        def _(act):
            act.wait_ge(ln_step, 2 * TT + 1)
            act.activation(ve[:, 1, :], ve[:, 0, :], ACT.Sqrt).then_inc(root_ok, 1)
            for t in range(TT):
                act.wait_ge(xt_ps, t + 1)
                act.activation(xnT[:, :, t * P:(t + 1) * P],
                               ps[t % 4][:].rearrange("p (c q) -> p c q", c=DC), ACT.Copy).then_inc(xt_ok, 1)

            def weights(w):
                act.wait_ge(w_in[w], 16)
                act.activation((sh.wk_s, sh.wv_s)[w][:, 0], wraw[:, w], ACT.Copy).then_inc(w_hi, 1)

            def context(c):
                act.wait_ge(sh.y_in[c], 16)
                act.activation(sh.y_hi[:, c, :], sh.y_raw[:, c, :], ACT.Copy).then_inc(sh.y_hi_ok, 1)

            for n in range(NQ):
                act.wait_ge(q_ps, n + 1)
                if n >= 4 and n % 2 == 0:
                    act.wait_ge(q_out[n // 2 % 2], 16 * (n // 4))
                act.activation(queries(n, 0), ps[n % 4][:], ACT.Copy).then_inc(q_hi, 1)
                after(n, weights, context)
            for c in range(KC):
                act.wait_ge(sh.full, c + 1)
                keys_high(act, sh, k_ps[c], 0, c)

        @block.tensor
        def _(pe):
            pe.wait_ge(ident_ok, 2)
            for t in range(TT):
                pe.wait_ge(xn_ok, t + 1)
                if t >= 4:
                    pe.wait_ge(xt_ok, t - 3)
                for c in range(DC):
                    mm = pe.transpose(ps[t % 4][:, c * P:(c + 1) * P], x_rows[:, t, c * P:(c + 1) * P], ident[:])
                mm.then_inc(xt_ps, 1)
            pe.wait_ge(wq_in, 16)
            pe.wait_ge(xt_ok, TT)
            for n in range(NQ):
                i, half = n // 2, n % 2
                if n >= 4:
                    pe.wait_ge(q_lo, n - 3)
                for c in range(DC):
                    mm = pe.matmul(ps[n % 4][:], wq_sb[:, c, i * P:(i + 1) * P],
                                   xnT[:, c, half * 512:half * 512 + 512], start=(c == 0), stop=(c == DC - 1))
                mm.then_inc(q_ps, 1)
            pe.wait_ge(w_lo, 1)
            pe.wait_ge(sh.y_lo_ok, POOL_LOW)
            pe.wait_ge(sh.y_pool_ok, 1)
            for c in range(KC):
                project_keys(pe, sh, k_ps[c], 0, c).then_inc(sh.full, 1)


def cross_attention(nc, yT, q_dram, o_dram, wp, sh, context, ident):
    ctx = ExitStack()
    with ctx:
        sb = lambda n, s, d=F32: ctx.enter_context(nc.sbuf_tensor(n, s, d))
        sem = lambda n: ctx.enter_context(nc.semaphore(n))
        y_raw, y_hi, y_lo, k_s = sh.y_raw, sh.y_hi, sh.y_lo, sh.k_s
        y_in, y_hi_ok, y_lo_ok, y_pool_ok = sh.y_in, sh.y_hi_ok, sh.y_lo_ok, sh.y_pool_ok
        full, act_out, dve_out = sh.full, sh.act_out, sh.dve_out
        v_sb = sb("v_sb", [P, JT, D])
        q_s = sb("q_s", [P, 2, NBLK * 2, P], F32R)
        prob = sb("prob", [P, P_RING, MP])
        pT = sb("pT", [P, PT_RING, 512])
        o_sb = sb("o_sb", [P, NBLK, N])
        peak = sb("peak", [P, 2, 4])
        total = sb("total", [P, 2, 4])
        s_ps = ctx.enter_context(nc.psum_tensor("s_ps", [P, KC * 512], F32))
        ring = [ctx.enter_context(nc.psum_tensor(f"ring{i}", [P, 512], F32)) for i in range(RING)]
        o_ps = ctx.enter_context(nc.psum_tensor("o_ps", [P, N], F32))
        s_v = s_ps[:].rearrange("p (c k) -> p c k", c=KC)

        q_zero, q_in = sem("q_zero"), sem("q_in")
        sum_ok = sem("sum_ok")
        s_full = sem("scores_full")
        peak_step = sem("peak_step")
        bias_ok, exp_ok, norm_ok = sem("bias_ok"), sem("exp_ok"), sem("norm_ok")
        pool_passed = sem("pool_passed")
        wp_in, o_back, out_hi, out_lo = sem("wp_in"), sem("o_back"), sem("out_hi"), sem("out_lo")
        o_raw = context.rows.rearrange("p (c t) -> p c t", c=DC)
        pv_ok = sem("pv_ok")
        o_out, o_stored = sem("o_out"), sem("o_stored")
        block = ctx.enter_context(nc.Block())

        def emptied(eng, batch, units, *which):
            acts, dves = [], []
            for u in which:
                _, _, by, a, d = units[u] if u >= 0 else UNITS[u]
                if by == "a":
                    acts.append(a - ACT_N if u < 0 else a)
                else:
                    dves.append(d - DVE_N if u < 0 else d)
            if acts:
                eng.wait_ge(act_out, FIRST + batch * ACT_N + max(acts))
            if dves:
                eng.wait_ge(dve_out, FIRST + batch * DVE_N + max(dves))

        def context_end(units):
            return max(n for n, x in enumerate(units) if x[0] == "V" or x[0] == "K" and x[1][0] == NBLK - 1)

        def out_operand(step):
            if step[0] == "W":
                return context.w_raw, context.w_out, wp_in, 16
            if step[0] == "P":
                return (o_raw[:, step[1]:step[1] + 2, 0:STORED], context.att[:, :, step[1]:step[1] + 2, 0:STORED],
                        o_back, 16)
            return o_sb[:], context.att[:, :, :, STORED:TOK], o_out, O_CREDIT + NBLK * B

        def first_v(units):
            return [next((x[1], by) for x in units if x[0] == "V" and x[2] == by) for by in "ad"]

        def bank(u):
            return ring[(FIRST + u) % RING]

        @block.sync
        def _(sp):
            sp.sem_inc(o_stored, ST_CREDIT)

            def load(batch, c):
                sp.dma_start(y_raw[:, c, :],
                             yT[bass.ds(batch, 1), c].rearrange("a p m -> (a p) m")).then_inc(y_in[c], 16)

            def load_q(batch):
                for k in range(4):
                    for second in range(2):
                        g = 2 * second + k % 2
                        sp.dma_start(
                            q_s[k * DH:(k + 1) * DH, second, :, (k % 2) * N:(k % 2 + 1) * N].bitcast(F32),
                            q_dram[g * DH:(g + 1) * DH, :, bass.ds(batch * N, N)]).then_inc(q_in, 16)

            sp.wait_ge(q_zero, 1)
            load_q(0)

            def store(batch):
                sp.wait_ge(o_out, O_CREDIT + NBLK * (batch + 1))
                sp.dma_start(o_dram[:, :, bass.ds(batch * N, N)], o_sb[:]).then_inc(o_stored, 16)

            with sp.Fori(0, B - 1) as b:
                for c in range(DC):
                    if c == POOL_LOW:
                        sp.wait_ge(y_pool_ok, b + 1)
                    else:
                        sp.wait_ge(y_lo_ok, POOL_LOW * b + c + 1)
                    load(b + 1, c)
                sp.wait_ge(s_full, S_CREDIT + 2 * PAIRS * (b + 1))
                load_q(b + 1)
                store(b)
            sp.wait_ge(y_lo_ok, POOL_LOW * B)
            sp.wait_ge(y_pool_ok, B)
            sp.dma_start(context.w_raw, wp.rearrange("(c p) e -> p c e", p=P)).then_inc(wp_in, 16)
            sp.wait_ge(o_stored, ST_CREDIT + 16 * (B - 1))
            sp.dma_start(o_raw[:, :, 0:STORED], o_dram).then_inc(o_back, 16)

        @block.gpsimd
        def _(pool):
            pool.sem_inc(norm_ok, N_CREDIT)

            def settle():
                pool.sem_inc(pool_passed, 1)

            def low(pool):
                pool.tensor_tensor(y_lo[:, POOL_LOW, :], y_raw[:, POOL_LOW, :], y_hi[:, POOL_LOW, :].bitcast(F32),
                                   ALU.subtract).then_inc(y_pool_ok, 1)

            def high(batch, c):
                pool.wait_ge(y_in[c], 16 * (batch + 1))
                settle()
                pool.tensor_scalar(y_hi[:, c, :], y_raw[:, c, :], 1.0, 1.0, ALU.mult,
                                   ALU.mult).then_inc(y_hi_ok, 1)

            def run(batch, order, units):
                for step in order:
                    if step[0] == "N":
                        p = step[1]
                        pool.wait_ge(sum_ok, PAIRS * batch + p + 1)
                        settle()
                        pool.tensor_scalar(prob[:, p % P_RING, 0:M], prob[:, p % P_RING, 0:M],
                                           total[:, p % 2, 3:4], 1.0, ALU.mult, ALU.mult).then_inc(norm_ok, 1)
                    elif step[0] == "H":
                        if step[1] == 0:
                            pool.wait_ge(full, FIRST + NU * batch + context_end(units) + 1)
                        high(batch + 1, step[1])
                    elif step[0] == "L" and step[1] == POOL_LOW:
                        pool.wait_ge(y_hi_ok, DC * (batch + 2))
                        low(pool)

            pool.memset(q_s[:].bitcast(F32), 0.0).then_inc(q_zero, 1)
            with pool.Fori(0, B - 1) as b:
                run(b, STEADY, UNITS)
            run(B - 1, LAST, LAST_UNITS)

        @block.scalar
        def _(act):
            act.sem_inc(exp_ok, EXP_CREDIT)
            act.sem_inc(o_out, O_CREDIT)

            def run(batch, order, units):
                u = 0
                for step in order:
                    if step[0] == "V":
                        for t in range(step[1], step[1] + len(step[2])):
                            if units[u][2] == "a":
                                if (t, "a") in first_v(units):
                                    act.wait_ge(pv_ok, PV_CREDIT + PV_N * batch)
                                act.wait_ge(full, FIRST + NU * batch + u + 1)
                                m = jtile(t)
                                act.activation(v_sb[0:m, t, :], bank(u)[0:m, :], ACT.Copy).then_inc(act_out, 1)
                            u += 1
                    elif step[0] == "K":
                        _, i, c = step
                        if c == 0:
                            act.wait_ge(s_full, S_CREDIT + 2 * PAIRS * batch + 4 * (i - 1))
                        act.wait_ge(full, FIRST + NU * batch + u + 1)
                        keys_high(act, sh, bank(u), i, c)
                        u += 1
                    elif step[0] == "E":
                        p = step[1]
                        pair = PAIRS * batch + p
                        act.wait_ge(pv_ok, PV_CREDIT + PV_N * batch + TG * (p // 2 - 1))
                        act.wait_ge(bias_ok, pair + 1)
                        dst = prob[:, p % P_RING, :]
                        act.activation(dst[:, 0:3 * KW].rearrange("p (c k) -> p c k", c=3),
                                       s_v[:, 0:3, 0:KW], ACT.Exp, bias=peak[:, p % 2, 2:3], scale=SCALE,
                                       accum_out=total[:, p % 2, 0:1]).then_inc(exp_ok, 1)
                        act.activation(dst[:, 3 * KW:M], s_v[:, 3, 0:M - 3 * KW], ACT.Exp,
                                       bias=peak[:, p % 2, 2:3], scale=SCALE,
                                       accum_out=total[:, p % 2, 1:2]).then_inc(exp_ok, 1)
                    elif step[0] == "T":
                        _, i, g0, by = step
                        for g in range(g0, g0 + len(by)):
                            if units[u][2] == "a":
                                act.wait_ge(pv_ok, PV_CREDIT + PV_N * batch + TG * i + g - PT_RING + 1)
                                act.wait_ge(full, FIRST + NU * batch + u + 1)
                                m, w = (P, 512) if g < TG - 1 else (JL, 256)
                                act.activation(pT[0:m, (TG * i + g) % PT_RING, 0:w], bank(u)[0:m, 0:w],
                                               ACT.Copy).then_inc(act_out, 1)
                            u += 1
                    elif step[0] == "O":
                        i = step[1]
                        act.wait_ge(pv_ok, PV_CREDIT + PV_N * batch + TG * (i + 1))
                        if i == 0:
                            act.wait_ge(o_stored, ST_CREDIT + 16 * batch)
                        act.activation(o_sb[:, i, :], o_ps[:], ACT.Copy).then_inc(o_out, 1)
                    elif step[0] in "WPZ":
                        raw, parts, loaded, count = out_operand(step)
                        if step[0] == "W":
                            act.wait_ge(full, FIRST + NU * batch + context_end(units) + 1)
                        act.wait_ge(loaded, count)
                        act.activation(parts[:, 0], raw, ACT.Copy).then_inc(out_hi, 1)

            with act.Fori(0, B - 1) as b:
                run(b, STEADY, UNITS)
            run(B - 1, LAST, LAST_UNITS)

        @block.vector
        def _(dve):
            def split(batch, c):
                dve.wait_ge(y_hi_ok, DC * batch + c + 1)
                dve.tensor_tensor(y_lo[:, c, :], y_raw[:, c, :], y_hi[:, c, :].bitcast(F32),
                                  ALU.subtract).then_inc(y_lo_ok, 1)

            def run(batch, order, units):
                u = 0
                for step in order:
                    if step[0] == "V":
                        for t in range(step[1], step[1] + len(step[2])):
                            if units[u][2] == "d":
                                if (t, "d") in first_v(units):
                                    dve.wait_ge(pv_ok, PV_CREDIT + PV_N * batch)
                                dve.wait_ge(full, FIRST + NU * batch + u + 1)
                                m = jtile(t)
                                dve.tensor_copy(v_sb[0:m, t, :], bank(u)[0:m, :]).then_inc(dve_out, 1)
                            u += 1
                    elif step[0] == "K":
                        _, i, c = step
                        keys_low(dve, sh, bank(u), FIRST + batch * ACT_N + units[u][3], i, c)
                        u += 1
                    elif step[0] == "S":
                        p = step[1]
                        done = S_CREDIT + 2 * (PAIRS * batch + p)
                        small = 3 * (PAIRS * batch + p)
                        dve.wait_ge(s_full, done + 1)
                        dve.tensor_reduce(peak[:, p % 2, 0:1], s_v[:, 0:3, 0:KW], AX.XY, ALU.max).then_inc(peak_step, 1)
                        dve.wait_ge(s_full, done + 2)
                        dve.tensor_reduce(peak[:, p % 2, 1:2], s_v[:, 3, 0:M - 3 * KW], AX.X,
                                          ALU.max).then_inc(peak_step, 1)
                        dve.wait_ge(peak_step, small + 2)
                        dve.tensor_scalar(peak[:, p % 2, 2:3], peak[:, p % 2, 0:1], peak[:, p % 2, 1:2],
                                          -SCALE, ALU.max, ALU.mult).then_inc(bias_ok, 1)
                    elif step[0] == "N":
                        p = step[1]
                        small = 3 * (PAIRS * batch + p)
                        dve.wait_ge(exp_ok, EXP_CREDIT + 2 * (PAIRS * batch + p) + 2)
                        dve.tensor_tensor(total[:, p % 2, 2:3], total[:, p % 2, 0:1], total[:, p % 2, 1:2],
                                          ALU.add).then_inc(peak_step, 1)
                        dve.wait_ge(norm_ok, N_CREDIT + PAIRS * batch + p - 1)
                        dve.wait_ge(peak_step, small + 3)
                        dve.reciprocal(total[:, p % 2, 3:4], total[:, p % 2, 2:3]).then_inc(sum_ok, 1)
                    elif step[0] == "L" and step[1] != POOL_LOW:
                        split(batch + 1, step[1])
                    elif step[0] in "WPZ":
                        raw, parts, loaded, count = out_operand(step)
                        dve.wait_ge(out_hi, OUT_STEPS.index(step) + 1)
                        dve.tensor_tensor(parts[:, 1], raw, parts[:, 0].bitcast(F32), ALU.subtract).then_inc(out_lo, 1)
                    elif step[0] == "T":
                        _, i, g0, by = step
                        for g in range(g0, g0 + len(by)):
                            if units[u][2] == "d":
                                dve.wait_ge(pv_ok, PV_CREDIT + PV_N * batch + TG * i + g - PT_RING + 1)
                                dve.wait_ge(full, FIRST + NU * batch + u + 1)
                                m, w = (P, 512) if g < TG - 1 else (JL, 256)
                                dve.tensor_copy(pT[0:m, (TG * i + g) % PT_RING, 0:w],
                                                bank(u)[0:m, 0:w]).then_inc(dve_out, 1)
                            u += 1

            with dve.Fori(0, B - 1) as b:
                run(b, STEADY, UNITS)
            run(B - 1, LAST, LAST_UNITS)

        @block.tensor
        def _(pe):
            def project_v(out, t):
                m = jtile(t)
                return three_passes(pe, out[0:m, :], lambda a, d: (y_hi, y_lo)[a][:, d, t * P:t * P + m],
                                    lambda a, d: sh.wv_s[:, a, d, :])

            def scores(batch, p):
                pair = PAIRS * batch + p
                for c in range(KC):
                    at, w = kchunk(c)
                    if c == 0:
                        pe.wait_ge(exp_ok, EXP_CREDIT + 2 * pair - 1)
                    if c == KC - 1:
                        pe.wait_ge(exp_ok, EXP_CREDIT + 2 * pair)
                    for part in range(2):
                        mm = pe.matmul(s_v[:, c, 0:w], q_s[:, p % 2, p // 2 * 2 + part, :],
                                       k_s[:, (p // 2) % 2, p % 2, at:at + w], start=(part == 0), stop=(part == 1))
                    if c >= KC - 2:
                        mm.then_inc(s_full, 1)

            def run(batch, order, units):
                u = 0
                number = {(x[0], x[1]): n for n, x in enumerate(units)}
                for step in order:
                    if step[0] == "V":
                        for t in range(step[1], step[1] + len(step[2])):
                            emptied(pe, batch, units, u - RING)
                            project_v(bank(u), t).then_inc(full, 1)
                            u += 1
                    elif step[0] == "K":
                        _, i, c = step
                        if i == NBLK and c == 0:
                            pe.wait_ge(y_lo_ok, POOL_LOW * (batch + 2))
                            pe.wait_ge(y_pool_ok, batch + 2)
                        emptied(pe, batch, units, u - RING)
                        project_keys(pe, sh, bank(u), i % NBLK, c).then_inc(full, 1)
                        u += 1
                    elif step[0] == "S":
                        p = step[1]
                        if p == 0:
                            pe.wait_ge(q_in, 128 * (batch + 1))
                            emptied(pe, batch, units, block0_keys - NU)
                        elif p % 2 == 0:
                            emptied(pe, batch, units, number["K", (p // 2, KC - 1)])
                        scores(batch, p)
                    elif step[0] == "T":
                        _, i, g0, by = step
                        if g0 == 0:
                            pe.wait_ge(norm_ok, N_CREDIT + PAIRS * batch + 2 * i + 2)
                        for g in range(g0, g0 + len(by)):
                            emptied(pe, batch, units, u - RING)
                            for k, t in enumerate(range(2 * g, min(2 * g + 2, JT))):
                                m = jtile(t)
                                for second in range(2):
                                    at = k * 256 + second * P
                                    mm = pe.transpose(bank(u)[0:m, at:at + P],
                                                      prob[:, (2 * i + second) % P_RING, t * P:t * P + m], ident[:])
                            mm.then_inc(full, 1)
                            u += 1
                            if g >= 2:
                                weigh(batch, units, number, i, g - 2)
                    elif step[0] == "F":
                        weigh(batch, units, number, step[1], TG - 2)
                        weigh(batch, units, number, step[1], TG - 1)

            def weigh(batch, units, number, i, g):
                if g == 0:
                    pe.wait_ge(o_out, O_CREDIT + NBLK * batch + i)
                values = [number["V", t] for t in range(2 * g, min(2 * g + 2, JT))] if i == 0 else []
                emptied(pe, batch, units, number["T", (i, g)], *values)
                for k, t in enumerate(range(2 * g, min(2 * g + 2, JT))):
                    m = jtile(t)
                    for head in range(4):
                        at = k * 256 + head * N
                        mm = pe.matmul(o_ps[head * DH:(head + 1) * DH, :],
                                       v_sb[0:m, t, (4 * i + head) * DH:(4 * i + head + 1) * DH],
                                       pT[0:m, (TG * i + g) % PT_RING, at:at + N],
                                       start=(t == 0), stop=(t == JT - 1))
                mm.then_inc(pv_ok, 1)

            block0_keys = max(n for n, x in enumerate(UNITS) if x[0] == "K")
            pe.sem_inc(pv_ok, PV_CREDIT)
            pe.sem_inc(s_full, S_CREDIT)
            with pe.Fori(0, B - 1) as b:
                run(b, STEADY, UNITS)
            run(B - 1, LAST, LAST_UNITS)


class OutputAndNorm:

    HALF = TT // 2

    def __init__(self, nc, ctx, tag, att, w, x, xnT, rows, ident, bank):
        sb = lambda n, s, d=F32: ctx.enter_context(nc.sbuf_tensor(f"{tag}_{n}", s, d))
        sem = lambda n: ctx.enter_context(nc.semaphore(f"{tag}_{n}"))
        self.att, self.w, self.x, self.xnT, self.ident = att, w, x, xnT, ident
        self.product, self.turn = bank[:4], bank[4:]
        self.xn = rows.rearrange("p (t d) -> p t d", t=TT)
        self.stats, self.mv, self.ve = sb("stats", [P, TT, 6]), sb("mv", [P, TT, 2]), sb("ve", [P, 5, TT])
        self.biased, self.added, self.step, self.var_ok, self.root_ok = (
            sem("biased"), sem("added"), sem("step"), sem("var"), sem("root"))
        self.xn_ok, self.full, self.turned, self.hi_ok, self.lo_ok = (
            sem("xn_ok"), sem("full"), sem("turned"), sem("hi_ok"), sem("lo_ok"))
        self.n = 0

    def pe_products(self, pe, tiles):
        for t in tiles:
            if t >= 4:
                pe.wait_ge(self.added, t - 3)
            three_passes(pe, self.product[t % 4][:], lambda a, c: self.att[:, a, c, t * P:(t + 1) * P],
                         lambda a, c: self.w[:, a, c, :]).then_inc(self.full, 1)

    def pe_turn(self, pe, tiles):
        for t in tiles:
            pe.wait_ge(self.xn_ok, t + 1)
            if t >= 4:
                pe.wait_ge(self.lo_ok, t - 3)
            for c in range(DC):
                mm = pe.transpose(self.turn[t % 4][:, c * P:(c + 1) * P], self.xn[:, t, c * P:(c + 1) * P],
                                  self.ident[:])
            mm.then_inc(self.turned, 1)

    def act_root(self, act, half):
        at = slice(half * self.HALF, (half + 1) * self.HALF)
        act.wait_ge(self.var_ok, half + 1)
        act.activation(self.ve[:, 1, at], self.ve[:, 0, at], ACT.Sqrt).then_inc(self.root_ok, 1)

    def act_high(self, act, tiles):
        for t in tiles:
            act.wait_ge(self.turned, t + 1)
            act.activation(self.xnT[:, 0, :, t * P:(t + 1) * P],
                           self.turn[t % 4][:].rearrange("p (c q) -> p c q", c=DC), ACT.Copy).then_inc(self.hi_ok, 1)

    def dve_low(self, dve, tiles):
        for t in tiles:
            dve.wait_ge(self.hi_ok, t + 1)
            dve.tensor_tensor(self.xnT[:, 1, :, t * P:(t + 1) * P],
                              self.turn[t % 4][:].rearrange("p (c q) -> p c q", c=DC),
                              self.xnT[:, 0, :, t * P:(t + 1) * P].bitcast(F32), ALU.subtract).then_inc(self.lo_ok, 1)

    def dve_add(self, dve, tiles):
        x = self.x
        for t in tiles:
            dve.wait_ge(self.biased, t + 1)
            dve.wait_ge(self.full, t + 1)
            dve.tensor_tensor(x[:, t, :], self.product[t % 4][:], x[:, t, :], ALU.add).then_inc(self.added, 1)
            dve.wait_ge(self.added, t + 1)
            dve.bn_stats(self.stats[:, t, :], x[:, t, :]).then_inc(self.step, 1)
            self.n += 1

    def dve_norm(self, dve, half):
        mv, ve, step = self.mv, self.ve, self.step
        tiles = range(half * self.HALF, (half + 1) * self.HALF)
        at = slice(half * self.HALF, (half + 1) * self.HALF)
        dve.wait_ge(step, self.n)
        for t in tiles:
            dve.bn_aggr(mv[:, t, :], self.stats[:, t, :]).then_inc(step, 1)
            self.n += 1
        dve.wait_ge(step, self.n)
        dve.tensor_scalar_add(ve[:, 0, at], mv[:, at, 1], EPS).then_inc(self.var_ok, 1)
        dve.wait_ge(self.root_ok, half + 1)
        dve.reciprocal(ve[:, 2, at], ve[:, 1, at]).then_inc(step, 1)
        self.n += 1
        for out, a, b in ((3, 2, 2), (4, 3, 0)):
            dve.wait_ge(step, self.n)
            dve.tensor_tensor(ve[:, out, at], ve[:, a, at], ve[:, b, at], ALU.mult).then_inc(step, 1)
            self.n += 1
        dve.wait_ge(step, self.n)
        dve.tensor_scalar(ve[:, 3, at], ve[:, 4, at], -0.5, 1.5, ALU.mult, ALU.add).then_inc(step, 1)
        self.n += 1
        dve.wait_ge(step, self.n)
        dve.tensor_tensor(ve[:, 4, at], ve[:, 2, at], ve[:, 3, at], ALU.mult).then_inc(step, 1)
        self.n += 1
        dve.wait_ge(step, self.n)
        for t in tiles:
            dve.tensor_scalar(self.xn[:, t, :], self.x[:, t, :], mv[:, t, 0:1], ve[:, 4, t:t + 1],
                              ALU.subtract, ALU.mult).then_inc(self.xn_ok, 1)


def output_and_qkv(nc, x, bp, attn_w, attn_b, context, x_sb, xnT, qT, kT, v_sb, ident):
    ctx = ExitStack()
    with ctx:
        sb = lambda n, s, d=F32: ctx.enter_context(nc.sbuf_tensor(n, s, d))
        sem = lambda n: ctx.enter_context(nc.semaphore(n))
        bp_sb, bv_sb, b_col = sb("bp_sb", [P, D]), sb("bv_sb", [P, D]), sb("b_col", [P, 2, NBLK])
        wq_s = sb("awq_s", [P, 2, DC, D], F32R)
        w_qk = sb("aw_raw", [P, 2, DC, D])
        w_raw = [w_qk[:, 0], w_qk[:, 1], context.w_raw]
        att_room = [context.att[:, a].rearrange("p c t -> p (c t)").rearrange("p (s c e) -> p s c e", s=2, c=DC)
                    for a in range(2)]
        w_s = [wq_s[:], *att_room]
        bank = [ctx.enter_context(nc.psum_tensor(f"co_ps{i}", [P, 512], F32)) for i in range(8)]
        norm = OutputAndNorm(nc, ctx, "co", context.att, context.w_out, x_sb, xnT, context.rows, ident, bank)
        x_in, bp_in, b_in, bv_in = [sem(f"x_in{n}") for n in range(4)], sem("bp_in"), sem("b_in"), sem("bv_in")
        w_in = [sem(f"aw_in{n}") for n in range(3)]
        w_hi, w_lo, full, qk_out, v_out = sem("aw_hi"), sem("aw_lo"), sem("qkv_full"), sem("qk_out"), sem("v_out")
        block = ctx.enter_context(nc.Block())
        HALF = OutputAndNorm.HALF
        QK = 2 * NBLK * 2
        EARLY = NBLK

        @block.sync
        def _(sp):
            sp.dma_start(bp_sb[:], bp.rearrange("(a d) -> a d", a=1).broadcast_to((P, D))).then_inc(bp_in, 16)
            for n in range(4):
                sp.dma_start(x_sb[:, 2 * n:2 * n + 2], x[2 * n * P:(2 * n + 2) * P].rearrange(
                    "(t p) d -> p t d", p=P)).then_inc(x_in[n], 16)
            for n, w in enumerate(attn_w):
                sp.dma_start(w_raw[n], w.rearrange("(c p) e -> p c e", p=P)).then_inc(w_in[n], 16)
            for n, b in enumerate(attn_b[:2]):
                sp.dma_start(b_col[:, n, :], b).then_inc(b_in, 16)
            sp.dma_start(bv_sb[:], attn_b[2].rearrange("(a d) -> a d", a=1).broadcast_to((P, D))).then_inc(bv_in, 16)

        @block.gpsimd
        def _(pool):
            pool.wait_ge(bp_in, 16)
            for t in range(TT):
                if t % 2 == 0:
                    pool.wait_ge(x_in[t // 2], 16)
                pool.tensor_tensor(x_sb[:, t, :], x_sb[:, t, :], bp_sb[:], ALU.add).then_inc(norm.biased, 1)

        @block.scalar
        def _(act):
            def weights(n):
                act.wait_ge(w_in[n], 16)
                act.activation(w_s[n][:, 0], w_raw[n], ACT.Copy).then_inc(w_hi, 1)

            def units(which):
                for u in which:
                    half, n, i = u // 8, u // 4 % 2, u % 4
                    act.wait_ge(full, u + 1)
                    act.activation((qT, kT)[n][:, i, half * 512:(half + 1) * 512], bank[u % 4][:], ACT.Identity,
                                   bias=b_col[:, n, i:i + 1]).then_inc(qk_out, 1)

            norm.act_root(act, 0)
            weights(0)
            norm.act_high(act, range(HALF))
            norm.act_root(act, 1)
            act.wait_ge(norm.full, TT)
            weights(1)
            act.wait_ge(b_in, 32)
            units(range(EARLY))
            norm.act_high(act, range(HALF, TT))
            weights(2)
            units(range(EARLY, QK))

        @block.vector
        def _(dve):
            def weights(n):
                dve.wait_ge(w_hi, n + 1)
                dve.tensor_tensor(w_s[n][:, 1], w_raw[n], w_s[n][:, 0].bitcast(F32), ALU.subtract).then_inc(w_lo, 1)

            norm.dve_add(dve, range(HALF))
            norm.dve_norm(dve, 0)
            norm.dve_add(dve, range(HALF, HALF + 1))
            weights(0)
            norm.dve_add(dve, range(HALF + 1, TT - 2))
            norm.dve_low(dve, range(HALF))
            norm.dve_add(dve, range(TT - 2, TT))
            norm.dve_norm(dve, 1)
            weights(1)
            norm.dve_low(dve, range(HALF, TT))
            weights(2)
            dve.wait_ge(bv_in, 16)
            for t in range(TT):
                dve.wait_ge(full, QK + t + 1)
                dve.tensor_tensor(v_sb[:, t, :], bank[t % 4][:], bv_sb[:], ALU.add).then_inc(v_out, 1)

        @block.tensor
        def _(pe):
            def units(which):
                for u in which:
                    half, n, i = u // 8, u // 4 % 2, u % 4
                    pe.wait_ge(w_lo, n + 1)
                    pe.wait_ge(norm.lo_ok, HALF * (half + 1))
                    if u < 4:
                        pe.wait_ge(norm.added, HALF + u + 1)
                    else:
                        pe.wait_ge(qk_out, u - 3)
                    three_passes(pe, bank[u % 4][:], lambda a, c: w_s[n][:, a, c, i * P:(i + 1) * P],
                                 lambda a, c: xnT[:, a, c, half * 512:(half + 1) * 512]).then_inc(full, 1)

            norm.pe_products(pe, range(TT - 2))
            norm.pe_turn(pe, range(HALF))
            norm.pe_products(pe, range(TT - 2, TT))
            units(range(EARLY))
            norm.pe_turn(pe, range(HALF, TT))
            units(range(EARLY, QK))
            pe.wait_ge(w_lo, 3)
            for t in range(TT):
                if t < 4:
                    pe.wait_ge(qk_out, QK - 3 + t)
                else:
                    pe.wait_ge(v_out, t - 3)
                three_passes(pe, bank[t % 4][:], lambda a, c: xnT[:, a, c, t * P:(t + 1) * P],
                             lambda a, c: w_s[2][:, a, c, :]).then_inc(full, 1)


def self_attention(nc, qT, kT, v_sb, alibi, wo, context, ident):
    ctx = ExitStack()
    with ctx:
        sb = lambda n, s, d=F32: ctx.enter_context(nc.sbuf_tensor(n, s, d))
        sem = lambda n: ctx.enter_context(nc.semaphore(n))
        wo_raw, att, wo_s = context.w_raw, context.att, context.w_out
        al_sb = sb("al_sb", [P, 4, 4 * N])
        sc, ex, pr, pT = (sb(f"sa_{n}", [P, 2, H, N]) for n in ("scores", "exp", "prob", "prob_t"))
        small = sb("sa_small", [P, 2, 3, H])
        s_ps = ctx.enter_context(nc.psum_tensor("sa_s", [P, 4, 512], F32))
        t_ps = [ctx.enter_context(nc.psum_tensor(f"sa_t{i}", [P, 4, 2, N], F32)) for i in range(2)]
        o_ps = ctx.enter_context(nc.psum_tensor("sa_o", [P, 2, 512], F32))
        al_in, wo_in, wo_hi, wo_lo = sem("al_in"), sem("wo_in"), sem("wo_hi"), sem("wo_lo")
        s_full, s_out, max_ok = sem("sa_s_full"), sem("sa_s_out"), sem("sa_max")
        sub_ok, exp_ok = sem("sa_sub"), sem("sa_exp")
        sum_ok, rec_ok, pr_ok = sem("sa_sum"), sem("sa_rec"), sem("sa_pr")
        turned, pT_act, pT_dve, pv_ok, o_hi, o_lo = (sem("sa_turned"), sem("sa_pT_act"), sem("sa_pT_dve"),
                                                     sem("sa_pv"), sem("sa_o_hi"), sem("sa_o_lo"))
        block = ctx.enter_context(nc.Block())

        @block.sync
        def _(sp):
            sp.dma_start(al_sb[:].rearrange("p g k -> p (g k)"), alibi.broadcast_to((P, H * N))).then_inc(al_in, 16)
            sp.dma_start(wo_raw, wo.rearrange("(c p) e -> p c e", p=P)).then_inc(wo_in, 16)

        @block.gpsimd
        def _(pool):
            for t in range(TT + 1):
                if t >= 1:
                    k = (t - 1) % 2
                    pool.wait_ge(rec_ok, t)
                    if t >= 3:
                        pool.wait_ge(turned, 2 * (t - 2))
                    pool.tensor_tensor(pr[:, k], ex[:, k],
                                       small[:, k, 2, :].unsqueeze(2).broadcast_to((P, H, N)),
                                       ALU.mult).then_inc(pr_ok, 1)
                if t < TT:
                    k = t % 2
                    pool.wait_ge(max_ok, t + 1)
                    if t >= 2:
                        pool.wait_ge(pr_ok, t - 1)
                    pool.tensor_tensor(ex[:, k], sc[:, k], small[:, k, 0, :].unsqueeze(2).broadcast_to((P, H, N)),
                                       ALU.subtract).then_inc(sub_ok, 1)

        def turned_blocks(t, n):
            for a in range(2):
                for b in range(2):
                    yield (pT[b * N:(b + 1) * N, t % 2, 8 * n + a:8 * n + 8:2, :],
                           t_ps[n][a * N:(a + 1) * N, :, b, :])

        @block.vector
        def _(dve):
            dve.wait_ge(al_in, 16)

            def soft(t):
                k = t % 2
                dve.wait_ge(s_full, t + 1)
                if t >= 2:
                    dve.wait_ge(sub_ok, t - 1)
                dve.scalar_tensor_tensor(sc[:, k].rearrange("p (g i) n -> p g (i n)", g=4), s_ps[:, :, 0:4 * N],
                                         SCALE, al_sb[:], ALU.mult, ALU.add).then_inc(s_out, 1)
                dve.wait_ge(s_out, t + 1)
                dve.tensor_reduce(small[:, k, 0, :], sc[:, k], AX.X, ALU.max).then_inc(max_ok, 1)

            def normal(t):
                k = t % 2
                dve.wait_ge(exp_ok, t + 1)
                if t >= 2:
                    dve.wait_ge(pr_ok, t - 1)
                dve.tensor_reduce(small[:, k, 1, :], ex[:, k], AX.X, ALU.add).then_inc(sum_ok, 1)
                dve.wait_ge(sum_ok, t + 1)
                dve.reciprocal(small[:, k, 2, :], small[:, k, 1, :]).then_inc(rec_ok, 1)

            def turn(t):
                for n in range(2):
                    dve.wait_ge(turned, 2 * t + n + 1)
                    dve.wait_ge(pT_act, 2 * t + n + 1)
                    if t >= 2:
                        dve.wait_ge(pv_ok, t - 1)
                    for dst, src in list(turned_blocks(t, n))[2:]:
                        ins = dve.tensor_copy(dst, src)
                    ins.then_inc(pT_dve, 1)

            def low(t):
                dve.wait_ge(o_hi, t + 1)
                dst = att[:, :, :, t * P:(t + 1) * P].rearrange("p s i (b q) -> p s b i q", b=2)
                src = o_ps[:, :, 0:4 * N].rearrange("p b (i q) -> p b i q", i=4)
                for b in range(2):
                    ins = dve.tensor_tensor(dst[:, 1, b], src[:, b], dst[:, 0, b].bitcast(F32), ALU.subtract)
                ins.then_inc(o_lo, 1)

            for t in range(TT + 2):
                if t >= 2:
                    turn(t - 2)
                if 1 <= t <= TT:
                    normal(t - 1)
                if t < TT:
                    soft(t)
                if t == TT // 2 + 1:
                    dve.wait_ge(wo_hi, 1)
                    dve.tensor_tensor(wo_s[:, 1], wo_raw, wo_s[:, 0].bitcast(F32), ALU.subtract).then_inc(wo_lo, 1)
                if t >= 2:
                    low(t - 2)
            dve.wait_ge(wo_lo, 1)

        @block.scalar
        def _(act):
            def exponentials(t):
                act.wait_ge(sub_ok, t + 1)
                act.activation(ex[:, t % 2], ex[:, t % 2], ACT.Exp).then_inc(exp_ok, 1)

            for t in range(TT + 2):
                if t >= 2:
                    u = t - 2
                    for n in range(2):
                        act.wait_ge(turned, 2 * u + n + 1)
                        if u >= 2:
                            act.wait_ge(pv_ok, u - 1)
                        for dst, src in list(turned_blocks(u, n))[:2]:
                            ins = act.activation(dst, src, ACT.Copy)
                        ins.then_inc(pT_act, 1)
                if t < TT:
                    exponentials(t)
                if t == TT // 2:
                    act.wait_ge(wo_in, 16)
                    act.activation(wo_s[:, 0], wo_raw, ACT.Copy).then_inc(wo_hi, 1)
                if t >= 2:
                    act.wait_ge(pv_ok, u + 1)
                    dst = att[:, 0, :, u * P:(u + 1) * P].rearrange("p i (b q) -> p b i q", b=2)
                    src = o_ps[:, :, 0:4 * N].rearrange("p b (i q) -> p b i q", i=4)
                    for b in range(2):
                        ins = act.activation(dst[:, b], src[:, b], ACT.Copy)
                    ins.then_inc(o_hi, 1)

        @block.tensor
        def _(pe):
            def scores(t):
                if t >= 1:
                    pe.wait_ge(s_out, t)
                for i in range(4):
                    for g in range(4):
                        rows = slice(g * DH, (g + 1) * DH)
                        for b in range(2):
                            at = slice(t * P + b * N, t * P + (b + 1) * N)
                            mm = pe.matmul(s_ps[b * N:(b + 1) * N, g, i * N:(i + 1) * N], qT[rows, i, at],
                                           kT[rows, i, at], start=True, stop=True)
                mm.then_inc(s_full, 1)

            def transposes(t):
                pe.wait_ge(pr_ok, t + 1)
                for n in range(2):
                    if t >= 1:
                        pe.wait_ge(pT_dve, 2 * t + n - 1)
                    for j in range(4):
                        mm = pe.transpose(t_ps[n][:, j].rearrange("p b q -> p (b q)"),
                                          pr[:, t % 2, 2 * (4 * n + j):2 * (4 * n + j + 1)].rearrange(
                                              "p h n -> p (h n)"), ident[:])
                    mm.then_inc(turned, 1)

            def weigh(t):
                pe.wait_ge(pT_dve, 2 * t + 2)
                if t >= 1:
                    pe.wait_ge(o_lo, t)
                for b in range(2):
                    rows = slice(b * N, (b + 1) * N)
                    for i in range(4):
                        for g in range(4):
                            mm = pe.matmul(o_ps[g * DH:(g + 1) * DH, b, i * N:(i + 1) * N],
                                           v_sb[rows, t, (4 * i + g) * DH:(4 * i + g + 1) * DH],
                                           pT[rows, t % 2, 4 * g + i, :], start=True, stop=True)
                mm.then_inc(pv_ok, 1)

            for t in range(TT + 2):
                if t >= 2:
                    transposes(t - 2)
                if t < TT:
                    scores(t)
                if t >= 2:
                    weigh(t - 2)


def output_and_feed_forward(nc, bo, w_ffn, context, x_sb, xnT, ident, out):
    FB = FF // P
    STEPS, BETA = 5, 0.9
    GROUPS = [range(0, 4), range(4, 6), range(6, 8)]
    LAST_TILES = GROUPS[-1]
    BANKS = [(0, 1, 2, 3), (0, 1), (2, 3)]
    ALL = len(GROUPS) * FB
    OPS = 3 * (STEPS - 1) + 2
    PER_BLOCK = 3
    RAW, WS, AS, HS, HB = 4, 5, 2, 4, 4
    HALF = OutputAndNorm.HALF
    AHEAD = 2
    EARLY = 1
    ctx = ExitStack()
    with ctx:
        sb = lambda n, s, d=F32: ctx.enter_context(nc.sbuf_tensor(n, s, d))
        sem = lambda n: ctx.enter_context(nc.semaphore(n))
        w_raw = sb("f_raw", [P, RAW, 2 * D])
        w_s = sb("f_w", [P, WS, 2, 2 * D], F32R)
        relu = sb("f_relu", [P, AS, 512])
        sq = sb("f_sq", [P, AS, 512])
        h_s = sb("f_h", [P, HS, 2, 512], F32R)
        bo_sb = sb("bo_sb", [P, D])
        bank = [ctx.enter_context(nc.psum_tensor(f"f_ps{i}", [P, 512], F32)) for i in range(8)]
        h_ps, y_ps = bank[:4], bank[4:]
        norm = OutputAndNorm(nc, ctx, "so", context.att, context.w_out, x_sb, xnT, context.rows, ident, bank)
        y_sb = context.rows.rearrange("p (t d) -> p t d", t=TT)
        acc = context.w_raw
        w_in = [sem(f"f_w_in{n}") for n in range(RAW)]
        state = w_raw[:].rearrange("p r (h d) -> p (r h) d", d=D)
        bo_in = sem("bo_in")
        w_hi, w_lo, h_full, relu_ok, sq_ok, h_hi, h_lo = (sem("f_w_hi"), sem("f_w_lo"), sem("f_h_full"), sem("f_relu"),
                                                          sem("f_sq"), sem("f_h_hi"), sem("f_h_lo"))
        y_part, y_out, spike, done, stored = (sem("f_y_part"), sem("f_y_out"), sem("f_spike"), sem("f_done"),
                                              sem("f_stored"))
        block = ctx.enter_context(nc.Block())

        def tokens(n):
            tiles = GROUPS[n // FB]
            return slice(tiles[0] * P, (tiles[-1] + 1) * P), len(tiles) * P

        @block.sync
        def _(sp):
            sp.dma_start(bo_sb[:], bo.rearrange("(a d) -> a d", a=1).broadcast_to((P, D))).then_inc(bo_in, 16)
            for n in range(ALL):
                if n >= RAW:
                    sp.wait_ge(w_lo, n - RAW + 1)
                sp.dma_start(w_raw[:, n % RAW, :], w_ffn[n % FB]).then_inc(w_in[n % RAW], 16)
            for t in range(TT):
                sp.wait_ge(done, t + 1)
                sp.dma_start(out[t * P:(t + 1) * P, :], x_sb[:, t, :]).then_inc(stored, 16)
            sp.wait_ge(stored, 16 * TT)

        @block.gpsimd
        def _(pool):
            pool.wait_ge(bo_in, 16)
            for t in range(TT):
                pool.tensor_tensor(x_sb[:, t, :], x_sb[:, t, :], bo_sb[:], ALU.add).then_inc(norm.biased, 1)
            for n in range(ALL):
                pool.wait_ge(w_hi, n + 1)
                pool.tensor_tensor(w_s[:, n % WS, 1, :], w_raw[:, n % RAW, :], w_s[:, n % WS, 0, :].bitcast(F32),
                                   ALU.subtract).then_inc(w_lo, 1)

        @block.scalar
        def _(act):
            def weights(n):
                act.wait_ge(w_in[n % RAW], 16 * (n // RAW + 1))
                if n >= WS:
                    act.wait_ge(y_part, n - WS + 1)
                act.activation(w_s[:, n % WS, 0, :], w_raw[:, n % RAW, :], ACT.Copy).then_inc(w_hi, 1)

            norm.act_root(act, 0)
            for n in range(WS - 2):
                weights(n)
            norm.act_high(act, range(HALF))
            norm.act_root(act, 1)
            def high(n):
                w = tokens(n)[1]
                act.wait_ge(sq_ok, n + 1)
                if n >= HS:
                    act.wait_ge(y_part, n - HS + 1)
                act.activation(h_s[:, n % HS, 0, 0:w], sq[:, n % AS, 0:w], ACT.Copy).then_inc(h_hi, 1)

            for n in range(ALL + 1):
                if n == EARLY:
                    norm.act_high(act, range(HALF, TT))
                if n < ALL:
                    w = tokens(n)[1]
                    act.wait_ge(h_full, n + 1)
                    if n >= AS:
                        act.wait_ge(sq_ok, n - AS + 1)
                    act.activation(relu[:, n % AS, 0:w], h_ps[n % HB][:, 0:w], ACT.Relu).then_inc(relu_ok, 1)
                if n >= 1:
                    high(n - 1)
                if n % FB == AHEAD - 1 and n >= FB or n == ALL:
                    group = n // FB - 1
                    act.wait_ge(y_part, (group + 1) * FB)
                    for t, k in zip(GROUPS[group], BANKS[group]):
                        act.activation(y_sb[:, t, :], y_ps[k][:], ACT.Copy).then_inc(y_out, 1)
                if n + WS - 2 < ALL:
                    weights(n + WS - 2)

        @block.vector
        def _(dve):
            def neuron(t, k, acc):
                y, (m0, m1, charge, total) = y_sb[:, t, :], (acc[:, n, :] for n in range(4))
                step = (k - 1) // 3
                old, new = (y if step == 0 else (m0, m1)[(step - 1) % 2]), (m0, m1)[step % 2]
                if k == 0:
                    return dve.tensor_scalar(total, y, 1.0, None, ALU.is_gt)
                if k == OPS - 1:
                    return dve.scalar_tensor_tensor(x_sb[:, t, :], total, 1.0 / STEPS, x_sb[:, t, :],
                                                    ALU.mult, ALU.add)
                if k % 3 == 1:
                    return dve.scalar_tensor_tensor(charge, old, BETA, y, ALU.mult, ALU.add)
                if k % 3 == 2:
                    return dve.scalar_tensor_tensor(new, old, 1.0, charge, ALU.is_gt, ALU.subtract, reverse1=True)
                return dve.scalar_tensor_tensor(total, new, 1.0, total, ALU.is_gt, ALU.add)

            def spikes(q):
                t, k = q // OPS, q % OPS
                if q:
                    dve.wait_ge(spike, q)
                if k == 0:
                    dve.wait_ge(y_out, t + 1)
                neuron(t, k, acc).then_inc(spike, 1)
                if k == OPS - 1:
                    dve.wait_ge(spike, q + 1)
                    dve.sem_inc(done, 1)

            norm.dve_add(dve, range(HALF))
            norm.dve_norm(dve, 0)
            norm.dve_add(dve, range(HALF, TT - 2))
            norm.dve_low(dve, range(HALF))
            norm.dve_add(dve, range(TT - 2, TT))
            norm.dve_norm(dve, 1)

            def square(n):
                w = tokens(n)[1]
                dve.wait_ge(relu_ok, n + 1)
                if n >= AS:
                    dve.wait_ge(h_lo, n - AS + 1)
                dve.scalar_tensor_tensor(sq[:, n % AS, 0:w], h_ps[n % HB][:, 0:w], 0.0, relu[:, n % AS, 0:w],
                                         ALU.max, ALU.mult).then_inc(sq_ok, 1)

            def low(n):
                w = tokens(n)[1]
                dve.wait_ge(h_hi, n + 1)
                dve.tensor_tensor(h_s[:, n % HS, 1, 0:w], sq[:, n % AS, 0:w], h_s[:, n % HS, 0, 0:w].bitcast(F32),
                                  ALU.subtract).then_inc(h_lo, 1)

            q = 0
            for n in range(ALL + 1):
                end = q
                if n < ALL and n % FB >= AHEAD:
                    end = max(q, min(q + PER_BLOCK, OPS * GROUPS[n // FB][0]))
                if n == EARLY:
                    norm.dve_low(dve, range(HALF, TT))
                if n < ALL:
                    square(n)
                if q < end:
                    spikes(q)
                    q += 1
                if n >= 1:
                    low(n - 1)
                for q in range(q, end):
                    spikes(q)
                q = max(q, end)
            for q in range(q, OPS * LAST_TILES[0]):
                spikes(q)
            dve.wait_ge(w_lo, ALL)
            q = OPS * LAST_TILES[0]
            for k in range(OPS):
                for j, t in enumerate(LAST_TILES):
                    if k == 0:
                        dve.wait_ge(y_out, t + 1)
                    dve.wait_ge(spike, q - 1)
                    neuron(t, k, state[:, 4 * j:4 * j + 4]).then_inc(spike, 1)
                    q += 1
            for j in range(len(LAST_TILES)):
                dve.wait_ge(spike, q - 1 + j)
                dve.sem_inc(done, 1)

        @block.tensor
        def _(pe):
            def hidden(n):
                at, w = tokens(n)
                pe.wait_ge(w_lo, n + 1)
                if n >= HB:
                    pe.wait_ge(sq_ok, n - HB + 1)
                else:
                    pe.wait_ge(norm.added, TT - HB + n + 1)
                if n == 0 or n == FB:
                    pe.wait_ge(norm.lo_ok, TT if n else HALF)
                fc = w_s[:, n % WS].rearrange("p s (m c f) -> p s m c f", m=2, c=DC)
                three_passes(pe, h_ps[n % HB][:, 0:w], lambda a, c: fc[:, a, 0, c, :],
                             lambda a, c: xnT[:, a, c, at]).then_inc(h_full, 1)

            def project(n):
                group, f = n // FB, n % FB
                pe.wait_ge(h_lo, n + 1)
                if n == 0:
                    pe.wait_ge(norm.lo_ok, TT)
                if f == 0 and group:
                    pe.wait_ge(y_out, BANKS[group][-1] + 1)
                for k, bank in enumerate(BANKS[group]):
                    for m, (a, b) in enumerate(((0, 0), (1, 0), (0, 1))):
                        mm = pe.matmul(y_ps[bank][:], h_s[:, n % HS, a, k * P:(k + 1) * P],
                                       w_s[:, n % WS, b, D:2 * D],
                                       start=(f == 0 and m == 0), stop=(f == FB - 1 and m == 2))
                mm.then_inc(y_part, 1)

            norm.pe_products(pe, range(TT - 2))
            norm.pe_turn(pe, range(HALF))
            norm.pe_products(pe, range(TT - 2, TT))
            for n in range(ALL + AHEAD):
                if n < ALL:
                    hidden(n)
                if n == EARLY:
                    norm.pe_turn(pe, range(HALF, TT))
                if n >= AHEAD:
                    project(n - AHEAD)


def perceiver(nc, x, yT, xwq, xwk, xwv, xwp, xbp, awq, abq, awk, abk, awv, abv, awo, abo, w_ffn, alibi,
              out, q_dram, o_dram):
    ctx = ExitStack()
    with ctx:
        sb = lambda n, s, d=F32: ctx.enter_context(nc.sbuf_tensor(n, s, d))
        ident = sb("ident", [P, P])
        context = Context(nc, ctx)
        with ExitStack() as first:
            sh = Shared(nc, first, context)
            prologue(nc, x, yT, xwq, xwk, xwv, q_dram, sh, ident)
            cross_attention(nc, yT, q_dram, o_dram, xwp, sh, context, ident)
        x_sb = sb("x_sb", [P, TT, D])
        xnT = sb("xnT", [P, 2, DC, TOK], F32R)
        with nc.sbuf_tensor("qT", [P, NBLK, TOK], F32) as qT, nc.sbuf_tensor("kT", [P, NBLK, TOK], F32) as kT:
            v_sb = context.rows.rearrange("p (t d) -> p t d", t=TT)
            output_and_qkv(nc, x, xbp, (awq, awk, awv), (abq, abk, abv), context, x_sb, xnT, qT, kT, v_sb, ident)
            self_attention(nc, qT, kT, v_sb, alibi, awo, context, ident)
        output_and_feed_forward(nc, abo, w_ffn, context, x_sb, xnT, ident, out)


def kernel(x, ctx_1024, L0_xattn_Wq, L0_xattn_Wk, L0_xattn_Wv, L0_xattn_Wp, L0_xattn_bp, L0_attn_Wq, L0_attn_bq,
           L0_attn_Wk, L0_attn_bk, L0_attn_Wv, L0_attn_bv, L0_attn_Wo, L0_attn_bo, L0_ffn_W_fc, L0_ffn_W_proj):
    import concourse.bacc as bacc
    from concourse.bass_utils import run_bass_kernel_spmd

    y = np.zeros((B, D, MP), np.float32)
    y[:, :, :M] = np.asarray(ctx_1024).transpose(0, 2, 1)
    fc = np.asarray(L0_ffn_W_fc).reshape(FF // P, P, DC, P).transpose(0, 3, 2, 1).reshape(FF // P, P, D)
    proj = np.asarray(L0_ffn_W_proj).T.reshape(FF // P, P, D)
    slopes = np.power(np.float32(2.0), np.linspace(-4.0, -0.3, H, dtype=np.float32))
    bias = -(slopes[:, None] * np.arange(N, dtype=np.float32)[None, :])
    bias = bias.reshape(4, 4, N).transpose(1, 0, 2).reshape(1, H * N)

    def turn(w):
        return np.ascontiguousarray(np.asarray(w).T)

    def columns(b):
        return np.ascontiguousarray(np.asarray(b).reshape(NBLK, P).T)

    arrays = {
        "x": np.asarray(x).reshape(TOK, D), "yT": y.reshape(B, DC, P, MP),
        "xwq": L0_xattn_Wq, "xwk": L0_xattn_Wk, "xwv": L0_xattn_Wv, "xwp": L0_xattn_Wp, "xbp": L0_xattn_bp,
        "awq": turn(L0_attn_Wq), "abq": columns(L0_attn_bq), "awk": turn(L0_attn_Wk), "abk": columns(L0_attn_bk),
        "awv": turn(L0_attn_Wv), "abv": L0_attn_bv, "awo": turn(L0_attn_Wo), "abo": L0_attn_bo,
        "w_ffn": np.stack([fc, proj], axis=2).reshape(FF // P, P, 2 * D), "alibi": bias,
    }
    nc = bacc.Bacc("TRN2", target_bir_lowering=False, num_devices=1)
    given = {}
    for name, a in arrays.items():
        arrays[name] = a = np.ascontiguousarray(a)
        given[name] = nc.dram_tensor(name, a.shape, mybir.dt.from_np(a.dtype), kind="ExternalInput").ap()
    out = nc.dram_tensor("out", (TOK, D), F32, kind="ExternalOutput").ap()
    q_dram = nc.dram_tensor("q_scratch", (P, NBLK * 2, TOK), F32, kind="Internal").ap()
    o_dram = nc.dram_tensor("o_scratch", (P, NBLK, STORED), F32, kind="Internal").ap()
    perceiver(nc, **given, out=out, q_dram=q_dram, o_dram=o_dram)
    result = run_bass_kernel_spmd(nc, [arrays], core_ids=[0])
    return result.results[0]["out"].reshape(B, N, D)
```
